# Optimizing a Trainium2 kernel written in Bass

```python
import numpy as np
import jax
import jax.numpy as jnp

def _softmax(x, axis=-1):
    return jax.nn.softmax(x, axis=axis)

def _gelu(x):
    return jax.nn.gelu(x, approximate=True)

def _silu(x):
    return jax.nn.silu(x)

def _sigmoid(x):
    return jax.nn.sigmoid(x)

def _layernorm(x, axis=-1, eps=1e-05):
    m = jnp.mean(x, axis=axis, keepdims=True)
    v = jnp.var(x, axis=axis, keepdims=True)
    return (x - m) / jnp.sqrt(v + eps)

def _scatter_add(tgt, idx, src, axis=0):
    return tgt.at[idx].add(src)

def _segment_sum(src, seg, n):
    return jax.ops.segment_sum(src, seg, n)
kernel_name = 'mk_seq_preln_d1_jaxref_r8_d5e567'

def setup_inputs(seed: int=0):
    np.random.seed(seed)
    _w = jnp.asarray

    def _L0_attn_setup():
        import jax, jax.numpy as jnp
        import numpy as np
        H = 16
        G = 16
        R = 4
        WIN = 64
        NEG = -1000000000.0
        key = jax.random.key(seed)
        ks = jax.random.split(key, 9)
        dm, D = (128, 128 // H)
        s = 0.02
        return {'x': jax.random.normal(ks[0], (1, 256, dm), dtype=jnp.float32), 'Wq': jax.random.normal(ks[1], (dm, dm), dtype=jnp.float32) * s, 'Wk': jax.random.normal(ks[2], (dm, dm), dtype=jnp.float32) * s, 'Wv': jax.random.normal(ks[3], (dm, dm), dtype=jnp.float32) * s, 'Wo': jax.random.normal(ks[4], (dm, dm), dtype=jnp.float32) * s, 'Wck': jax.random.normal(ks[5], (G * D, D), dtype=jnp.float32) * s, 'Wcv': jax.random.normal(ks[6], (G * D, D), dtype=jnp.float32) * s, 'Wg': jax.random.normal(ks[7], (D, 3), dtype=jnp.float32) * s, 'bg': jnp.zeros((3,), dtype=jnp.float32)}
    _L0_attn_in = _L0_attn_setup()

    def _L0_ffn_setup():
        import jax, jax.numpy as jnp
        import numpy as np
        D = 128
        F = 128
        E = 8
        K = 2
        B, T = (2, 256)

        def _moe_forward(x, router_w, w1, w2, shared_gate_up, shared_down, shared_gate_w):
            b, t, d = x.shape
            xf = x.reshape(-1, d)
            n = xf.shape[0]
            logits = xf @ router_w
            probs = jax.nn.softmax(logits, axis=-1)
            topw, topi = jax.lax.top_k(probs, K)
            combine = jnp.zeros((n, E), dtype=probs.dtype).at[jnp.arange(n)[:, None], topi].add(topw)
            h = jax.nn.silu(jnp.einsum('nd,edf->nef', xf, w1))
            ye = jnp.einsum('nef,efd->ned', h, w2)
            routed = jnp.einsum('ne,ned->nd', combine, ye)
            gu = xf @ shared_gate_up
            gate, up = (gu[:, :F], gu[:, F:])
            shared = jax.nn.silu(gate) * up @ shared_down
            shared = jax.nn.sigmoid(xf @ shared_gate_w) * shared
            return (routed + shared).reshape(b, t, d)
        key = jax.random.key(seed)
        ks = jax.random.split(key, 7)
        std = 0.02
        x = jax.random.normal(ks[0], (B, T, D), dtype=jnp.float32)
        router_w = jax.random.normal(ks[1], (D, E), dtype=jnp.float32) * std
        w1 = jax.random.normal(ks[2], (E, D, F), dtype=jnp.float32) * std
        w2 = jax.random.normal(ks[3], (E, F, D), dtype=jnp.float32) * std
        shared_gate_up = jax.random.normal(ks[4], (D, 2 * F), dtype=jnp.float32) * std
        shared_down = jax.random.normal(ks[5], (F, D), dtype=jnp.float32) * std
        shared_gate_w = jax.random.normal(ks[6], (D, 1), dtype=jnp.float32) * std
        return {'x': x, 'router_w': router_w, 'w1': w1, 'w2': w2, 'shared_gate_up': shared_gate_up, 'shared_down': shared_down, 'shared_gate_w': shared_gate_w}
    _L0_ffn_in = _L0_ffn_setup()
    _d = {'L0_attn_x': _L0_attn_in['x'], 'L0_attn_Wq': _L0_attn_in['Wq'], 'L0_attn_Wk': _L0_attn_in['Wk'], 'L0_attn_Wv': _L0_attn_in['Wv'], 'L0_attn_Wo': _L0_attn_in['Wo'], 'L0_attn_Wck': _L0_attn_in['Wck'], 'L0_attn_Wcv': _L0_attn_in['Wcv'], 'L0_attn_Wg': _L0_attn_in['Wg'], 'L0_attn_bg': _L0_attn_in['bg'], 'L0_ffn_router_w': _L0_ffn_in['router_w'], 'L0_ffn_w1': _L0_ffn_in['w1'], 'L0_ffn_w2': _L0_ffn_in['w2'], 'L0_ffn_shared_gate_up': _L0_ffn_in['shared_gate_up'], 'L0_ffn_shared_down': _L0_ffn_in['shared_down'], 'L0_ffn_shared_gate_w': _L0_ffn_in['shared_gate_w']}
    _x0 = _d['L0_attn_x']
    _d['L0_attn_x'] = jax.random.normal(jax.random.fold_in(jax.random.key(seed), 1), (4, 1024, 128), dtype=_x0.dtype)
    del _x0
    return _d

def reference(L0_attn_x, L0_attn_Wq, L0_attn_Wk, L0_attn_Wv, L0_attn_Wo, L0_attn_Wck, L0_attn_Wcv, L0_attn_Wg, L0_attn_bg, L0_ffn_router_w, L0_ffn_w1, L0_ffn_w2, L0_ffn_shared_gate_up, L0_ffn_shared_down, L0_ffn_shared_gate_w):

    def _L0_attn_ref(x, Wq, Wk, Wv, Wo, Wck, Wcv, Wg, bg):
        import jax, jax.numpy as jnp
        import numpy as np
        H = 16
        G = 16
        R = 4
        WIN = 64
        NEG = -1000000000.0
        B, T, dm = x.shape
        D = dm // H
        scale = float(np.sqrt(D))

        def split_heads(y):
            return y.reshape(B, T, H, D).transpose(0, 2, 1, 3)
        q = split_heads(x @ Wq)
        k = split_heads(x @ Wk)
        v = split_heads(x @ Wv)
        pad = -T % G
        T_pad = T + pad
        k_pad = jnp.pad(k, ((0, 0), (0, 0), (0, pad), (0, 0)))
        v_pad = jnp.pad(v, ((0, 0), (0, 0), (0, pad), (0, 0)))
        nb = T_pad // G
        k_c = k_pad.reshape(B, H, nb, G * D) @ Wck
        v_c = v_pad.reshape(B, H, nb, G * D) @ Wcv
        pos = jnp.arange(T)
        blk_end = (jnp.arange(nb) + 1) * G
        c_ok = pos[:, None] >= blk_end[None, :]
        s_b = jnp.einsum('bhtd,bhnd->bhtn', q, k_c) / scale
        logits_c = jnp.where(c_ok, s_b, NEG)
        out_c = jnp.einsum('bhtn,bhnd->bhtd', jax.nn.softmax(logits_c, axis=-1), v_c)
        out_c = out_c * jnp.any(c_ok, axis=-1)[:, None].astype(out_c.dtype)
        r_eff = min(R, nb)
        _, top_idx = jax.lax.top_k(logits_c, r_eff)
        tok = (top_idx[..., None] * G + jnp.arange(G)).reshape(B, H, T, r_eff * G)
        tok = jnp.clip(tok, 0, T_pad - 1)
        bi = jnp.arange(B)[:, None, None, None]
        hi = jnp.arange(H)[None, :, None, None]
        k_s = k_pad[bi, hi, tok]
        v_s = v_pad[bi, hi, tok]
        allowed = tok <= pos[None, None, :, None]
        logits_s = jnp.where(allowed, jnp.einsum('bhtd,bhtnd->bhtn', q, k_s) / scale, NEG)
        out_s = jnp.einsum('bhtn,bhtnd->bhtd', jax.nn.softmax(logits_s, axis=-1), v_s)
        out_s = out_s * jnp.any(allowed, axis=-1)[..., None].astype(out_s.dtype)
        wmask = (jnp.abs(pos[:, None] - pos[None, :]) <= WIN // 2) & (pos[:, None] >= pos[None, :])
        logits_l = jnp.where(wmask, jnp.einsum('bhtd,bhsd->bhts', q, k) / scale, NEG)
        out_l = jnp.einsum('bhts,bhsd->bhtd', jax.nn.softmax(logits_l, axis=-1), v)
        gates = jax.nn.softmax(q.mean(axis=1) @ Wg + bg, axis=-1)

        def merge(o):
            return o.transpose(0, 2, 1, 3).reshape(B, T, dm)
        out = gates[..., 0:1] * merge(out_c) + gates[..., 1:2] * merge(out_s) + gates[..., 2:3] * merge(out_l)
        return out @ Wo

    def _L0_ffn_ref(x, router_w, w1, w2, shared_gate_up, shared_down, shared_gate_w):
        import jax, jax.numpy as jnp
        import numpy as np
        D = 128
        F = 128
        E = 8
        K = 2
        B, T = (2, 256)

        def _moe_forward(x, router_w, w1, w2, shared_gate_up, shared_down, shared_gate_w):
            b, t, d = x.shape
            xf = x.reshape(-1, d)
            n = xf.shape[0]
            logits = xf @ router_w
            probs = jax.nn.softmax(logits, axis=-1)
            topw, topi = jax.lax.top_k(probs, K)
            combine = jnp.zeros((n, E), dtype=probs.dtype).at[jnp.arange(n)[:, None], topi].add(topw)
            h = jax.nn.silu(jnp.einsum('nd,edf->nef', xf, w1))
            ye = jnp.einsum('nef,efd->ned', h, w2)
            routed = jnp.einsum('ne,ned->nd', combine, ye)
            gu = xf @ shared_gate_up
            gate, up = (gu[:, :F], gu[:, F:])
            shared = jax.nn.silu(gate) * up @ shared_down
            shared = jax.nn.sigmoid(xf @ shared_gate_w) * shared
            return (routed + shared).reshape(b, t, d)
        return _moe_forward(x, router_w, w1, w2, shared_gate_up, shared_down, shared_gate_w)
    x = L0_attn_x
    x = x + _L0_attn_ref(_layernorm(x, axis=-1), L0_attn_Wq, L0_attn_Wk, L0_attn_Wv, L0_attn_Wo, L0_attn_Wck, L0_attn_Wcv, L0_attn_Wg, L0_attn_bg)
    x = x + _L0_ffn_ref(_layernorm(x, axis=-1), L0_ffn_router_w, L0_ffn_w1, L0_ffn_w2, L0_ffn_shared_gate_up, L0_ffn_shared_down, L0_ffn_shared_gate_w)
    return x

_drawn_inputs = setup_inputs


def setup_inputs(seed=0):
    import zlib

    import numpy as np

    out = dict(_drawn_inputs(seed))
    spreads = {'L0_attn_bg': (0.0, 0.8)}
    factors = {'L0_attn_Wq': 8.0,
     'L0_attn_Wk': 8.0,
     'L0_attn_Wv': 8.0,
     'L0_attn_Wo': 8.0,
     'L0_attn_Wck': 8.0,
     'L0_attn_Wcv': 8.0,
     'L0_attn_Wg': 8.0,
     'L0_ffn_router_w': 8.0,
     'L0_ffn_w1': 8.0,
     'L0_ffn_w2': 8.0,
     'L0_ffn_shared_gate_up': 8.0,
     'L0_ffn_shared_down': 8.0,
     'L0_ffn_shared_gate_w': 8.0}
    for name, (base, spread) in spreads.items():
        noise = np.random.default_rng([zlib.crc32(name.encode()), seed]).standard_normal(out[name].shape)
        drawn = base * np.exp(spread * noise) if base else spread * noise
        out[name] = jnp.asarray(drawn.astype(out[name].dtype))
    for name, factor in factors.items():
        out[name] = (out[name] * factor).astype(out[name].dtype)
    return out
```

```python
from contextlib import ExitStack

import concourse.bass as bass
from concourse import mybir

F32 = mybir.dt.float32
BF16 = mybir.dt.bfloat16
ALU = mybir.AluOpType
ACT = mybir.ActivationFunctionType
AX = mybir.AxisListType

P = 128
B, T, DM = 4, 1024, 128
H, D = 16, 8
G, NB = 16, T // 16
TOP = 4
WIN = 32
TILES = B * T // P
NT = T // P
CH = 512
TC = CH // P
CHUNKS = B * T // CH
HC = T // CH
NK = T + NB
SCALE = float(D) ** -0.5
EPS = 1e-5
OUT_OF_REACH = -1e30
SENTINEL = -3e38
TAKEN = 3e38
HG = 4
GROUPS = B * H // HG
QUADS = H // HG
SP_Q = (0, 1, 2, 0, 1, 0)
SP_K = (0, 0, 0, 1, 1, 2)
R_SPLIT = 64
R_SHIFT = R_SPLIT + len(SP_Q) * D
ROWS = R_SHIFT + 3
E, F = 8, 128
K2 = 2
ds = bass.ds

BAND = P + WIN
SEL = [(c, j) for c in range(HC) for j in range(TC * (c + 1))]
SECOND = [x for c in range(HC) for x in
          [("selected", c, j) for j in range(TC * (c + 1))]
          + [("local", c, j) for j in range(TC * c, TC * (c + 1))] + [("compressed", c, 0)]]
BACK_AT = [n + 1 for n, x in enumerate(SECOND) if x[0] == "compressed"]


def width(c, j):
    return min(CH, (c + 1) * CH - j * P)


def band_width(j):
    return BAND if j < NT - 1 else P


def uses_of_b():
    sel, loc, back, u = [], [], [], 0
    for n in range(len(SECOND) + 1):
        kind = SECOND[n][0] if n < len(SECOND) else None
        if kind == "selected":
            sel.append(u)
            u += 2
        elif kind == "local":
            loc.append(u)
            u += 1
        if n in BACK_AT:
            back.append(u)
            u += 2
    return sel, loc, back, u


B_SEL, B_LOC, B_BACK, B_USES = uses_of_b()


def b_count(g, u):
    return B_USES // 2 * g + u // 2


def units_of_a():
    out, end = [], []
    for i in range(NT):
        keys = (i + 1) * P
        for w, k0, local in ((min(keys, CH), max(keys - CH, 0), True), (max(keys - CH, 0), 0, False)):
            if w:
                n = CH // w
                out += [(i, tuple(range(h, h + n)), k0, w, local) for h in range(0, HG, n)]
        if i % TC == TC - 1:
            end.append(len(out))
    return out, end


A_UNITS, A_END = units_of_a()
A_USES = len(A_UNITS)
A_AT = [5 + u * 16 // A_USES for u in range(A_USES)]
M_WHAT = ([("logit", n) for n in range(4)] + [("bias", 0), ("bias", 1), ("prob", (0, 0)), ("prob", (0, 1)),
          ("shift", 0), ("prob", (1, 0)), ("prob", (1, 1)), ("shift", 1)])
M_USES = len(M_WHAT)
M_LOGIT = [M_WHAT.index(("logit", n)) for n in range(4)]
M_BIAS = [M_WHAT.index(("bias", n)) for n in range(2)]
M_PROB = [M_WHAT.index(("prob", (n, 1))) for n in range(2)]
M_SHIFT = [M_WHAT.index(("shift", n)) for n in range(2)]
FIRST_AT = {0: (0, 1), 1: (2, 3), 5: (4,), 7: (5,), 9: (6, 7), 13: (8,), 15: (9, 10), len(SECOND): (11,)}
EXP_AT = (4, 6)
SHIFT_AT = (13, len(SECOND))
N_CONST = 28


def is_first(group):
    return isinstance(group[0], int) and group[0] == 0


def is_last(group):
    return isinstance(group[0], int) and group[0] == GROUPS - 1


def after(group):
    g, p, k = group
    return g + 1, 1 - p, k + p


def project(nc, dram, ident_f, ident_b):
    with ExitStack() as ctx:
        def sb(name, shape, dt=F32):
            return ctx.enter_context(nc.sbuf_tensor(name, shape, dt))

        def ps(name, shape, dt=F32):
            return ctx.enter_context(nc.psum_tensor(name, shape, dt))

        def sem(name):
            return ctx.enter_context(nc.semaphore(name))

        xs = sb("xs", [P, TILES, DM])
        wq = sb("wq", [P, DM])
        wk = sb("wk", [P, DM])
        wv = sb("wv", [P, DM])
        wqt = sb("wqt", [P, DM])
        wvg = sb("wvg", [P, DM + 3])
        wg_rep = sb("wg_rep", [P, 3])
        bg_rep = sb("bg_rep", [P, 3])
        wc_rep = sb("wc_rep", [P, 2, G, D])
        wc_diag = sb("wc_diag", [P, 2, G, H, D])
        head_of_row = sb("head_of_row", [P, H])
        late = sb("late", [P, 1])
        eps = sb("eps", [P, 1])
        total = sb("total", [P, TC])
        mean = sb("mean", [P, TC])
        centred = sb("centred", [P, TC, DM])
        squares = sb("squares", [P, TC, DM])
        sqsum = sb("sqsum", [P, TC])
        sdev = sb("sdev", [P, TC])
        rstd = sb("rstd", [P, TC])
        normed = sb("normed", [P, TC, DM])
        normed_t = sb("normed_t", [P, CH])
        kt = sb("kt", [P, B * T])
        vt = sb("vt", [P, B * T])
        q_split = sb("q_split", [P, 3, CH], BF16)
        k_split = sb("k_split", [P, 3, CH], BF16)
        q_rest = sb("q_rest", [P, CH])
        k_rest = sb("k_rest", [P, CH])
        v_out = sb("v_out", [P, TC, DM])
        gates = sb("gates", [P, TILES, 3])
        gate_max = sb("gate_max", [P, TILES])
        gate_sum = sb("gate_sum", [P, TILES])
        gate_inv = sb("gate_inv", [P, TILES])
        kc_split = sb("kc_split", [P, 3, B * NB], BF16)
        kc_rest = sb("kc_rest", [P, B * NB])
        vct = sb("vct", [P, B * NB])
        vc_out = sb("vc_out", [NB, B, DM])

        ps_t = ps("ps_t", [P, CH])
        ps_q = ps("ps_q", [P, CH])
        ps_k = ps("ps_k", [P, CH])
        ps_vt = ps("ps_vt", [P, CH])
        ps_v = ps("ps_v", [P, TC, 256])
        ps_w = ps("ps_w", [P, CH])

        x_in, w_in, w_made, diag_made, wqt_ready = map(sem, ("x_in", "w_in", "w_made", "diag_made", "wqt_ready"))
        wt_ps, wqt_done, wg_ps, wvg_done = map(sem, ("wt_ps", "wqt_done", "wg_ps", "wvg_done"))
        consts, const_step, sums, means, centre = map(sem, ("consts", "const_step", "sums", "means", "centre"))
        squared, sqsums, sdevs, rstds, norms = map(sem, ("squared", "sqsums", "sdevs", "rstds", "norms"))
        t_ps, nt_done, q_ps, k_ps, vt_ps, v_ps = map(sem, ("t_ps", "nt_done", "q_ps", "k_ps", "vt_ps", "v_ps"))
        q0_done, k0_done, vt_done, v_done = map(sem, ("q0_done", "k0_done", "vt_done", "v_done"))
        qr_done, q1_done, q2_done, kr_done, k1_done, k2_done = map(
            sem, ("qr_done", "q1_done", "q2_done", "kr_done", "k1_done", "k2_done"))
        q_out, k_out, v_stored = map(sem, ("q_out", "k_out", "v_stored"))
        kc_ps, vc_ps, kc_step, vct_done, vc_tr, vc_done = map(
            sem, ("kc_ps", "vc_ps", "kc_step", "vct_done", "vc_tr", "vc_done"))
        gate_step, gate_exp, end_out = map(sem, ("gate_step", "gate_exp", "end_out"))
        ctx.enter_context(nc.allow_non_contiguous_dma(reason="rows of a few elements"))
        block = ctx.enter_context(nc.Block())
        N_W = 3 + H + 1 + 2 * H

        def chunks(engine, chunk):
            chunk(0)
            with engine.Fori(1, CHUNKS) as c:
                chunk(c)

        def started(c):
            return not (isinstance(c, int) and c == 0)

        @block.sync
        def _(sp):
            for c in range(CHUNKS):
                sp.dma_start(xs[:, c * TC:(c + 1) * TC, :],
                             dram["x"][c * CH:(c + 1) * CH, :].rearrange("(i p) n -> p i n", p=P)).then_inc(x_in, 16)
            with sp.Fori(0, B) as b:
                for half in range(HC):
                    c = b * HC + half
                    for name, split, last, out in (("q", q_split, q2_done, q_out), ("k", k_split, k2_done, k_out)):
                        sp.wait_ge(last, c + 1)
                        for s in range(3):
                            at = dram[name][ds(b, 1), s * D:(s + 1) * D]
                            if name == "q":
                                at = at[:, :, half, :, :].rearrange("a r h t -> h (a r) t")
                            else:
                                at = at[:, :, :, half * CH:(half + 1) * CH].rearrange("a r h t -> h (a r) t")
                            sp.dma_start(at, split[:, s, :]).then_inc(out, 16)
                    sp.wait_ge(v_done, 2 * c + 2)
                    sp.dma_start(dram["v"][ds(b, 1), half * CH:(half + 1) * CH, :]
                                 .rearrange("a (i p) r -> p (a i) r", p=P), v_out[:, :, :]).then_inc(v_stored, 16)
            sp.wait_ge(kc_step, 6)
            for b in range(B):
                for s in range(3):
                    sp.dma_start(dram["k"][b, s * D:(s + 1) * D, :, T:NK].rearrange("r h n -> h r n"),
                                 kc_split[:, s, b * NB:(b + 1) * NB]).then_inc(end_out, 16)
            sp.wait_ge(vc_done, 1)
            sp.dma_start(dram["vc"].rearrange("b n r -> n b r"), vc_out[:, :, :]).then_inc(end_out, 16)
            sp.wait_ge(gate_step, 7)
            for b in range(B):
                sp.dma_start(dram["gates"][b], gates[:, b * NT:(b + 1) * NT, :]).then_inc(end_out, 16)
            sp.wait_ge(q_out, 3 * 16 * CHUNKS)
            sp.wait_ge(k_out, 3 * 16 * CHUNKS)
            sp.wait_ge(v_stored, 16 * CHUNKS)
            sp.wait_ge(end_out, 16 * (4 * B + 1))

        @block.gpsimd
        def _(pool):
            pool.memset(ident_f[:, :], 0.0).then_inc(const_step, 1)
            pool.memset(ident_b[:, :], 0.0).then_inc(const_step, 1)
            pool.memset(head_of_row[:, :], 1.0).then_inc(const_step, 1)
            pool.memset(late[:, :], 1.0).then_inc(const_step, 1)
            pool.memset(eps[:, :], EPS).then_inc(consts, 1)
            pool.wait_ge(const_step, 4)
            for m in (ident_f, ident_b):
                pool.affine_select(out=m[:, :], in_=m[:, :], compare_op=ALU.not_equal, fill=1.0, base=0,
                                   pattern=[[-1, P]], channel_multiplier=1).then_inc(consts, 1)
            pool.affine_select(out=late[:, :], in_=late[:, :], compare_op=ALU.is_ge, fill=0.0, base=-G,
                               pattern=[[0, 1]], channel_multiplier=1).then_inc(consts, 1)
            pool.affine_select(out=head_of_row[:, :], in_=head_of_row[:, :], compare_op=ALU.is_ge, fill=0.0,
                               base=0, pattern=[[-D, H]], channel_multiplier=1).then_inc(const_step, 1)
            pool.wait_ge(const_step, 5)
            pool.affine_select(out=head_of_row[:, :], in_=head_of_row[:, :], compare_op=ALU.is_ge, fill=0.0,
                               base=D - 1, pattern=[[D, H]], channel_multiplier=-1).then_inc(consts, 1)
            pool.wait_ge(consts, 5)
            pool.wait_ge(w_in, 16 * N_W)
            for i in range(2):
                for g in range(G):
                    last = pool.tensor_tensor(
                        wc_diag[:, i, g, :, :], wc_rep[:, i, g, :].unsqueeze(1).broadcast_to([P, H, D]),
                        head_of_row[:, :].unsqueeze(2).broadcast_to([P, H, D]), ALU.mult)
                    last.then_inc(diag_made, 1)

        @block.scalar
        def _(act):
            for w, name in ((wq, "wq"), (wk, "wk"), (wv, "wv")):
                act.dma_start(w[:, :], dram[name]).then_inc(w_in, 16)
            act.dma_start(bg_rep[:, :], dram["bg"].partition_broadcast(P)).then_inc(w_in, 16)
            for h in range(H):
                rows = slice(h * D, (h + 1) * D)
                act.dma_start(wg_rep[rows, :], dram["wg"]).then_inc(w_in, 16)
                for i, name in enumerate(("wck", "wcv")):
                    act.dma_start(wc_rep[rows, i, :, :], dram[name].rearrange("(g d) e -> d g e", d=D)).then_inc(w_in, 16)
            act.wait_ge(consts, 1)
            def chunk(c):
                act.wait_ge(centre, c + 1)
                act.activation(squares[:, :, :], centred[:, :, :], ACT.Square).then_inc(squared, 1)
                act.wait_ge(sqsums, c + 1)
                act.activation(sdev[:, :], sqsum[:, :], ACT.Sqrt, bias=eps[:, 0:1], scale=1.0 / DM).then_inc(sdevs, 1)
                act.wait_ge(t_ps, c + 1)
                act.activation(normed_t[:, :], ps_t[:, :], ACT.Copy).then_inc(nt_done, 1)
                act.wait_ge(q_ps, c + 1)
                if started(c):
                    act.wait_ge(q_out, c * 48)
                act.activation(q_split[:, 0, :], ps_q[:, :], ACT.Copy, scale=SCALE).then_inc(q0_done, 1)
                act.wait_ge(k_ps, c + 1)
                if started(c):
                    act.wait_ge(k_out, c * 48)
                act.activation(k_split[:, 0, :], ps_k[:, :], ACT.Copy).then_inc(k0_done, 1)
                act.activation(kt[:, ds(c * CH, CH)], ps_k[:, :], ACT.Copy).then_inc(k0_done, 1)
                act.wait_ge(vt_ps, c + 1)
                act.activation(vt[:, ds(c * CH, CH)], ps_vt[:, :], ACT.Copy).then_inc(vt_done, 1)
                act.wait_ge(v_ps, c + 1)
                if started(c):
                    act.wait_ge(v_stored, c * 16)
                act.activation(v_out[:, :, :], ps_v[:, :, 0:DM], ACT.Copy).then_inc(v_done, 1)
                act.activation(gates[:, ds(c * TC, TC), :], ps_v[:, :, DM:DM + 3], ACT.Copy).then_inc(v_done, 1)
            chunks(act, chunk)
            act.wait_ge(vc_ps, 1)
            act.activation(vct[:, :], ps_vt[:, 0:B * NB], ACT.Copy).then_inc(vct_done, 1)
            act.wait_ge(gate_step, 3)
            act.activation(gates[:, :, :], gates[:, :, :], ACT.Exp).then_inc(gate_exp, 1)
            act.wait_ge(vc_tr, 1)
            act.activation(vc_out[:, :, :], ps_t[0:NB, :].rearrange("n (b r) -> n b r", b=B), ACT.Copy).then_inc(vc_done, 1)

        @block.vector
        def _(dve):
            dve.wait_ge(wt_ps, 1)
            dve.tensor_copy(wqt[:, :], ps_w[:, 0:DM]).then_inc(wqt_done, 1)
            dve.wait_ge(w_in, 16 * N_W)
            dve.tensor_copy(wvg[:, 0:DM], wv[:, :]).then_inc(wvg_done, 1)
            dve.wait_ge(wg_ps, 1)
            dve.tensor_scalar(wvg[:, DM:DM + 3], ps_w[:, DM:DM + 3], 1.0 / H, None, ALU.mult).then_inc(wvg_done, 1)
            def chunk(c):
                dve.wait_ge(x_in, 16 * CHUNKS)
                x = xs[:, ds(c * TC, TC), :]
                dve.tensor_reduce(total[:, :], x, AX.X, ALU.add).then_inc(sums, 1)
                dve.wait_ge(sums, c + 1)
                dve.tensor_scalar(mean[:, :], total[:, :], 1.0 / DM, None, ALU.mult).then_inc(means, 1)
                dve.wait_ge(means, c + 1)
                dve.tensor_tensor(centred[:, :, :], x, mean[:, :].unsqueeze(2).broadcast_to([P, TC, DM]),
                                  ALU.subtract).then_inc(centre, 1)
                dve.wait_ge(squared, c + 1)
                dve.tensor_reduce(sqsum[:, :], squares[:, :, :], AX.X, ALU.add).then_inc(sqsums, 1)
                dve.wait_ge(sdevs, c + 1)
                dve.reciprocal(rstd[:, :], sdev[:, :]).then_inc(rstds, 1)
                dve.wait_ge(rstds, c + 1)
                dve.wait_ge(centre, c + 1)
                dve.tensor_tensor(normed[:, :, :], centred[:, :, :],
                                  rstd[:, :].unsqueeze(2).broadcast_to([P, TC, DM]), ALU.mult).then_inc(norms, 1)
                dve.wait_ge(q0_done, c + 1)
                dve.scalar_tensor_tensor(q_rest[:, :], ps_q[:, :], SCALE, q_split[:, 0, :],
                                         ALU.mult, ALU.subtract).then_inc(qr_done, 1)
                dve.wait_ge(k0_done, 2 * c + 2)
                dve.tensor_tensor(k_rest[:, :], kt[:, ds(c * CH, CH)], k_split[:, 0, :], ALU.subtract).then_inc(kr_done, 1)
                dve.wait_ge(qr_done, c + 1)
                dve.tensor_copy(q_split[:, 1, :], q_rest[:, :]).then_inc(q1_done, 1)
                dve.wait_ge(kr_done, c + 1)
                dve.tensor_copy(k_split[:, 1, :], k_rest[:, :]).then_inc(k1_done, 1)
                dve.wait_ge(q1_done, c + 1)
                dve.tensor_tensor(q_split[:, 2, :], q_rest[:, :], q_split[:, 1, :], ALU.subtract).then_inc(q2_done, 1)
                dve.wait_ge(k1_done, c + 1)
                dve.tensor_tensor(k_split[:, 2, :], k_rest[:, :], k_split[:, 1, :], ALU.subtract).then_inc(k2_done, 1)
            chunks(dve, chunk)
            dve.wait_ge(v_done, 2 * CHUNKS)
            dve.tensor_tensor(gates[:, :, :], gates[:, :, :], bg_rep[:, :].unsqueeze(1).broadcast_to([P, TILES, 3]),
                              ALU.add).then_inc(gate_step, 1)
            dve.wait_ge(gate_step, 1)
            dve.tensor_reduce(gate_max[:, :], gates[:, :, :], AX.X, ALU.max).then_inc(gate_step, 1)
            dve.wait_ge(gate_step, 2)
            dve.tensor_tensor(gates[:, :, :], gates[:, :, :], gate_max[:, :].unsqueeze(2).broadcast_to([P, TILES, 3]),
                              ALU.subtract).then_inc(gate_step, 1)
            dve.wait_ge(gate_exp, 1)
            dve.tensor_reduce(gate_sum[:, :], gates[:, :, :], AX.X, ALU.add).then_inc(gate_step, 1)
            dve.wait_ge(gate_step, 4)
            dve.reciprocal(gate_inv[:, :], gate_sum[:, :]).then_inc(gate_step, 1)
            dve.wait_ge(gate_step, 5)
            dve.tensor_tensor(gates[:, :, :], gates[:, :, :], gate_inv[:, :].unsqueeze(2).broadcast_to([P, TILES, 3]),
                              ALU.mult).then_inc(gate_step, 1)
            dve.wait_ge(gate_step, 6)
            dve.wait_ge(consts, 5)
            first = gates[:, :, :].rearrange("p (b i) k -> p b (i k)", b=B)[:, :, 0:1]
            dve.tensor_tensor(first, first, late[:, 0:1].unsqueeze(1).broadcast_to([P, B, 1]), ALU.mult).then_inc(gate_step, 1)
            dve.wait_ge(kc_ps, 1)
            dve.tensor_copy(kc_split[:, 0, :], ps_k[:, 0:B * NB]).then_inc(kc_step, 1)
            dve.wait_ge(kc_step, 1)
            dve.tensor_tensor(kc_rest[:, :], ps_k[:, 0:B * NB], kc_split[:, 0, :], ALU.subtract).then_inc(kc_step, 1)
            dve.wait_ge(kc_step, 2)
            dve.tensor_copy(kc_split[:, 1, :], kc_rest[:, :]).then_inc(kc_step, 1)
            dve.wait_ge(kc_step, 3)
            dve.tensor_tensor(kc_split[:, 2, :], kc_rest[:, :], kc_split[:, 1, :], ALU.subtract).then_inc(kc_step, 3)

        @block.tensor
        def _(pe):
            pe.wait_ge(w_in, 16 * N_W)
            pe.wait_ge(consts, 5)
            pe.transpose(ps_w[:, 0:DM], wq[:, :], ident_f[:, :]).then_inc(wt_ps, 1)
            pe.wait_ge(wqt_done, 1)
            pe.matmul(ps_w[:, DM:DM + 3], wqt[:, :], wg_rep[:, :], start=True, stop=True).then_inc(wg_ps, 1)
            pe.wait_ge(wvg_done, 2)
            def chunk(c):
                pe.wait_ge(norms, c + 1)
                if started(c):
                    pe.wait_ge(nt_done, c)
                for i in range(TC):
                    last = pe.transpose(ps_t[:, i * P:(i + 1) * P], normed[:, i, :], ident_f[:, :])
                last.then_inc(t_ps, 1)
                pe.wait_ge(nt_done, c + 1)
                if started(c):
                    pe.wait_ge(q2_done, c)
                pe.matmul(ps_q[:, :], wq[:, :], normed_t[:, :], start=True, stop=True).then_inc(q_ps, 1)
                if started(c):
                    pe.wait_ge(k0_done, 2 * c)
                pe.matmul(ps_k[:, :], wk[:, :], normed_t[:, :], start=True, stop=True).then_inc(k_ps, 1)
                if started(c):
                    pe.wait_ge(vt_done, c)
                pe.matmul(ps_vt[:, :], wv[:, :], normed_t[:, :], start=True, stop=True).then_inc(vt_ps, 1)
                if started(c):
                    pe.wait_ge(v_done, 2 * c)
                for i in range(TC):
                    last = pe.matmul(ps_v[:, i, 0:DM + 3], normed_t[:, i * P:(i + 1) * P], wvg[:, :], start=True, stop=True)
                last.then_inc(v_ps, 1)
            chunks(pe, chunk)
            pe.wait_ge(diag_made, 2 * G)
            pe.wait_ge(k0_done, 2 * CHUNKS)
            pe.wait_ge(vt_done, CHUNKS)
            for i, (src, dst, made) in enumerate(((kt, ps_k, kc_ps), (vt, ps_vt, vc_ps))):
                of_offset = src[:, :].rearrange("p (n g) -> p g n", g=G)
                for g in range(G):
                    last = pe.matmul(dst[:, 0:B * NB], wc_diag[:, i, g, :, :].rearrange("p h d -> p (h d)"),
                                     of_offset[:, g, :], start=(g == 0), stop=(g == G - 1))
                last.then_inc(made, 1)
            pe.wait_ge(vct_done, 1)
            for b in range(B):
                last = pe.transpose(ps_t[0:NB, b * P:(b + 1) * P], vct[:, b * NB:(b + 1) * NB], ident_f[:, :])
            last.then_inc(vc_tr, 1)


def attend(nc, dram, ident_b, ident_f):
    with ExitStack() as ctx:
        def sb(name, shape, dt=F32):
            return ctx.enter_context(nc.sbuf_tensor(name, shape, dt))

        def ps(name, shape, dt=F32):
            return ctx.enter_context(nc.psum_tensor(name, shape, dt))

        def sem(name):
            return ctx.enter_context(nc.semaphore(name))

        cmask = sb("cmask", [P, NT, NB], BF16)
        causal_q = sb("causal_q", [P, TOP * G], BF16)
        causal_k = sb("causal_k", [P, TOP * G], BF16)
        band_q = sb("band_q", [P, BAND], BF16)
        band_k = sb("band_k", [P, BAND], BF16)
        q_loc = [sb(f"q_loc{p}", [ROWS, HC, HG, CH], BF16) for p in range(2)]
        q_sel = [sb(f"q_sel{p}", [ROWS, HC, HG, CH], BF16) for p in range(2)]
        keys = [sb(f"keys{p}", [ROWS, HG, NK], BF16) for p in range(2)]
        q_first = sb("q_first", [R_SHIFT, HC, HG, CH], BF16)
        k_first = sb("k_first", [R_SHIFT, HG, NK], BF16)
        v_in = [sb(f"v_in{p}", [P, NT, HG * D]) for p in range(2)]
        v_pad = [sb(f"v_pad{p}", [P, NT, HG, 32]) for p in range(2)]
        vc_pad = [sb(f"vc_pad{p}", [P, 2, 64]) for p in range(2)]
        gate = [sb(f"gate{p}", [P, NT, 3]) for p in range(2)]
        logit = sb("logit", [P, NT, HG, TOP + NB])
        best = sb("best", [P, NT, HG, 8])
        marked = sb("marked", [P, NT, HG, TOP + NB])
        bias = sb("bias", [P, NT, HG, NB], BF16)
        block_max = sb("block_max", [P, NT, HG, NB])
        sel_max = sb("sel_max", [P, TC, HG, NB])
        prob_c = sb("prob_c", [P, NT, HG, NB])
        prob_ct = [sb(f"prob_ct{p}", [P, 2, T]) for p in range(2)]
        peak = sb("peak", [P, 2, 2, TC * HG])
        peak_rest = sb("peak_rest", [P, 2, TC * HG])
        shift = sb("shift", [P, 2, 3, TC * HG], BF16)
        bias_t = [sb(f"bias_t{n}", [P, 2, CH], BF16) for n in range(2)]
        shift_t = [sb(f"shift_t{n}", [6 * TC * HG, P], BF16) for n in range(2)]
        banded = sb("banded", [P, 2, HG, BAND], BF16)
        pad = sb("pad", [P, 4])
        turn = sb("turn", [P, 4])
        prob_s = [sb(f"prob_s{n}", [P, HG, CH]) for n in range(2)]
        prob_l = [sb(f"prob_l{n}", [P, HG, BAND]) for n in range(4)]
        mixed_t = [sb(f"mixed_t{n}", [P, CH]) for n in range(3)]
        weight = sb("weight", [P, 3, TC, HG])
        gated = sb("gated", [P, 3, TC, HG])
        part = sb("part", [P, 3, TC, HG, D])
        part2 = sb("part2", [P, TC, HG, D])
        mixed = sb("mixed", [P, NT, HG * D])

        ps_a = ps("ps_a", [P, 2, CH])
        ps_b = ps("ps_b", [P, 2, 2, CH])
        ps_o = ps("ps_o", [P, CH])
        ps_m = ps("ps_m", [P, CH])
        ps_mb = ps_m[:, :].bitcast(BF16)

        loaded_first = sem("loaded_first")
        loaded = [sem(f"loaded{p}") for p in range(2)]
        bias_in = [[sem(f"bias_in{p}{n}") for n in range(2)] for p in range(2)]
        shift_in = [[sem(f"shift_in{p}{n}") for n in range(2)] for p in range(2)]
        consts, const_step, v_ready, vc_zero = map(sem, ("s_consts", "s_const_step", "v_ready", "vc_zero"))
        m_full, m_free, a_full, a_read = map(sem, ("m_full", "m_free", "a_full", "a_read"))
        maxed, ranked, picked, bias_done = map(sem, ("maxed", "ranked", "picked", "bias_done"))
        centred_c, exp_c, bm_done, sel_done, shift_step = map(
            sem, ("centred_c", "exp_c", "bm_done", "sel_done", "shift_step"))
        b_full = sem("b_full")
        b_read = [sem(f"b_read{n}") for n in range(2)]
        pv_sel, pv_loc, pv_comp = map(sem, ("pv_sel", "pv_loc", "pv_comp"))
        o_free, recip, gated_done, summed, mixed_done = map(
            sem, ("o_free", "recip", "gated_done", "summed", "mixed_done"))
        mixed_out = [sem(f"mixed_out{p}") for p in range(2)]
        ctx.enter_context(nc.allow_non_contiguous_dma(reason="rows of heads"))
        block = ctx.enter_context(nc.Block())

        def steps(engine, step):
            step(None, (0, 0, 0))
            step((0, 0, 0), (1, 1, 0))
            step((1, 1, 0), (2, 0, 1))
            with engine.Fori(1, GROUPS // 2 - 1) as k:
                step((2 * k, 0, k), (2 * k + 1, 1, k))
                step((2 * k + 1, 1, k), (2 * k + 2, 0, k + 1))
            last = GROUPS // 2 - 1
            step((GROUPS - 2, 0, last), (GROUPS - 1, 1, last))
            step((GROUPS - 1, 1, last), None)

        N_LOAD1 = 2 * 3
        N_LOAD2 = 3 * 3 + 1 + HG + 1

        def load_splits(sp, to, name, group, sem):
            g = group[0]
            b, h0 = ds(g // QUADS, 1), ds(g % QUADS * HG, HG)
            at = R_SPLIT
            for n in (3, 2, 1):
                if name == "q":
                    src = dram["q"][b, 0:n * D, :, h0, :].rearrange("a r c h t -> (a r) c (h t)")
                    dst = to[at:at + n * D, :, :, :].rearrange("r c h t -> r c (h t)")
                    sp.dma_start(dst, src).then_inc(sem, 16)
                else:
                    s = 3 - n
                    src = (dram["k"][b, s * D:(s + 1) * D, h0, :].rearrange("a r h t -> a r (h t)")
                           .broadcast_to([n, D, HG * NK]))
                    sp.dma_start(to[at:at + n * D, :, :].rearrange("r h t -> r (h t)"), src).then_inc(sem, 16)
                at += n * D

        @block.sync
        def _(sp):
            def load_first(group):
                g, p, k = group
                if not is_first(group):
                    sp.wait_ge(a_full, A_USES * g)
                load_splits(sp, q_first, "q", group, loaded_first)
                load_splits(sp, k_first, "k", group, loaded_first)

            def load_second(group):
                g, p, k = group
                if not (isinstance(g, int) and g < 2):
                    sp.wait_ge(b_full, B_USES * (g - 1))
                load_splits(sp, keys[p], "k", group, loaded[p])
                load_splits(sp, q_sel[p], "q", group, loaded[p])
                load_splits(sp, q_loc[p], "q", group, loaded[p])
                rows = ds(g % QUADS * (HG * D), HG * D)
                sp.dma_start(v_in[p][:, :, :], dram["v"][ds(g // QUADS, 1), :, rows]
                             .rearrange("a (i p) r -> p (a i) r", p=P)).then_inc(loaded[p], 16)
                sp.dma_start(gate[p][:, :, :], dram["gates"][ds(g // QUADS, 1), :, :, :]
                             .rearrange("a p i k -> p (a i) k")).then_inc(loaded[p], 16)
                for h in range(HG):
                    r0, c0 = h % 2 * NB, h % 2 * 32
                    sp.dma_start(vc_pad[p][r0:r0 + NB, h // 2, c0:c0 + D],
                                 dram["vc"][ds(g // QUADS, 1), :, ds(g % QUADS * (HG * D) + h * D, D)]
                                 .rearrange("a n r -> n (a r)")).then_inc(loaded[p], 16)

            def place(group, n):
                g, p, k = group
                sp.wait_ge(m_free, M_USES * g + M_BIAS[n] + 1)
                for odd in range(2):
                    sp.dma_start(q_sel[p][0:NB, n, odd::2, :],
                                 bias_t[n][odd * NB:(odd + 1) * NB, :, :]).then_inc(bias_in[p][n], 16)

            def place_shift(group, n):
                g, p, k = group
                sp.wait_ge(m_free, M_USES * g + M_SHIFT[n] + 1)
                w = TC * HG
                for kind, q in enumerate((q_sel, q_loc)):
                    for s in range(3):
                        r0 = (3 * kind + s) * w
                        sp.dma_start(q[p][R_SHIFT + s:R_SHIFT + s + 1, n, :, :].rearrange("s h (i q) -> s (h i) q", q=P),
                                     shift_t[n][r0:r0 + w, :]).then_inc(shift_in[p][n], 16)

            def store(group, c):
                g, p, k = group
                sp.wait_ge(mixed_done, 2 * g + c + 1)
                b, quad = g // QUADS, g % QUADS
                sp.dma_start(dram["attn"][ds(b, 1), c * CH:(c + 1) * CH, ds(quad * HG * D, HG * D)]
                             .rearrange("a (i p) r -> p (a i) r", p=P), mixed[:, c * TC:(c + 1) * TC, :]).then_inc(mixed_out[c], 16)

            def step(second, first):
                if first:
                    if is_first(first):
                        sp.wait_ge(consts, N_CONST)
                        load_first(first)
                        load_second(first)
                    place(first, 0)
                    place(first, 1)
                if second:
                    store(second, 0)
                if first:
                    place_shift(first, 0)
                    if not is_last(first):
                        load_first(after(first))
                    place_shift(first, 1)
                if second:
                    store(second, 1)
                if first and not is_last(first):
                    load_second(after(first))
            steps(sp, step)
            for n in range(2):
                sp.wait_ge(mixed_out[n], 16 * GROUPS)

        @block.gpsimd
        def _(pool):
            for m in (cmask, causal_q, causal_k, band_q, band_k):
                pool.memset(m[...], 0.0).then_inc(const_step, 1)
            pool.memset(logit[:, :, :, 0:TOP], SENTINEL).then_inc(consts, 1)
            pool.memset(marked[:, :, :, :], 0.0).then_inc(consts, 1)
            pool.memset(block_max[:, :, :, :], 0.0).then_inc(consts, 1)
            pool.memset(q_first[0:R_SPLIT, :, :], 0.0).then_inc(consts, 1)
            pool.memset(k_first[0:R_SPLIT, :, :], 0.0).then_inc(consts, 1)
            for p in range(2):
                pool.memset(keys[p][0:R_SPLIT, :, :], 1.0).then_inc(const_step, 1)
                pool.memset(q_loc[p][0:R_SPLIT, :, :], 0.0).then_inc(consts, 1)
                pool.memset(v_pad[p][:, :, :, :], 0.0).then_inc(const_step, 1)
            pool.memset(turn[:, 0:1], 0.0).then_inc(const_step, 1)
            pool.wait_ge(const_step, 10)

            def reach(m, base, pattern, multiplier, done):
                pool.affine_select(out=m, in_=m, compare_op=ALU.is_ge, fill=OUT_OF_REACH, base=base,
                                   pattern=pattern, channel_multiplier=multiplier).then_inc(done, 1)
            reach(cmask[:, :, :], -G, [[P, NT], [-G, NB]], 1, consts)
            reach(causal_q[:, :], 0, [[-1, TOP * G]], 1, consts)
            reach(causal_k[:, :], 0, [[1, TOP * G]], -1, consts)
            reach(band_q[:, :], 0, [[1, BAND]], -1, const_step)
            reach(band_k[:, :], 0, [[1, BAND]], -1, const_step)
            pool.wait_ge(const_step, 12)
            reach(band_q[:, :], WIN, [[-1, BAND]], 1, consts)
            reach(band_k[:, :], WIN, [[-1, BAND]], 1, consts)
            for p in range(2):
                for h in range(HG):
                    pool.affine_select(out=keys[p][0:NB, h, 0:T], in_=keys[p][0:NB, h, 0:T], compare_op=ALU.is_ge, fill=0.0,
                                       base=0, pattern=[[1, T]], channel_multiplier=-G).then_inc(const_step, 1)
                pool.memset(v_pad[p][:, :, :, D:D + 1], 1.0).then_inc(consts, 1)
            pool.wait_ge(const_step, 12 + 2 * HG)
            for p in range(2):
                for h in range(HG):
                    pool.affine_select(out=keys[p][0:NB, h, 0:T], in_=keys[p][0:NB, h, 0:T], compare_op=ALU.is_ge, fill=0.0,
                                       base=G - 1, pattern=[[-1, T]], channel_multiplier=G).then_inc(consts, 1)

            def widen(group):
                g, p, k = group
                pool.wait_ge(loaded[p], 16 * N_LOAD2 * (k + 1))
                if not (isinstance(g, int) and g < 2):
                    pool.wait_ge(b_full, B_USES * (g - 1))
                pool.tensor_tensor(turn[:, 1:2], turn[:, 0:1], turn[:, 0:1], ALU.add)
                pool.tensor_copy(v_pad[p][:, :, :, 0:D], v_in[p][:, :, :].rearrange("p i (h d) -> p i h d", d=D)).then_inc(v_ready, 1)

            def choose(group, n):
                g, p, k = group
                at = slice(n * TC, (n + 1) * TC)
                pool.wait_ge(maxed, 2 * g + n + 1)
                if not is_first(group):
                    pool.wait_ge(m_full, M_USES * (g - 1) + M_PROB[n] + 1)
                pool.tensor_tensor(prob_c[:, at, :, :], logit[:, at, :, TOP:], best[:, at, :, 0:1].broadcast_to([P, TC, HG, NB]),
                                   ALU.subtract).then_inc(centred_c, 1)
                pool.wait_ge(picked, 2 * g + n + 1)
                if not is_first(group):
                    pool.wait_ge(m_full, M_USES * (g - 1) + M_BIAS[n] + 1)
                pool.tensor_tensor(turn[:, 2 + n:3 + n], turn[:, 0:1], turn[:, 0:1], ALU.add)
                pool.tensor_scalar(bias[:, at, :, :], marked[:, at, :, TOP:], TAKEN / 2, OUT_OF_REACH,
                                   ALU.is_lt, ALU.mult).then_inc(bias_done, 1)

            def masked_max(group, n):
                g, p, k = group
                at = slice(n * TC, (n + 1) * TC)
                pool.wait_ge(a_read, A_USES * g + A_END[n])
                pool.wait_ge(bias_done, 2 * g + n + 1)
                if n or not is_first(group):
                    pool.wait_ge(sel_done, 2 * g + n)
                pool.tensor_tensor(sel_max[:, :, :, :], block_max[:, at, :, :], bias[:, at, :, :], ALU.add).then_inc(bm_done, 1)

            def total(group, c):
                g, p, k = group
                for n in range(2):
                    pool.wait_ge(b_read[n], b_count(g, B_BACK[c] + n) + 1)
                pool.tensor_tensor(part2[:, :, :, :], part[:, 0, :, :, :], part[:, 1, :, :, :], ALU.add).then_inc(summed, 1)
                pool.wait_ge(summed, 2 * g + c + 1)
                if not is_first(group):
                    pool.wait_ge(mixed_out[c], 16 * g)
                pool.tensor_tensor(mixed[:, c * TC:(c + 1) * TC, :].rearrange("p i (h d) -> p i h d", d=D),
                                   part2[:, :, :, :], part[:, 2, :, :, :], ALU.add).then_inc(mixed_done, 1)

            def step(second, first):
                if first:
                    widen(first)
                    choose(first, 0)
                    choose(first, 1)
                if second:
                    total(second, 0)
                if first:
                    masked_max(first, 0)
                    masked_max(first, 1)
                if second:
                    total(second, 1)
            steps(pool, step)

        @block.scalar
        def _(act):
            def take(group, use):
                g, p, k = group
                what, n = M_WHAT[use]
                old = is_first(group)
                act.wait_ge(m_full, M_USES * g + use + 1)
                if what == "logit":
                    if not old:
                        act.wait_ge(picked, 2 * (g - 1) + n // 2 + 1)
                        act.wait_ge(centred_c, 2 * (g - 1) + n // 2 + 1)
                    out, in_ = logit[:, 2 * n:2 * n + 2, :, TOP:], ps_m[:, :].rearrange("p (i h n) -> p i h n", i=2, n=NB)
                elif what == "bias":
                    if not old:
                        kk = k - 1 + p
                        act.wait_ge(bias_in[1 - p][n], 16 * 2 * (kk + 1))
                    out, in_ = bias_t[n][:, :, :], ps_mb.rearrange("p (r t) -> p r t", r=2)
                elif what == "prob":
                    half, pair = n
                    out, in_ = prob_ct[p][:, pair, half * CH:(half + 1) * CH], ps_m[:, :]
                    if not (isinstance(g, int) and g < 2):
                        act.wait_ge(b_full, B_USES * (g - 1))
                elif what == "shift":
                    if not old:
                        kk = k - 1 + p
                        act.wait_ge(shift_in[1 - p][n], 16 * 6 * (kk + 1))
                    out, in_ = shift_t[n][:, :], ps_mb[0:6 * TC * HG, 0:P]
                act.activation(out, in_, ACT.Copy).then_inc(m_free, 1)

            def exp_comp(group, n):
                g, p, k = group
                at = slice(n * TC, (n + 1) * TC)
                act.wait_ge(centred_c, 2 * g + n + 1)
                act.activation(prob_c[:, at, :, :], prob_c[:, at, :, :], ACT.Exp).then_inc(exp_c, 1)

            def exps(group, n):
                g, p, k = group
                kind, c, j = SECOND[n]
                if kind == "selected":
                    r, w = SEL.index((c, j)), width(c, j)
                    for pair in range(2):
                        u = B_SEL[r] + pair
                        act.wait_ge(b_full, B_USES * g + u + 1)
                        if pair == 0 and not (is_first(group) and r < 2):
                            act.wait_ge(pv_sel, len(SEL) * g + r - 1)
                        act.activation(prob_s[r % 2][:, 2 * pair:2 * pair + 2, 0:w], ps_b[:, u % 2, :, 0:w],
                                       ACT.Exp).then_inc(b_read[u % 2], 1)
                elif kind == "local":
                    u, w = B_LOC[j], band_width(j)
                    act.wait_ge(b_full, B_USES * g + u + 1)
                    if not (is_first(group) and j < 3):
                        act.wait_ge(pv_loc, NT * g + max(j - 2, 0))
                    act.activation(prob_l[j % 4][:, :, 0:w].rearrange("p (a h) q -> p a h q", a=2),
                                   ps_b[:, u % 2, :, 0:2 * BAND].rearrange("p a (h q) -> p a h q", h=2)[:, :, :, 0:w],
                                   ACT.Exp).then_inc(b_read[u % 2], 1)

            def evacuate(group, c, kind):
                g, p, k = group
                if kind == 0:
                    act.wait_ge(pv_sel, len(SEL) * g + (TC, len(SEL))[c])
                elif kind == 1:
                    act.wait_ge(pv_loc, NT * g + TC * (c + 1))
                else:
                    act.wait_ge(pv_comp, 2 * g + c + 1)
                if c or not is_first(group):
                    act.wait_ge(b_full, B_USES * g + (0, B_BACK[0] + 2)[c])
                act.activation(mixed_t[kind][:, :], ps_o[:, :], ACT.Copy).then_inc(o_free, 1)

            def step(second, first):
                for n in range(len(SECOND) + 1):
                    if second:
                        if n < len(SECOND):
                            exps(second, n)
                        if n and SECOND[n - 1][0] != SECOND[n % len(SECOND)][0] and SECOND[n - 1][0] != "compressed":
                            evacuate(second, SECOND[n - 1][1], ("selected", "local").index(SECOND[n - 1][0]))
                        if n < len(SECOND) and SECOND[n][0] == "compressed":
                            evacuate(second, SECOND[n][1], 2)
                    if first:
                        for use in FIRST_AT.get(n, ()):
                            take(first, use)
                        for half in range(2):
                            if n == EXP_AT[half]:
                                exp_comp(first, half)
            act.wait_ge(consts, N_CONST)
            steps(act, step)

        @block.vector
        def _(dve):
            def rank(group, n):
                g, p, k = group
                tiles = range(n * TC, (n + 1) * TC)
                at = slice(n * TC, (n + 1) * TC)
                dve.wait_ge(m_free, M_USES * g + M_LOGIT[2 * n + 1] + 1)
                if not is_first(group):
                    dve.wait_ge(centred_c, 2 * (g - 1) + n + 1)
                dve.memset(pad[:, 2 * n:2 * n + 1], 0.0)
                for i in tiles:
                    for h in range(HG):
                        last = dve.max(best[:, i, h, :], logit[:, i, h, 0:TOP + NB // NT * (i + 1)])
                last.then_inc(maxed, 1)
                dve.wait_ge(maxed, 2 * g + n + 1)
                dve.memset(best[:, at, :, TOP:], SENTINEL).then_inc(ranked, 1)
                dve.wait_ge(ranked, 2 * g + n + 1)
                if not is_first(group):
                    dve.wait_ge(bias_done, 2 * (g - 1) + n + 1)
                dve.memset(pad[:, 2 * n + 1:2 * n + 2], 0.0)
                for i in tiles:
                    for h in range(HG):
                        w = TOP + NB // NT * (i + 1)
                        last = dve.match_replace(marked[:, i, h, 0:w], best[:, i, h, :], logit[:, i, h, 0:w], TAKEN)
                last.then_inc(picked, 1)

            def block_maxima(group, u):
                g, p, k = group
                i, heads, k0, w, local = A_UNITS[u]
                n = i // TC
                bank = ps_a[:, u % 2, 0:len(heads) * w]
                dve.wait_ge(a_full, A_USES * g + u + 1)
                if u in (0, A_END[0]) and not is_first(group):
                    dve.wait_ge(bm_done, 2 * (g - 1) + n + 1)
                last = dve.tensor_reduce(block_max[:, i, heads[0]:heads[0] + len(heads), k0 // G:(k0 + w) // G],
                                         bank.rearrange("p (h b t) -> p h b t", h=len(heads), t=G), AX.X, ALU.max)
                for n_h, h in enumerate(heads if local else ()):
                    first_key = max(i * P - WIN, 0)
                    of = n_h * w + first_key - k0
                    size = (i + 1) * P - first_key
                    last = dve.tensor_tensor_reduce(
                        out=banded[:, u % 2, h, 0:size], in0=ps_a[:, u % 2, of:of + size], in1=band_q[:, BAND - size:],
                        scale=1.0, scalar=SENTINEL, op0=ALU.add, op1=ALU.max,
                        accum_out=peak[:, n, 1, h * TC + i % TC:h * TC + i % TC + 1])
                last.then_inc(a_read, 1)

            def shifts(group, n):
                g, p, k = group
                dve.wait_ge(bm_done, 2 * g + n + 1)
                dve.tensor_reduce(peak[:, n, 0, :].rearrange("p (h i) -> p i h", h=HG), sel_max[:, :, :, :],
                                  AX.X, ALU.max).then_inc(sel_done, 1)
                dve.wait_ge(sel_done, 2 * g + n + 1)
                if n or not is_first(group):
                    dve.wait_ge(m_full, M_USES * g + (0, M_SHIFT[0] + 1)[n])
                s0 = 8 * g + 4 * n
                dve.tensor_scalar(shift[:, :, 0, :], peak[:, n, :, :], -1.0, None, ALU.mult).then_inc(shift_step, 1)
                dve.wait_ge(shift_step, s0 + 1)
                dve.scalar_tensor_tensor(peak_rest[:, :, :], peak[:, n, :, :], -1.0, shift[:, :, 0, :],
                                         ALU.mult, ALU.subtract).then_inc(shift_step, 1)
                dve.wait_ge(shift_step, s0 + 2)
                dve.tensor_copy(shift[:, :, 1, :], peak_rest[:, :, :]).then_inc(shift_step, 1)
                dve.wait_ge(shift_step, s0 + 3)
                dve.tensor_tensor(shift[:, :, 2, :], peak_rest[:, :, :], shift[:, :, 1, :], ALU.subtract).then_inc(shift_step, 1)

            def weigh(group, c):
                g, p, k = group
                done = 4 * g + 2 * c
                if c or not is_first(group):
                    dve.wait_ge(mixed_done, 2 * g + c)
                dve.wait_ge(loaded[p], 16 * N_LOAD2 * (k + 1))
                for n, (kinds, gates) in enumerate(((slice(0, 2), slice(1, 3)), (slice(2, 3), slice(0, 1)))):
                    u = B_BACK[c] + n
                    m = kinds.stop - kinds.start
                    sums = ps_b[:, u % 2, 0:m, :].rearrange("p s (i h r) -> p s i h r", i=TC, h=HG)
                    dve.wait_ge(b_full, B_USES * g + u + 1)
                    dve.reciprocal(weight[:, kinds, :, :], sums[:, :, :, :, D]).then_inc(recip, 1)
                    dve.wait_ge(recip, done + n + 1)
                    dve.tensor_tensor(gated[:, kinds, :, :], weight[:, kinds, :, :],
                                      gate[p][:, c * TC:(c + 1) * TC, gates].rearrange("p i s -> p s i").unsqueeze(3)
                                      .broadcast_to([P, m, TC, HG]), ALU.mult).then_inc(gated_done, 1)
                    dve.wait_ge(gated_done, done + n + 1)
                    for s in range(m):
                        last = dve.tensor_tensor(part[:, kinds.start + s, :, :, :], sums[:, s, :, :, 0:D],
                                                 gated[:, kinds.start + s, :, :].unsqueeze(3).broadcast_to([P, TC, HG, D]), ALU.mult)
                    last.then_inc(b_read[u % 2], 1)

            def step(second, first):
                if first:
                    rank(first, 0)
                    rank(first, 1)
                for n in range(len(SECOND) + 1):
                    if second and n == BACK_AT[0]:
                        weigh(second, 0)
                    if first:
                        for u in range(A_USES):
                            if A_AT[u] == n:
                                block_maxima(first, u)
                        if n == SHIFT_AT[0] - 1:
                            shifts(first, 0)
                if second:
                    weigh(second, 1)
                if first:
                    shifts(first, 1)
            for p in range(2):
                dve.memset(keys[p][R_SPLIT:ROWS, :, :], 1.0).then_inc(consts, 1)
                dve.memset(vc_pad[p][:, :, :], 0.0).then_inc(vc_zero, 1)
            dve.wait_ge(vc_zero, 2)
            for p in range(2):
                for h in range(2):
                    dve.memset(vc_pad[p][h * NB:(h + 1) * NB, :, 32 * h + D:32 * h + D + 1], 1.0).then_inc(consts, 1)
            dve.wait_ge(consts, N_CONST)
            steps(dve, step)

        @block.tensor
        def _(pe):
            def bank_m(group, use):
                g, p, k = group
                if not (is_first(group) and use == 0):
                    pe.wait_ge(m_free, M_USES * g + use)

            def first_part(group, use):
                g, p, k = group
                what, n = M_WHAT[use]
                if what == "logit":
                    if n == 0:
                        pe.wait_ge(loaded_first, 16 * N_LOAD1 * (g + 1))
                    bank_m(group, use)
                    for i in (2 * n, 2 * n + 1):
                        at = i % 2 * HG * NB
                        pe.matmul(ps_m[:, at:at + HG * NB], ident_b[:, :],
                                  cmask[:, i, :].unsqueeze(1).broadcast_to([P, HG, NB]), start=True, stop=False)
                        for h in range(HG):
                            last = pe.matmul(ps_m[:, at + h * NB:at + (h + 1) * NB], q_first[:, i // TC, h, i % TC * P:(i % TC + 1) * P],
                                             k_first[:, h, T:NK], start=False, stop=(h == HG - 1))
                elif what == "bias":
                    pe.wait_ge(bias_done, 2 * g + n + 1)
                    bank_m(group, use)
                    for pair in range(2):
                        for i in range(TC):
                            at = (pair * TC + i) * P
                            last = pe.transpose(ps_mb[:, at:at + P],
                                                bias[:, n * TC + i, 2 * pair:2 * pair + 2, :].rearrange("p h n -> p (h n)"), ident_b[:, :])
                elif what == "prob":
                    half, pair = n
                    pe.wait_ge(exp_c, 2 * g + half + 1)
                    bank_m(group, use)
                    for i in range(TC):
                        last = pe.transpose(ps_m[:, i * P:(i + 1) * P],
                                            prob_c[:, half * TC + i, 2 * pair:2 * pair + 2, :].rearrange("p h n -> p (h n)"), ident_f[:, :])
                else:
                    pe.wait_ge(shift_step, 8 * g + 4 * n + 4)
                    bank_m(group, use)
                    last = pe.transpose(ps_mb[0:6 * TC * HG, 0:P], shift[:, :, :, :].rearrange("p a s r -> p (a s r)"), ident_b[:, :])
                last.then_inc(m_full, 1)

            def logits_a(group, u):
                g, p, k = group
                i, heads, k0, w, local = A_UNITS[u]
                if not (is_first(group) and u < 2):
                    pe.wait_ge(a_read, A_USES * g + u - 1)
                for n_h, h in enumerate(heads):
                    last = pe.matmul(ps_a[:, u % 2, n_h * w:(n_h + 1) * w], q_first[:, i // TC, h, i % TC * P:(i % TC + 1) * P],
                                     k_first[:, h, k0:k0 + w], start=True, stop=(i > 0))
                    if i == 0:
                        last = pe.matmul(ps_a[:, u % 2, n_h * w:n_h * w + TOP * G], ident_b[:, :], causal_q[:, :],
                                         start=False, stop=True)
                last.then_inc(a_full, 1)

            def bank_b(group, u):
                if not (is_first(group) and u < 2):
                    pe.wait_ge(b_read[u % 2], b_count(group[0], u))

            def logits_b(group, n):
                g, p, k = group
                kind, c, j = SECOND[n]
                tile = slice(j * P, (j + 1) * P)
                if kind == "selected":
                    r, w = SEL.index((c, j)), width(c, j)
                    if j == 0:
                        if c == 0:
                            pe.wait_ge(loaded[p], 16 * N_LOAD2 * (k + 1))
                        pe.wait_ge(bias_in[p][c], 16 * 2 * (k + 1))
                        pe.wait_ge(shift_in[p][c], 16 * 6 * (k + 1))
                    for pair in range(2):
                        u = B_SEL[r] + pair
                        bank_b(group, u)
                        for n_h in range(2):
                            h = 2 * pair + n_h
                            partial = c == 0 and j == 0
                            last = pe.matmul(ps_b[:, u % 2, n_h, 0:w], keys[p][:, h, tile], q_sel[p][:, c, h, CH - w:],
                                             start=True, stop=not partial)
                            if partial:
                                last = pe.matmul(ps_b[:, u % 2, n_h, 0:TOP * G], ident_b[:, :], causal_k[:, :],
                                                 start=False, stop=True)
                        last.then_inc(b_full, 1)
                elif kind == "local":
                    u, w = B_LOC[j], band_width(j)
                    if j == TC - 1:
                        pe.wait_ge(shift_in[p][1], 16 * 6 * (k + 1))
                    bank_b(group, u)
                    for h in range(HG):
                        out = ps_b[:, u % 2, h // 2, h % 2 * BAND:h % 2 * BAND + w]
                        at = j % TC * P
                        here = min(w, CH - at)
                        pe.matmul(out[:, 0:here], keys[p][:, h, tile], q_loc[p][:, c, h, at:at + here], start=True, stop=False)
                        if here < w:
                            pe.matmul(out[:, here:w], keys[p][:, h, tile], q_loc[p][:, c + 1, h, 0:w - here], start=False, stop=False)
                        last = pe.matmul(out, ident_b[:, :], band_k[:, 0:w], start=False, stop=True)
                    last.then_inc(b_full, 1)

            def sums(group, n):
                g, p, k = group
                kind, c, j = SECOND[n]
                if kind == "selected":
                    r, w = SEL.index((c, j)), width(c, j)
                    if j == 0:
                        if c == 0:
                            pe.wait_ge(v_ready, g + 1)
                        if c or not is_first(group):
                            pe.wait_ge(o_free, 6 * g + 3 * c)
                    for pair in range(2):
                        u = B_SEL[r] + pair
                        pe.wait_ge(b_read[u % 2], b_count(g, u) + 1)
                    for h in range(HG):
                        last = pe.matmul(ps_o[32 * h:32 * h + 32, CH - w:], v_pad[p][:, j, h, :],
                                         prob_s[r % 2][:, h, 0:w], start=(j == 0), stop=(j == TC * (c + 1) - 1))
                    last.then_inc(pv_sel, 1)
                elif kind == "local":
                    u = B_LOC[j]
                    at = j % TC * P
                    if j % TC == 0:
                        pe.wait_ge(o_free, 6 * g + 3 * c + 1)
                    pe.wait_ge(b_read[u % 2], b_count(g, u) + 1)
                    for h in range(HG):
                        last = pe.matmul(ps_o[32 * h:32 * h + 32, at:at + P], v_pad[p][:, j, h, :],
                                         prob_l[j % 4][:, h, 0:P], start=True, stop=(j == 0))
                    if j:
                        for h in range(HG):
                            last = pe.matmul(ps_o[32 * h:32 * h + 32, at:at + WIN], v_pad[p][:, j - 1, h, :],
                                             prob_l[(j - 1) % 4][:, h, P:BAND], start=False, stop=True)
                    last.then_inc(pv_loc, 1)
                else:
                    pe.wait_ge(o_free, 6 * g + 3 * c + 2)
                    pe.wait_ge(m_free, M_USES * g + M_PROB[c] + 1)
                    for pair in range(2):
                        last = pe.matmul(ps_o[64 * pair:64 * pair + 64, :], vc_pad[p][:, pair, :],
                                         prob_ct[p][:, pair, c * CH:(c + 1) * CH], start=True, stop=True)
                    last.then_inc(pv_comp, 1)

            def back(group, c):
                g, p, k = group
                pe.wait_ge(o_free, 6 * g + 3 * c + 3)
                for n, kinds in enumerate(((0, 1), (2,))):
                    u = B_BACK[c] + n
                    bank_b(group, u)
                    for s, kind in enumerate(kinds):
                        for i in range(TC):
                            last = pe.transpose(ps_b[:, u % 2, s, i * P:(i + 1) * P], mixed_t[kind][:, i * P:(i + 1) * P], ident_f[:, :])
                    last.then_inc(b_full, 1)

            def step(second, first):
                for n in range(len(SECOND) + 1):
                    if second:
                        if n < len(SECOND):
                            logits_b(second, n)
                        if n and SECOND[n - 1][0] != "compressed":
                            sums(second, n - 1)
                        if n < len(SECOND) and SECOND[n][0] == "compressed":
                            sums(second, n)
                        if n in BACK_AT:
                            back(second, BACK_AT.index(n))
                    if first:
                        for u in range(A_USES):
                            if A_AT[u] == n:
                                logits_a(first, u)
                        for use in FIRST_AT.get(n, ()):
                            first_part(first, use)
            pe.wait_ge(consts, N_CONST)
            steps(pe, step)


def feed_forward(nc, dram, ident_f, ident_b):
    with ExitStack() as ctx:
        def sb(name, shape, dt=F32):
            return ctx.enter_context(nc.sbuf_tensor(name, shape, dt))

        def ps(name, shape, dt=F32):
            return ctx.enter_context(nc.psum_tensor(name, shape, dt))

        def sem(name):
            return ctx.enter_context(nc.semaphore(name))

        NE1 = E + 1
        PAD = 8 - K2
        wo = sb("wo", [P, DM])
        w1 = sb("w1", [P, E, F])
        w2 = sb("w2", [P, E, DM])
        w_gu = sb("w_gu", [P, 2 * F])
        w_sd = sb("w_sd", [P, DM])
        w_rs = sb("w_rs", [P, NE1])
        xr = sb("xr", [P, TILES, DM])
        attn = [sb(f"attn_in{p}", [P, TC, DM]) for p in range(2)]
        attn_t = sb("attn_t", [P, CH])
        total = sb("total3", [P, TILES])
        mean = sb("mean3", [P, TILES])
        centred = sb("centred3", [P, TILES, DM])
        squares = sb("squares3", [P, TC, DM])
        sqsum = sb("sqsum3", [P, TILES])
        rstd = sb("rstd3", [P, TILES])
        eps = sb("eps3", [P, 1])
        normed = sb("normed3", [P, TC, DM])
        nt_chunk = sb("nt_chunk", [P, CH])
        nt = sb("nt", [P, B * T])
        logit = sb("logit3", [P, TILES, PAD + E])
        best = sb("best3", [P, TILES, 8])
        marked = sb("marked3", [P, TILES, PAD + E])
        chosen = sb("chosen", [P, TILES, E])
        prob = sb("prob3", [P, TILES, E])
        prob_sum = sb("prob_sum", [P, TILES])
        prob_inv = sb("prob_inv", [P, TILES])
        share = sb("share", [P, TILES, NE1])
        share_rest = sb("share_rest", [P, TILES, NE1])
        share_split = sb("share_split", [P, TILES, P], BF16)
        share_t = sb("share_t", [P, B * T], BF16)
        spread = sb("spread", [P, NE1, P], BF16)
        hidden = [sb(f"hidden{n}", [P, CH]) for n in range(3)]
        shared = sb("shared", [P, CH])
        weighed = [sb(f"weighed{n}", [P, CH]) for n in range(3)]
        out_t = sb("out_t", [P, CH])
        out_sb = sb("out_sb", [P, TC, DM])

        ps_t = ps("ps_t3", [P, CH])
        ps_y = ps("ps_y3", [P, TC, DM])
        ps_h = ps("ps_h3", [P, 2, CH])
        ps_c = ps("ps_c3", [P, 2, CH])
        ps_out = ps("ps_out3", [P, CH])

        a_in = [sem(f"a_in{p}") for p in range(2)]
        x3_in, w3_in, consts, const_step = map(sem, ("x3_in", "w3_in", "consts3", "const_step3"))
        at_ps, at_done, y_ps, added, totals, means, centre, squared, sqsums = map(
            sem, ("at_ps", "at_done", "y_ps", "added3", "totals3", "means3", "centre3", "squared3", "sqsums3"))
        sdevs, rstds, norms, t_ps, nt_done, l_ps, l_done = map(
            sem, ("sdevs3", "rstds3", "norms3", "t_ps3", "nt_done3", "l_ps3", "l_done3"))
        route, exp_done, ct_ps, ct_done = map(sem, ("route", "exp_done3", "ct_ps", "ct_done"))
        h_full, c_full, c_read, down, both, o_done, out_done = map(
            sem, ("h_full", "c_full", "c_read", "down", "both", "o_done", "out_done"))
        h_read = [sem(f"h_read{n}") for n in range(2)]
        stored = sem("stored")
        block = ctx.enter_context(nc.Block())
        N_W = 7

        def chunks(engine, chunk):
            chunk(0, 0, 0)
            chunk(1, 1, 0)
            with engine.Fori(1, CHUNKS // 2) as k:
                chunk(2 * k, 0, k)
                chunk(2 * k + 1, 1, k)

        def started(c):
            return not (isinstance(c, int) and c == 0)

        @block.sync
        def _(sp):
            def chunk(c, p, k):
                if not isinstance(c, int):
                    sp.wait_ge(at_ps, c - 1)
                sp.dma_start(attn[p][:, :, :], dram["attn"].rearrange("b t r -> (b t) r")[ds(c * CH, CH), :]
                             .rearrange("(i p) r -> p i r", p=P)).then_inc(a_in[p], 16)
            chunks(sp, chunk)

            def store(c, p, k):
                sp.wait_ge(out_done, c + 1)
                sp.dma_start(dram["out"][ds(c * CH, CH), :].rearrange("(i p) n -> p i n", p=P), out_sb[:, :, :]).then_inc(stored, 16)
            chunks(sp, store)
            sp.wait_ge(stored, 16 * CHUNKS)

        @block.gpsimd
        def _(pool):
            pool.memset(spread[:, :, :], 0.0).then_inc(const_step, 1)
            pool.memset(share_split[:, :, :], 0.0).then_inc(consts, 1)
            pool.memset(eps[:, :], EPS).then_inc(consts, 1)
            pool.memset(logit[:, :, 0:PAD], SENTINEL).then_inc(consts, 1)
            for s in range(3):
                pool.wait_ge(const_step, s + 1)
                pool.affine_select(out=spread[:, :, :], in_=spread[:, :, :], compare_op=ALU.not_equal, fill=1.0,
                                   base=-s * NE1, pattern=[[-1, NE1], [0, P]], channel_multiplier=1).then_inc(const_step, 1)
            pool.wait_ge(const_step, 4)

            def chunk(c, p, k):
                pool.wait_ge(centre, c + 1)
                if started(c):
                    pool.wait_ge(sqsums, c)
                x = centred[:, ds(c * TC, TC), :]
                pool.tensor_tensor(squares[:, :, :], x, x, ALU.mult).then_inc(squared, 1)
            chunks(pool, chunk)

        @block.scalar
        def _(act):
            act.dma_start(wo[:, :], dram["wo"]).then_inc(w3_in, 16)
            for c in range(CHUNKS):
                act.dma_start(xr[:, c * TC:(c + 1) * TC, :],
                              dram["x"][c * CH:(c + 1) * CH, :].rearrange("(i p) n -> p i n", p=P)).then_inc(x3_in, 16)
            act.dma_start(w_rs[:, 0:E], dram["router_w"]).then_inc(w3_in, 16)
            act.dma_start(w_rs[:, E:NE1], dram["sgate_w"]).then_inc(w3_in, 16)
            act.dma_start(w1[:, :, :], dram["w1"].rearrange("e d f -> d e f")).then_inc(w3_in, 16)
            act.dma_start(w2[:, :, :], dram["w2"].rearrange("e f d -> f e d")).then_inc(w3_in, 16)
            act.dma_start(w_gu[:, :], dram["sgu"]).then_inc(w3_in, 16)
            act.dma_start(w_sd[:, :], dram["sdown"]).then_inc(w3_in, 16)
            act.wait_ge(consts, 3)

            def copy_attn(c, p, k):
                act.wait_ge(at_ps, c + 1)
                if started(c):
                    act.wait_ge(y_ps, c)
                act.activation(attn_t[:, :], ps_t[:, :], ACT.Copy).then_inc(at_done, 1)
            chunks(act, copy_attn)
            act.wait_ge(sqsums, CHUNKS)
            act.activation(sqsum[:, :], sqsum[:, :], ACT.Sqrt, bias=eps[:, 0:1], scale=1.0 / DM).then_inc(sdevs, 1)

            def copy_normed(c, p, k):
                act.wait_ge(t_ps, c + 1)
                if started(c):
                    act.wait_ge(l_ps, c)
                act.activation(nt_chunk[:, :], ps_t[:, :], ACT.Copy).then_inc(nt_done, 1)
                act.activation(nt[:, ds(c * CH, CH)], ps_t[:, :], ACT.Copy).then_inc(nt_done, 1)
                act.wait_ge(l_ps, c + 1)
                act.activation(logit[:, ds(c * TC, TC), PAD:], ps_y[:, :, 0:E], ACT.Copy).then_inc(l_done, 1)
                act.activation(share[:, ds(c * TC, TC), E:NE1], ps_y[:, :, E:NE1], ACT.Copy).then_inc(l_done, 1)
            chunks(act, copy_normed)
            act.wait_ge(l_done, 2 * CHUNKS)
            act.activation(share[:, :, E:NE1], share[:, :, E:NE1], ACT.Exp, scale=-1.0).then_inc(exp_done, 1)
            act.wait_ge(route, 2)
            act.activation(prob[:, :, :], prob[:, :, :], ACT.Exp).then_inc(exp_done, 1)
            for n in range(4):
                act.wait_ge(ct_ps, n + 1)
                act.activation(share_t[:, n * 2 * CH:(n + 1) * 2 * CH], ps_t[:, :].bitcast(BF16), ACT.Copy).then_inc(ct_done, 1)

            def experts(c, p, k):
                for e in range(NE1):
                    act.wait_ge(h_full, (NE1 + 1) * c + e + 1)
                    if e >= 3 or started(c):
                        act.wait_ge(c_read, NE1 * c + e - 2)
                    act.activation(hidden[e % 3][:, :], ps_h[:, e % 2, :], ACT.Silu).then_inc(h_read[e % 2], 1)
                act.wait_ge(down, NE1 * (c + 1))
                if started(c):
                    act.wait_ge(c_full, (NE1 + 1) * c)
                act.activation(out_t[:, :], ps_out[:, :], ACT.Copy).then_inc(o_done, 1)
            chunks(act, experts)

        @block.vector
        def _(dve):
            dve.wait_ge(x3_in, 16 * CHUNKS)
            dve.wait_ge(consts, 3)

            def residual(c, p, k):
                at = ds(c * TC, TC)
                dve.wait_ge(y_ps, c + 1)
                dve.tensor_tensor(xr[:, at, :], xr[:, at, :], ps_y[:, :, :], ALU.add).then_inc(added, 1)
                dve.wait_ge(added, c + 1)
                dve.tensor_reduce(total[:, at], xr[:, at, :], AX.X, ALU.add).then_inc(totals, 1)
                dve.wait_ge(totals, c + 1)
                dve.tensor_scalar(mean[:, at], total[:, at], 1.0 / DM, None, ALU.mult).then_inc(means, 1)
                dve.wait_ge(means, c + 1)
                dve.tensor_tensor(centred[:, at, :], xr[:, at, :], mean[:, at].unsqueeze(2).broadcast_to([P, TC, DM]),
                                  ALU.subtract).then_inc(centre, 1)
                dve.wait_ge(squared, c + 1)
                dve.tensor_reduce(sqsum[:, at], squares[:, :, :], AX.X, ALU.add).then_inc(sqsums, 1)
            chunks(dve, residual)
            dve.wait_ge(sdevs, 1)
            dve.reciprocal(rstd[:, :], sqsum[:, :]).then_inc(rstds, 1)
            dve.wait_ge(rstds, 1)

            def norm(c, p, k):
                at = ds(c * TC, TC)
                if started(c):
                    dve.wait_ge(t_ps, c)
                dve.tensor_tensor(normed[:, :, :], centred[:, at, :], rstd[:, at].unsqueeze(2).broadcast_to([P, TC, DM]),
                                  ALU.mult).then_inc(norms, 1)
            chunks(dve, norm)
            dve.wait_ge(l_done, 2 * CHUNKS)
            for i in range(TILES):
                last = dve.max(best[:, i, :], logit[:, i, :])
            last.then_inc(route, 1)
            dve.wait_ge(route, 1)
            dve.tensor_tensor(prob[:, :, :], logit[:, :, PAD:], best[:, :, 0:1].broadcast_to([P, TILES, E]), ALU.subtract).then_inc(route, 1)
            dve.memset(best[:, :, K2:], SENTINEL).then_inc(route, 1)
            dve.wait_ge(route, 3)
            for i in range(TILES):
                last = dve.match_replace(marked[:, i, :], best[:, i, :], logit[:, i, :], TAKEN)
            last.then_inc(route, 1)
            dve.wait_ge(exp_done, 2)
            dve.tensor_reduce(prob_sum[:, :], prob[:, :, :], AX.X, ALU.add).then_inc(route, 1)
            dve.tensor_scalar(share[:, :, E:NE1], share[:, :, E:NE1], 1.0, None, ALU.add).then_inc(route, 1)
            dve.wait_ge(route, 6)
            dve.reciprocal(prob_inv[:, :], prob_sum[:, :]).then_inc(route, 1)
            dve.reciprocal(share[:, :, E:NE1], share[:, :, E:NE1]).then_inc(route, 1)
            dve.tensor_scalar(chosen[:, :, :], marked[:, :, PAD:], TAKEN / 2, None, ALU.is_ge).then_inc(route, 1)
            dve.wait_ge(route, 9)
            dve.tensor_tensor(chosen[:, :, :], chosen[:, :, :], prob[:, :, :], ALU.mult).then_inc(route, 1)
            dve.wait_ge(route, 10)
            dve.tensor_tensor(share[:, :, 0:E], chosen[:, :, :], prob_inv[:, :].unsqueeze(2).broadcast_to([P, TILES, E]),
                              ALU.mult).then_inc(route, 1)
            dve.wait_ge(route, 11)
            dve.tensor_copy(share_split[:, :, 0 * NE1:1 * NE1], share[:, :, :]).then_inc(route, 1)
            dve.wait_ge(route, 12)
            dve.tensor_tensor(share_rest[:, :, :], share[:, :, :], share_split[:, :, 0 * NE1:1 * NE1], ALU.subtract).then_inc(route, 1)
            dve.wait_ge(route, 13)
            dve.tensor_copy(share_split[:, :, 1 * NE1:2 * NE1], share_rest[:, :, :]).then_inc(route, 1)
            dve.wait_ge(route, 14)
            dve.tensor_tensor(share_split[:, :, 2 * NE1:3 * NE1], share_rest[:, :, :], share_split[:, :, 1 * NE1:2 * NE1], ALU.subtract).then_inc(route, 1)

            def experts(c, p, k):
                n = NE1 + 1
                for e in range(NE1):
                    u = n * c + e
                    dve.wait_ge(h_read[e % 2], n // 2 * c + e // 2 + 1)
                    if e == E:
                        dve.wait_ge(h_full, n * c + n)
                        if started(c):
                            dve.wait_ge(c_read, NE1 * c)
                        dve.tensor_tensor(shared[:, :], hidden[e % 3][:, :], ps_h[:, 1, :], ALU.mult).then_inc(h_read[1], 1)
                        dve.wait_ge(h_read[1], n // 2 * (c + 1))
                    dve.wait_ge(c_full, u + 1)
                    if e >= 3 or started(c):
                        dve.wait_ge(down, NE1 * c + e - 2)
                    of = shared if e == E else hidden[e % 3]
                    dve.tensor_tensor(weighed[e % 3][:, :], of[:, :], ps_c[:, e % 2, :], ALU.mult).then_inc(c_read, 1)
                dve.wait_ge(c_full, n * (c + 1))
                if started(c):
                    dve.wait_ge(stored, 16 * c)
                dve.tensor_tensor(out_sb[:, :, :], xr[:, ds(c * TC, TC), :],
                                  ps_c[:, 1, :].rearrange("p (i n) -> p i n", i=TC), ALU.add).then_inc(out_done, 1)
            chunks(dve, experts)

        @block.tensor
        def _(pe):
            pe.wait_ge(w3_in, 16 * N_W)
            pe.wait_ge(const_step, 4)

            def project(c, p, k):
                pe.wait_ge(a_in[p], 16 * (k + 1))
                if started(c):
                    pe.wait_ge(at_done, c)
                for i in range(TC):
                    last = pe.transpose(ps_t[:, i * P:(i + 1) * P], attn[p][:, i, :], ident_f[:, :])
                last.then_inc(at_ps, 1)
                pe.wait_ge(at_done, c + 1)
                if started(c):
                    pe.wait_ge(added, c)
                for i in range(TC):
                    last = pe.matmul(ps_y[:, i, :], attn_t[:, i * P:(i + 1) * P], wo[:, :], start=True, stop=True)
                last.then_inc(y_ps, 1)
            chunks(pe, project)

            def route_logits(c, p, k):
                pe.wait_ge(norms, c + 1)
                if started(c):
                    pe.wait_ge(nt_done, 2 * c)
                else:
                    pe.wait_ge(at_done, CHUNKS)
                for i in range(TC):
                    last = pe.transpose(ps_t[:, i * P:(i + 1) * P], normed[:, i, :], ident_f[:, :])
                last.then_inc(t_ps, 1)
                pe.wait_ge(nt_done, 2 * c + 1)
                if started(c):
                    pe.wait_ge(l_done, 2 * c)
                else:
                    pe.wait_ge(added, CHUNKS)
                for i in range(TC):
                    last = pe.matmul(ps_y[:, i, 0:NE1], nt_chunk[:, i * P:(i + 1) * P], w_rs[:, :], start=True, stop=True)
                last.then_inc(l_ps, 1)
            chunks(pe, route_logits)
            pe.wait_ge(route, 15)
            pe.wait_ge(nt_done, 2 * CHUNKS)
            for n in range(4):
                if n:
                    pe.wait_ge(ct_done, n)
                for i in range(2 * TC):
                    last = pe.transpose(ps_t[:, :].bitcast(BF16)[:, i * P:(i + 1) * P],
                                        share_split[:, n * 2 * TC + i, :], ident_b[:, :])
                last.then_inc(ct_ps, 1)
            pe.wait_ge(ct_done, 4)

            def experts(c, p, k):
                n = NE1 + 1
                x = nt[:, ds(c * CH, CH)]

                def up(u):
                    w = w1[:, u, :] if u < E else w_gu[:, (u - E) * F:(u - E + 1) * F]
                    if u >= 2 or started(c):
                        pe.wait_ge(h_read[u % 2], n // 2 * c + u // 2)
                    pe.matmul(ps_h[:, u % 2, :], w, x, start=True, stop=True).then_inc(h_full, 1)

                def shares(e):
                    if e >= 2:
                        pe.wait_ge(c_read, NE1 * c + e - 1)
                    elif started(c):
                        pe.wait_ge(*((c_read, NE1 * c) if e == 0 else (out_done, c)))
                    pe.matmul(ps_c[:, e % 2, :], spread[:, e, :], share_t[:, ds(c * CH, CH)], start=True, stop=True).then_inc(c_full, 1)

                def join(e):
                    if e == 0 and started(c):
                        pe.wait_ge(o_done, c)
                    pe.wait_ge(c_read, NE1 * c + e + 1)
                    w = w2[:, e, :] if e < E else w_sd[:, :]
                    pe.matmul(ps_out[:, :], w, weighed[e % 3][:, :], start=(e == 0), stop=(e == NE1 - 1)).then_inc(down, 1)
                for e in range(NE1):
                    up(e)
                    if e == E:
                        up(n - 1)
                    shares(e)
                    if e:
                        join(e - 1)
                join(NE1 - 1)
                pe.wait_ge(o_done, c + 1)
                for i in range(TC):
                    last = pe.transpose(ps_c[:, 1, i * P:(i + 1) * P], out_t[:, i * P:(i + 1) * P], ident_f[:, :])
                last.then_inc(c_full, 1)
            chunks(pe, experts)


def program(nc, dram, made):
    dram["x"] = dram["x"].rearrange("b t n -> (b t) n")
    dram["out"] = dram["out"].rearrange("b t n -> (b t) n")
    for name, shape, dt in (("q", (B, 3 * D, HC, H, CH), BF16), ("k", (B, 3 * D, H, NK), BF16), ("v", (B, T, DM), F32),
                            ("vc", (B, NB, DM), F32), ("gates", (B, P, NT, 3), F32), ("attn", (B, T, DM), F32)):
        dram[name] = nc.dram_tensor(f"made_{name}", shape, dt, kind=made).ap()
    with nc.sbuf_tensor("ident_f", [P, P], F32) as ident_f, nc.sbuf_tensor("ident_b", [P, P], BF16) as ident_b:
        project(nc, dram, ident_f, ident_b)
        attend(nc, dram, ident_b, ident_f)
        feed_forward(nc, dram, ident_f, ident_b)


_INS = {"L0_attn_x": "x", "L0_attn_Wq": "wq", "L0_attn_Wk": "wk", "L0_attn_Wv": "wv", "L0_attn_Wo": "wo",
        "L0_attn_Wck": "wck", "L0_attn_Wcv": "wcv", "L0_attn_Wg": "wg", "L0_attn_bg": "bg",
        "L0_ffn_router_w": "router_w", "L0_ffn_w1": "w1", "L0_ffn_w2": "w2", "L0_ffn_shared_gate_up": "sgu",
        "L0_ffn_shared_down": "sdown", "L0_ffn_shared_gate_w": "sgate_w"}


def kernel(**inputs):
    import numpy as np
    import concourse.bacc as bacc
    from concourse.bass_utils import run_bass_kernel_spmd

    nc = bacc.Bacc("TRN2", target_bir_lowering=False, num_devices=1)
    arrays, dram = {}, {}
    for name, short in _INS.items():
        a = np.ascontiguousarray(inputs[name])
        arrays[f"in_{short}"] = a
        dram[short] = nc.dram_tensor(f"in_{short}", a.shape, mybir.dt.from_np(a.dtype), kind="ExternalInput").ap()
    dram["out"] = nc.dram_tensor("out", (B, T, DM), F32, kind="ExternalOutput").ap()
    program(nc, dram, "Internal")
    return run_bass_kernel_spmd(nc, [arrays], core_ids=[0]).results[0]["out"]
```

```python
from contextlib import ExitStack

import numpy as np

import concourse.bass as bass
from concourse import mybir

F32 = mybir.dt.float32
BF16 = mybir.dt.bfloat16
ALU = mybir.AluOpType
ACT = mybir.ActivationFunctionType
AX = mybir.AxisListType

P = 128
B, T, DM = 4, 1024, 128
H, D = 16, 8
G, NB = 16, T // 16
TOP = 4
WIN = 32
TILES = B * T // P
NT = T // P
CH = 512
TC = CH // P
CHUNKS = B * T // CH
HC = T // CH
NK = T + NB
SCALE = float(D) ** -0.5
EPS = 1e-5
OUT_OF_REACH = -1e30
SENTINEL = -3e38
TAKEN = 3e38
HG = 4
GROUPS = B * H // HG
QUADS = H // HG
SP_Q = (0, 1, 2, 0, 1, 0)
SP_K = (0, 0, 0, 1, 1, 2)
R_SPLIT = 64
R_SHIFT = R_SPLIT + len(SP_Q) * D
ROWS = R_SHIFT + 3
E, F = 8, 128
PAIR_OF_ONES = float(np.array([0x3F803F80], np.uint32).view(np.float32)[0])
K2 = 2
ds = bass.ds

BAND = P + WIN
SEL = [(c, j) for c in range(HC) for j in range(TC * (c + 1))]
SECOND = [("compressed", 0, 0)] + [x for c in range(HC) for x in
                                   [("selected", c, j) for j in range(TC * (c + 1))]
                                   + [("local", c, j) for j in range(TC * c, TC * (c + 1))]]
END = len(SECOND) + 1
BACK_AT = [SECOND.index(("local", c, TC * (c + 1) - 1)) + 2 for c in range(HC)]


def width(c, j):
    return min(CH, (c + 1) * CH - j * P)


def band_width(j):
    return BAND if j < NT - 1 else P


def uses_of_b():
    sel, loc, back, u = [], [], [], 2
    for n in range(END + 1):
        kind = SECOND[n][0] if n < len(SECOND) else None
        if kind == "selected":
            sel.append(u)
            u += 2
        elif kind == "local":
            loc.append(u)
            u += 1
        if n in BACK_AT:
            back.append(u)
            u += 2
    return sel, loc, back, u


B_SEL, B_LOC, B_BACK, B_USES = uses_of_b()


def b_count(g, u):
    return B_USES // 2 * g + u // 2


def units_of_a():
    out, end = [], []
    for i in range(NT):
        keys = (i + 1) * P
        for w, k0, local in ((min(keys, CH), max(keys - CH, 0), True), (max(keys - CH, 0), 0, False)):
            if w:
                n = CH // w
                out += [(i, tuple(range(h, h + n)), k0, w, local) for h in range(0, HG, n)]
        if i % TC == TC - 1:
            end.append(len(out))
    return out, end


A_UNITS, A_END = units_of_a()
A_USES = len(A_UNITS)
SLOTS = 3


def pace():
    rest = []
    for n in range(END + 1):
        kind, c, j = SECOND[n] if n < len(SECOND) else (None, 0, 0)
        slot = {"selected": 6 * width(c, j) / CH, "local": 4, "compressed": 5, None: 1}[kind]
        rest += [slot, slot, slot + 5 * (n in BACK_AT)]
    work = [0.6 + 0.25 * len(heads) * local + EXTRA.get(u, 0) for u, (i, heads, k0, w, local) in enumerate(A_UNITS)]
    at, n, done, passed = [], 0, 0.0, 0.0
    for u in range(A_USES):
        while passed * sum(work) < done * sum(rest) and n < SLOTS * (END + 1) - 1:
            passed += rest[n]
            n += 1
        at.append(n)
        done += work[u]
    return at


M_WHAT = ([("logit", n) for n in range(4)] + [("bias", 0), ("bias", 1), ("shift", 0), ("prob", (0, 0)),
          ("prob", (0, 1)), ("prob", (1, 0)), ("prob", (1, 1)), ("shift", 1)])
M_USES = len(M_WHAT)
M_LOGIT = [M_WHAT.index(("logit", n)) for n in range(4)]
M_BIAS = [M_WHAT.index(("bias", n)) for n in range(2)]
M_PROB = [M_WHAT.index(("prob", (n, 1))) for n in range(2)]
M_SHIFT = [M_WHAT.index(("shift", n)) for n in range(2)]
FIRST_AT = {2: (0,), 3: (1,), 4: (2,), 5: (3,), 12: (4,), 14: (5,), 16: (6,), 17: (7,), 18: (8,), 19: (9,), 20: (10,)}
LATE_SHIFT_AT = 2
EXP_AT = (15, 17)
LATE_SHIFT_AFTER = 1
MAX_AFTER = [6 + i for i in range(NT)]
MARK_AFTER = [8 + i for i in range(NT)]
BIAS_AFTER = [13, 17]
SHIFT_AFTER = 24
EXTRA = {LATE_SHIFT_AFTER: 1.6, SHIFT_AFTER: 1.6, BIAS_AFTER[0]: 0.6, BIAS_AFTER[1]: 0.6}
for after_unit in MAX_AFTER + MARK_AFTER:
    EXTRA[after_unit] = EXTRA.get(after_unit, 0) + 0.45
A_AT = pace()
N_CONST = (18, 11)


def is_first(group):
    return isinstance(group[0], int) and group[0] == 0


def is_last(group):
    return isinstance(group[0], int) and group[0] == GROUPS - 1


def before(group):
    g, p, k = group
    return g - 1, 1 - p, k - 1 + p


def after(group):
    g, p, k = group
    return g + 1, 1 - p, k + p


def project(nc, dram, ident_f, ident_b):
    with ExitStack() as ctx:
        def sb(name, shape, dt=F32):
            return ctx.enter_context(nc.sbuf_tensor(name, shape, dt))

        def ps(name, shape, dt=F32):
            return ctx.enter_context(nc.psum_tensor(name, shape, dt))

        def sem(name):
            return ctx.enter_context(nc.semaphore(name))

        xs = sb("xs", [P, TILES, DM])
        wq = sb("wq", [P, DM])
        wk = sb("wk", [P, DM])
        wv = sb("wv", [P, DM])
        wqt = sb("wqt", [P, DM])
        wvg = sb("wvg", [P, DM + 3])
        wg_rep = sb("wg_rep", [P, 3])
        bg_rep = sb("bg_rep", [P, 3])
        wc_rep = sb("wc_rep", [P, 2, G, D])
        wc_diag = sb("wc_diag", [P, 2, G, H, D])
        head_of_row = sb("head_of_row", [P, H])
        late = sb("late", [P, 1])
        eps = sb("eps", [P, 1])
        total = sb("total", [P, TC])
        mean = sb("mean", [P, TC])
        centred = sb("centred", [P, TC, DM])
        squares = sb("squares", [P, TC, DM])
        sqsum = sb("sqsum", [P, TC])
        sdev = sb("sdev", [P, TC])
        rstd = sb("rstd", [P, TC])
        normed = sb("normed", [P, TC, DM])
        normed_t = sb("normed_t", [P, CH])
        kt = sb("kt", [P, B * T])
        vt = sb("vt", [P, B * T])
        q_split = sb("q_split", [P, 3, CH], BF16)
        k_split = sb("k_split", [P, 3, CH], BF16)
        q_rest = sb("q_rest", [P, CH])
        k_rest = sb("k_rest", [P, CH])
        v_out = sb("v_out", [P, TC, DM])
        gates = sb("gates", [P, TILES, 3])
        gate_max = sb("gate_max", [P, TILES])
        gate_sum = sb("gate_sum", [P, TILES])
        gate_inv = sb("gate_inv", [P, TILES])
        kc_split = sb("kc_split", [P, 3, B * NB], BF16)
        kc_rest = sb("kc_rest", [P, B * NB])
        vct = sb("vct", [P, B * NB])
        vc_out = sb("vc_out", [NB, B, DM])

        ps_t = ps("ps_t", [P, CH])
        ps_q = ps("ps_q", [P, CH])
        ps_k = ps("ps_k", [P, CH])
        ps_vt = ps("ps_vt", [P, CH])
        ps_v = ps("ps_v", [P, TC, 256])
        ps_w = ps("ps_w", [P, CH])

        x_in, w_in, w_made, diag_made, wqt_ready = map(sem, ("x_in", "w_in", "w_made", "diag_made", "wqt_ready"))
        wt_ps, wqt_done, wg_ps, wvg_done = map(sem, ("wt_ps", "wqt_done", "wg_ps", "wvg_done"))
        consts, const_step, sums, means, centre = map(sem, ("consts", "const_step", "sums", "means", "centre"))
        squared, sqsums, sdevs, rstds, norms = map(sem, ("squared", "sqsums", "sdevs", "rstds", "norms"))
        t_ps, nt_done, q_ps, k_ps, vt_ps, v_ps = map(sem, ("t_ps", "nt_done", "q_ps", "k_ps", "vt_ps", "v_ps"))
        q0_done, k0_done, vt_done, v_done = map(sem, ("q0_done", "k0_done", "vt_done", "v_done"))
        qr_done, q1_done, q2_done, kr_done, k1_done, k2_done = map(
            sem, ("qr_done", "q1_done", "q2_done", "kr_done", "k1_done", "k2_done"))
        q_out, k_out, v_stored = map(sem, ("q_out", "k_out", "v_stored"))
        kc_ps, vc_ps, kc_step, vct_done, vc_tr, vc_done = map(
            sem, ("kc_ps", "vc_ps", "kc_step", "vct_done", "vc_tr", "vc_done"))
        gate_step, gate_exp, end_out = map(sem, ("gate_step", "gate_exp", "end_out"))
        ctx.enter_context(nc.allow_non_contiguous_dma(reason="rows of a few elements"))
        block = ctx.enter_context(nc.Block())
        N_W = 3 + H + 1 + 2 * H

        def chunks(engine, chunk):
            chunk(0)
            with engine.Fori(1, CHUNKS) as c:
                chunk(c)

        def started(c):
            return not (isinstance(c, int) and c == 0)

        @block.sync
        def _(sp):
            for c in range(CHUNKS):
                sp.dma_start(xs[:, c * TC:(c + 1) * TC, :],
                             dram["x"][c * CH:(c + 1) * CH, :].rearrange("(i p) n -> p i n", p=P)).then_inc(x_in, 16)
            with sp.Fori(0, B) as b:
                for half in range(HC):
                    c = b * HC + half
                    for name, split, last, out in (("q", q_split, q2_done, q_out), ("k", k_split, k2_done, k_out)):
                        sp.wait_ge(last, c + 1)
                        for s in range(3):
                            at = dram[name][ds(b, 1), s * D:(s + 1) * D]
                            if name == "q":
                                at = at[:, :, half, :, :].rearrange("a r h t -> h (a r) t")
                            else:
                                at = at[:, :, :, half * CH:(half + 1) * CH].rearrange("a r h t -> h (a r) t")
                            sp.dma_start(at, split[:, s, :]).then_inc(out, 16)
                    sp.wait_ge(v_done, 2 * c + 2)
                    sp.dma_start(dram["v"][ds(b, 1), half * CH:(half + 1) * CH, :]
                                 .rearrange("a (i p) r -> p (a i) r", p=P), v_out[:, :, :]).then_inc(v_stored, 16)
            sp.wait_ge(kc_step, 6)
            for b in range(B):
                for s in range(3):
                    sp.dma_start(dram["k"][b, s * D:(s + 1) * D, :, T:NK].rearrange("r h n -> h r n"),
                                 kc_split[:, s, b * NB:(b + 1) * NB]).then_inc(end_out, 16)
            sp.wait_ge(vc_done, 1)
            sp.dma_start(dram["vc"].rearrange("b n r -> n b r"), vc_out[:, :, :]).then_inc(end_out, 16)
            sp.wait_ge(gate_step, 7)
            for b in range(B):
                sp.dma_start(dram["gates"][b], gates[:, b * NT:(b + 1) * NT, :]).then_inc(end_out, 16)
            sp.wait_ge(q_out, 3 * 16 * CHUNKS)
            sp.wait_ge(k_out, 3 * 16 * CHUNKS)
            sp.wait_ge(v_stored, 16 * CHUNKS)
            sp.wait_ge(end_out, 16 * (4 * B + 1))

        @block.gpsimd
        def _(pool):
            pool.memset(ident_f[:, :], 0.0).then_inc(const_step, 1)
            pool.memset(ident_b[:, :], 0.0).then_inc(const_step, 1)
            pool.memset(head_of_row[:, :], 1.0).then_inc(const_step, 1)
            pool.memset(late[:, :], 1.0).then_inc(const_step, 1)
            pool.memset(eps[:, :], EPS).then_inc(consts, 1)
            pool.wait_ge(const_step, 4)
            for m in (ident_f, ident_b):
                pool.affine_select(out=m[:, :], in_=m[:, :], compare_op=ALU.not_equal, fill=1.0, base=0,
                                   pattern=[[-1, P]], channel_multiplier=1).then_inc(consts, 1)
            pool.affine_select(out=late[:, :], in_=late[:, :], compare_op=ALU.is_ge, fill=0.0, base=-G,
                               pattern=[[0, 1]], channel_multiplier=1).then_inc(consts, 1)
            pool.affine_select(out=head_of_row[:, :], in_=head_of_row[:, :], compare_op=ALU.is_ge, fill=0.0,
                               base=0, pattern=[[-D, H]], channel_multiplier=1).then_inc(const_step, 1)
            pool.wait_ge(const_step, 5)
            pool.affine_select(out=head_of_row[:, :], in_=head_of_row[:, :], compare_op=ALU.is_ge, fill=0.0,
                               base=D - 1, pattern=[[D, H]], channel_multiplier=-1).then_inc(consts, 1)
            pool.wait_ge(consts, 5)
            pool.wait_ge(w_in, 16 * N_W)
            for i in range(2):
                for g in range(G):
                    last = pool.tensor_tensor(
                        wc_diag[:, i, g, :, :], wc_rep[:, i, g, :].unsqueeze(1).broadcast_to([P, H, D]),
                        head_of_row[:, :].unsqueeze(2).broadcast_to([P, H, D]), ALU.mult)
                    last.then_inc(diag_made, 1)

        @block.scalar
        def _(act):
            for w, name in ((wq, "wq"), (wk, "wk"), (wv, "wv")):
                act.dma_start(w[:, :], dram[name]).then_inc(w_in, 16)
            act.dma_start(bg_rep[:, :], dram["bg"].partition_broadcast(P)).then_inc(w_in, 16)
            for h in range(H):
                rows = slice(h * D, (h + 1) * D)
                act.dma_start(wg_rep[rows, :], dram["wg"]).then_inc(w_in, 16)
                for i, name in enumerate(("wck", "wcv")):
                    act.dma_start(wc_rep[rows, i, :, :], dram[name].rearrange("(g d) e -> d g e", d=D)).then_inc(w_in, 16)
            act.wait_ge(consts, 1)
            def chunk(c):
                act.wait_ge(centre, c + 1)
                act.activation(squares[:, :, :], centred[:, :, :], ACT.Square).then_inc(squared, 1)
                act.wait_ge(sqsums, c + 1)
                act.activation(sdev[:, :], sqsum[:, :], ACT.Sqrt, bias=eps[:, 0:1], scale=1.0 / DM).then_inc(sdevs, 1)
                act.wait_ge(t_ps, c + 1)
                act.activation(normed_t[:, :], ps_t[:, :], ACT.Copy).then_inc(nt_done, 1)
                act.wait_ge(q_ps, c + 1)
                if started(c):
                    act.wait_ge(q_out, c * 48)
                act.activation(q_split[:, 0, :], ps_q[:, :], ACT.Copy, scale=SCALE).then_inc(q0_done, 1)
                act.wait_ge(k_ps, c + 1)
                if started(c):
                    act.wait_ge(k_out, c * 48)
                act.activation(k_split[:, 0, :], ps_k[:, :], ACT.Copy).then_inc(k0_done, 1)
                act.activation(kt[:, ds(c * CH, CH)], ps_k[:, :], ACT.Copy).then_inc(k0_done, 1)
                act.wait_ge(vt_ps, c + 1)
                act.activation(vt[:, ds(c * CH, CH)], ps_vt[:, :], ACT.Copy).then_inc(vt_done, 1)
                act.wait_ge(v_ps, c + 1)
                if started(c):
                    act.wait_ge(v_stored, c * 16)
                act.activation(v_out[:, :, :], ps_v[:, :, 0:DM], ACT.Copy).then_inc(v_done, 1)
                act.activation(gates[:, ds(c * TC, TC), :], ps_v[:, :, DM:DM + 3], ACT.Copy).then_inc(v_done, 1)
            chunks(act, chunk)
            act.wait_ge(vc_ps, 1)
            act.activation(vct[:, :], ps_vt[:, 0:B * NB], ACT.Copy).then_inc(vct_done, 1)
            act.wait_ge(gate_step, 3)
            act.activation(gates[:, :, :], gates[:, :, :], ACT.Exp).then_inc(gate_exp, 1)
            act.wait_ge(vc_tr, 1)
            act.activation(vc_out[:, :, :], ps_t[0:NB, :].rearrange("n (b r) -> n b r", b=B), ACT.Copy).then_inc(vc_done, 1)

        @block.vector
        def _(dve):
            dve.wait_ge(wt_ps, 1)
            dve.tensor_copy(wqt[:, :], ps_w[:, 0:DM]).then_inc(wqt_done, 1)
            dve.wait_ge(w_in, 16 * N_W)
            dve.tensor_copy(wvg[:, 0:DM], wv[:, :]).then_inc(wvg_done, 1)
            dve.wait_ge(wg_ps, 1)
            dve.tensor_scalar(wvg[:, DM:DM + 3], ps_w[:, DM:DM + 3], 1.0 / H, None, ALU.mult).then_inc(wvg_done, 1)
            def chunk(c):
                dve.wait_ge(x_in, 16 * CHUNKS)
                x = xs[:, ds(c * TC, TC), :]
                dve.tensor_reduce(total[:, :], x, AX.X, ALU.add).then_inc(sums, 1)
                dve.wait_ge(sums, c + 1)
                dve.tensor_scalar(mean[:, :], total[:, :], 1.0 / DM, None, ALU.mult).then_inc(means, 1)
                dve.wait_ge(means, c + 1)
                dve.tensor_tensor(centred[:, :, :], x, mean[:, :].unsqueeze(2).broadcast_to([P, TC, DM]),
                                  ALU.subtract).then_inc(centre, 1)
                dve.wait_ge(squared, c + 1)
                dve.tensor_reduce(sqsum[:, :], squares[:, :, :], AX.X, ALU.add).then_inc(sqsums, 1)
                dve.wait_ge(sdevs, c + 1)
                dve.reciprocal(rstd[:, :], sdev[:, :]).then_inc(rstds, 1)
                dve.wait_ge(rstds, c + 1)
                dve.wait_ge(centre, c + 1)
                dve.tensor_tensor(normed[:, :, :], centred[:, :, :],
                                  rstd[:, :].unsqueeze(2).broadcast_to([P, TC, DM]), ALU.mult).then_inc(norms, 1)
                dve.wait_ge(q0_done, c + 1)
                dve.scalar_tensor_tensor(q_rest[:, :], ps_q[:, :], SCALE, q_split[:, 0, :],
                                         ALU.mult, ALU.subtract).then_inc(qr_done, 1)
                dve.wait_ge(k0_done, 2 * c + 2)
                dve.tensor_tensor(k_rest[:, :], kt[:, ds(c * CH, CH)], k_split[:, 0, :], ALU.subtract).then_inc(kr_done, 1)
                dve.wait_ge(qr_done, c + 1)
                dve.tensor_copy(q_split[:, 1, :], q_rest[:, :]).then_inc(q1_done, 1)
                dve.wait_ge(kr_done, c + 1)
                dve.tensor_copy(k_split[:, 1, :], k_rest[:, :]).then_inc(k1_done, 1)
                dve.wait_ge(q1_done, c + 1)
                dve.tensor_tensor(q_split[:, 2, :], q_rest[:, :], q_split[:, 1, :], ALU.subtract).then_inc(q2_done, 1)
                dve.wait_ge(k1_done, c + 1)
                dve.tensor_tensor(k_split[:, 2, :], k_rest[:, :], k_split[:, 1, :], ALU.subtract).then_inc(k2_done, 1)
            chunks(dve, chunk)
            dve.wait_ge(v_done, 2 * CHUNKS)
            dve.tensor_tensor(gates[:, :, :], gates[:, :, :], bg_rep[:, :].unsqueeze(1).broadcast_to([P, TILES, 3]),
                              ALU.add).then_inc(gate_step, 1)
            dve.wait_ge(gate_step, 1)
            dve.tensor_reduce(gate_max[:, :], gates[:, :, :], AX.X, ALU.max).then_inc(gate_step, 1)
            dve.wait_ge(gate_step, 2)
            dve.tensor_tensor(gates[:, :, :], gates[:, :, :], gate_max[:, :].unsqueeze(2).broadcast_to([P, TILES, 3]),
                              ALU.subtract).then_inc(gate_step, 1)
            dve.wait_ge(gate_exp, 1)
            dve.tensor_reduce(gate_sum[:, :], gates[:, :, :], AX.X, ALU.add).then_inc(gate_step, 1)
            dve.wait_ge(gate_step, 4)
            dve.reciprocal(gate_inv[:, :], gate_sum[:, :]).then_inc(gate_step, 1)
            dve.wait_ge(gate_step, 5)
            dve.tensor_tensor(gates[:, :, :], gates[:, :, :], gate_inv[:, :].unsqueeze(2).broadcast_to([P, TILES, 3]),
                              ALU.mult).then_inc(gate_step, 1)
            dve.wait_ge(gate_step, 6)
            dve.wait_ge(consts, 5)
            first = gates[:, :, :].rearrange("p (b i) k -> p b (i k)", b=B)[:, :, 0:1]
            dve.tensor_tensor(first, first, late[:, 0:1].unsqueeze(1).broadcast_to([P, B, 1]), ALU.mult).then_inc(gate_step, 1)
            dve.wait_ge(kc_ps, 1)
            dve.tensor_copy(kc_split[:, 0, :], ps_k[:, 0:B * NB]).then_inc(kc_step, 1)
            dve.wait_ge(kc_step, 1)
            dve.tensor_tensor(kc_rest[:, :], ps_k[:, 0:B * NB], kc_split[:, 0, :], ALU.subtract).then_inc(kc_step, 1)
            dve.wait_ge(kc_step, 2)
            dve.tensor_copy(kc_split[:, 1, :], kc_rest[:, :]).then_inc(kc_step, 1)
            dve.wait_ge(kc_step, 3)
            dve.tensor_tensor(kc_split[:, 2, :], kc_rest[:, :], kc_split[:, 1, :], ALU.subtract).then_inc(kc_step, 3)

        @block.tensor
        def _(pe):
            pe.wait_ge(w_in, 16 * N_W)
            pe.wait_ge(consts, 5)
            pe.transpose(ps_w[:, 0:DM], wq[:, :], ident_f[:, :]).then_inc(wt_ps, 1)
            pe.wait_ge(wqt_done, 1)
            pe.matmul(ps_w[:, DM:DM + 3], wqt[:, :], wg_rep[:, :], start=True, stop=True).then_inc(wg_ps, 1)
            pe.wait_ge(wvg_done, 2)
            def chunk(c):
                pe.wait_ge(norms, c + 1)
                if started(c):
                    pe.wait_ge(nt_done, c)
                for i in range(TC):
                    last = pe.transpose(ps_t[:, i * P:(i + 1) * P], normed[:, i, :], ident_f[:, :])
                last.then_inc(t_ps, 1)
                pe.wait_ge(nt_done, c + 1)
                if started(c):
                    pe.wait_ge(q2_done, c)
                pe.matmul(ps_q[:, :], wq[:, :], normed_t[:, :], start=True, stop=True).then_inc(q_ps, 1)
                if started(c):
                    pe.wait_ge(k0_done, 2 * c)
                pe.matmul(ps_k[:, :], wk[:, :], normed_t[:, :], start=True, stop=True).then_inc(k_ps, 1)
                if started(c):
                    pe.wait_ge(vt_done, c)
                pe.matmul(ps_vt[:, :], wv[:, :], normed_t[:, :], start=True, stop=True).then_inc(vt_ps, 1)
                if started(c):
                    pe.wait_ge(v_done, 2 * c)
                for i in range(TC):
                    last = pe.matmul(ps_v[:, i, 0:DM + 3], normed_t[:, i * P:(i + 1) * P], wvg[:, :], start=True, stop=True)
                last.then_inc(v_ps, 1)
            chunks(pe, chunk)
            pe.wait_ge(diag_made, 2 * G)
            pe.wait_ge(k0_done, 2 * CHUNKS)
            pe.wait_ge(vt_done, CHUNKS)
            for i, (src, dst, made) in enumerate(((kt, ps_k, kc_ps), (vt, ps_vt, vc_ps))):
                of_offset = src[:, :].rearrange("p (n g) -> p g n", g=G)
                for g in range(G):
                    last = pe.matmul(dst[:, 0:B * NB], wc_diag[:, i, g, :, :].rearrange("p h d -> p (h d)"),
                                     of_offset[:, g, :], start=(g == 0), stop=(g == G - 1))
                last.then_inc(made, 1)
            pe.wait_ge(vct_done, 1)
            for b in range(B):
                last = pe.transpose(ps_t[0:NB, b * P:(b + 1) * P], vct[:, b * NB:(b + 1) * NB], ident_f[:, :])
            last.then_inc(vc_tr, 1)


def attend(nc, dram, ident_b, ident_f):
    with ExitStack() as ctx:
        def sb(name, shape, dt=F32):
            return ctx.enter_context(nc.sbuf_tensor(name, shape, dt))

        def ps(name, shape, dt=F32):
            return ctx.enter_context(nc.psum_tensor(name, shape, dt))

        def sem(name):
            return ctx.enter_context(nc.semaphore(name))

        cmask = sb("cmask", [P, NT, NB], BF16)
        causal_q = sb("causal_q", [P, TOP * G], BF16)
        causal_k = sb("causal_k", [P, TOP * G], BF16)
        band_q = sb("band_q", [P, BAND], BF16)
        band_k = sb("band_k", [P, BAND], BF16)
        q_loc = [sb(f"q_loc{p}", [ROWS, HC, HG, CH], BF16) for p in range(2)]
        q_sel = [sb(f"q_sel{p}", [ROWS, HC, HG, CH], BF16) for p in range(2)]
        keys = [sb(f"keys{p}", [ROWS, HG, NK], BF16) for p in range(2)]
        q_first = [sb(f"q_first{p}", [R_SHIFT, HC, HG, CH], BF16) for p in range(2)]
        k_first = [sb(f"k_first{p}", [R_SHIFT, HG, NK], BF16) for p in range(2)]
        v_in = [sb(f"v_in{p}", [P, NT, HG * D]) for p in range(2)]
        v_pad = [sb(f"v_pad{p}", [P, NT, HG, 32]) for p in range(2)]
        vc_pad = [sb(f"vc_pad{p}", [P, 2, 64]) for p in range(2)]
        gate = [sb(f"gate{p}", [P, NT, 3]) for p in range(2)]
        logit = sb("logit", [P, NT, HG, TOP + NB])
        best = sb("best", [P, NT, HG, 8])
        marked = sb("marked", [P, NT, HG, TOP + NB])
        bias = sb("bias", [P, NT, HG, NB], BF16)
        block_max = sb("block_max", [P, NT, HG, NB])
        sel_max = sb("sel_max", [P, TC, HG, NB])
        prob_c = (marked[:, :, :, :].rearrange("p i h n -> p (i h n)")[:, 0:NT * HG * NB]
                  .rearrange("p (i h n) -> p i h n", i=NT, h=HG))
        prob_ct = sb("prob_ct", [P, 2, T])
        peak = sb("peak", [P, 2, 2, TC * HG])
        peak_rest = sb("peak_rest", [P, 2, TC * HG])
        shift = sb("shift", [P, 2, 3, TC * HG], BF16)
        bias_t = [sb(f"bias_t{n}", [P, 2, CH], BF16) for n in range(2)]
        shift_t = [sb(f"shift_t{n}", [6 * TC * HG, P], BF16) for n in range(2)]
        banded = sb("banded", [P, 2, HG, BAND], BF16)
        pad = sb("pad", [P, TC + NT])
        turn = sb("turn", [P, 4])
        prob_s = [sb(f"prob_s{n}", [P, HG, CH]) for n in range(2)]
        prob_l = [sb(f"prob_l{n}", [P, HG, BAND]) for n in range(4)]
        mixed_t = sb("mixed_t", [P, 4, CH])
        weight = sb("weight", [P, 3, TC, HG])
        gated = sb("gated", [P, 3, TC, HG])
        part = sb("part", [P, 3, TC, HG, D])
        part2 = sb("part2", [P, TC, HG, D])
        mixed = sb("mixed", [P, NT, HG * D])

        ps_a = ps("ps_a", [P, 2, CH])
        ps_b = ps("ps_b", [P, 2, 2, CH])
        ps_o = ps("ps_o", [P, CH])
        ps_m = ps("ps_m", [P, CH])
        ps_mb = ps_m[:, :].bitcast(BF16)

        loaded_first = [sem(f"loaded_first{p}") for p in range(2)]
        loaded = [sem(f"loaded{p}") for p in range(2)]
        bias_in = [[sem(f"bias_in{p}{n}") for n in range(2)] for p in range(2)]
        shift_in = [[sem(f"shift_in{p}{n}") for n in range(2)] for p in range(2)]
        consts = [sem(f"s_consts{p}") for p in range(2)]
        const_step, key_blocks, v_ready, zeros = map(sem, ("s_const_step", "key_blocks", "v_ready", "zeros"))
        m_full, m_free, a_full, a_read = map(sem, ("m_full", "m_free", "a_full", "a_read"))
        maxed, ranked, picked, bias_done = map(sem, ("maxed", "ranked", "picked", "bias_done"))
        centred_c, exp_c, bm_done, sel_done, shift_step = map(
            sem, ("centred_c", "exp_c", "bm_done", "sel_done", "shift_step"))
        b_full = sem("b_full")
        b_read = [sem(f"b_read{n}") for n in range(2)]
        pv_sel, pv_loc = map(sem, ("pv_sel", "pv_loc"))
        o_free, recip, gated_done, summed, mixed_done = map(
            sem, ("o_free", "recip", "gated_done", "summed", "mixed_done"))
        mixed_out = [sem(f"mixed_out{p}") for p in range(2)]
        ctx.enter_context(nc.allow_non_contiguous_dma(reason="rows of heads"))
        block = ctx.enter_context(nc.Block())

        def steps(engine, step):
            step(None, (0, 0, 0))
            step((0, 0, 0), (1, 1, 0))
            step((1, 1, 0), (2, 0, 1))
            last = GROUPS // 2 - 1
            with engine.Fori(1, last - 1) as k:
                step((2 * k, 0, k), (2 * k + 1, 1, k))
                step((2 * k + 1, 1, k), (2 * k + 2, 0, k + 1))
            step((GROUPS - 4, 0, last - 1), (GROUPS - 3, 1, last - 1))
            step((GROUPS - 3, 1, last - 1), (GROUPS - 2, 0, last))
            step((GROUPS - 2, 0, last), (GROUPS - 1, 1, last))
            step((GROUPS - 1, 1, last), None)

        N_LOAD1 = 2 * 3
        N_LOAD2 = 3 * 3 + 1 + HG + 1

        def load_splits(sp, to, name, group, sem):
            g = group[0]
            b, h0 = ds(g // QUADS, 1), ds(g % QUADS * HG, HG)
            at = R_SPLIT
            for n in (3, 2, 1):
                if name == "q":
                    src = dram["q"][b, 0:n * D, :, h0, :].rearrange("a r c h t -> (a r) c (h t)")
                    dst = to[at:at + n * D, :, :, :].rearrange("r c h t -> r c (h t)")
                    sp.dma_start(dst, src).then_inc(sem, 16)
                else:
                    s = 3 - n
                    src = (dram["k"][b, s * D:(s + 1) * D, h0, :].rearrange("a r h t -> a r (h t)")
                           .broadcast_to([n, D, HG * NK]))
                    sp.dma_start(to[at:at + n * D, :, :].rearrange("r h t -> r (h t)"), src).then_inc(sem, 16)
                at += n * D

        @block.sync
        def _(sp):
            def load_first(group):
                g, p, k = group
                if not (isinstance(g, int) and g < 2):
                    sp.wait_ge(a_full, A_USES * (g - 1))
                load_splits(sp, q_first[p], "q", group, loaded_first[p])
                load_splits(sp, k_first[p], "k", group, loaded_first[p])

            def load_second(group):
                g, p, k = group
                if not (isinstance(g, int) and g < 2):
                    sp.wait_ge(b_full, B_USES * (g - 1))
                load_splits(sp, keys[p], "k", group, loaded[p])
                load_splits(sp, q_sel[p], "q", group, loaded[p])
                load_splits(sp, q_loc[p], "q", group, loaded[p])
                rows = ds(g % QUADS * (HG * D), HG * D)
                sp.dma_start(v_in[p][:, :, :], dram["v"][ds(g // QUADS, 1), :, rows]
                             .rearrange("a (i p) r -> p (a i) r", p=P)).then_inc(loaded[p], 16)
                sp.dma_start(gate[p][:, :, :], dram["gates"][ds(g // QUADS, 1), :, :, :]
                             .rearrange("a p i k -> p (a i) k")).then_inc(loaded[p], 16)
                for h in range(HG):
                    r0, c0 = h % 2 * NB, h % 2 * 32
                    sp.dma_start(vc_pad[p][r0:r0 + NB, h // 2, c0:c0 + D],
                                 dram["vc"][ds(g // QUADS, 1), :, ds(g % QUADS * (HG * D) + h * D, D)]
                                 .rearrange("a n r -> n (a r)")).then_inc(loaded[p], 16)

            def place(group, n):
                g, p, k = group
                sp.wait_ge(m_free, M_USES * g + M_BIAS[n] + 1)
                for odd in range(2):
                    sp.dma_start(q_sel[p][0:NB, n, odd::2, :],
                                 bias_t[n][odd * NB:(odd + 1) * NB, :, :]).then_inc(bias_in[p][n], 16)

            def place_shift(group, n):
                g, p, k = group
                sp.wait_ge(m_free, M_USES * g + M_SHIFT[n] + 1)
                w = TC * HG
                for kind, q in enumerate((q_sel, q_loc)):
                    for s in range(3):
                        r0 = (3 * kind + s) * w
                        sp.dma_start(q[p][R_SHIFT + s:R_SHIFT + s + 1, n, :, :].rearrange("s h (i q) -> s (h i) q", q=P),
                                     shift_t[n][r0:r0 + w, :]).then_inc(shift_in[p][n], 16)

            def store(group, c):
                g, p, k = group
                sp.wait_ge(mixed_done, 2 * g + c + 1)
                b, quad = g // QUADS, g % QUADS
                sp.dma_start(dram["attn"][ds(b, 1), c * CH:(c + 1) * CH, ds(quad * HG * D, HG * D)]
                             .rearrange("a (i p) r -> p (a i) r", p=P), mixed[:, c * TC:(c + 1) * TC, :]).then_inc(mixed_out[c], 16)

            def step(second, first):
                if first and is_first(first):
                    sp.wait_ge(consts[0], N_CONST[0])
                    load_first(first)
                    sp.wait_ge(consts[1], N_CONST[1])
                    load_first(after(first))
                if second:
                    place_shift(second, 1)
                    if not is_first(second):
                        store(before(second), 1)
                if first:
                    load_second(first)
                    place(first, 0)
                if second:
                    store(second, 0)
                if first:
                    place(first, 1)
                    place_shift(first, 0)
                    if not (isinstance(first[0], int) and first[0] >= GROUPS - 2):
                        load_first(after(after(first)))
                elif second:
                    store(second, 1)
            steps(sp, step)
            for n in range(2):
                sp.wait_ge(mixed_out[n], 16 * GROUPS)

        @block.gpsimd
        def _(pool):
            for m in (cmask, causal_q, causal_k, band_q, band_k):
                pool.memset(m[...], 0.0).then_inc(const_step, 1)
            pool.memset(logit[:, :, :, 0:TOP], SENTINEL).then_inc(consts[0], 1)
            pool.memset(keys[0][0:R_SPLIT, 0, 0:T], 1.0).then_inc(const_step, 1)
            pool.memset(turn[:, 0:1], 0.0).then_inc(const_step, 1)
            pool.wait_ge(const_step, 7)

            def reach(m, base, pattern, multiplier, done):
                pool.affine_select(out=m, in_=m, compare_op=ALU.is_ge, fill=OUT_OF_REACH, base=base,
                                   pattern=pattern, channel_multiplier=multiplier).then_inc(done, 1)
            reach(cmask[:, :, :], -G, [[P, NT], [-G, NB]], 1, consts[0])
            reach(causal_q[:, :], 0, [[-1, TOP * G]], 1, consts[0])
            reach(causal_k[:, :], 0, [[1, TOP * G]], -1, consts[0])
            reach(band_q[:, :], 0, [[1, BAND]], -1, const_step)
            reach(band_k[:, :], 0, [[1, BAND]], -1, const_step)
            pool.affine_select(out=keys[0][0:NB, 0, 0:T], in_=keys[0][0:NB, 0, 0:T], compare_op=ALU.is_ge, fill=0.0,
                               base=0, pattern=[[1, T]], channel_multiplier=-G).then_inc(const_step, 1)
            pool.wait_ge(const_step, 10)
            reach(band_q[:, :], WIN, [[-1, BAND]], 1, consts[0])
            reach(band_k[:, :], WIN, [[-1, BAND]], 1, consts[0])
            pool.affine_select(out=keys[0][0:NB, 0, 0:T], in_=keys[0][0:NB, 0, 0:T], compare_op=ALU.is_ge, fill=0.0,
                               base=G - 1, pattern=[[-1, T]], channel_multiplier=G).then_inc(key_blocks, 1)

            pool.memset(v_pad[1][:, :, :, :], 0.0).then_inc(const_step, 1)
            for m in (q_first[1][0:R_SPLIT, :, :, :], k_first[1][0:R_SPLIT, :, :], q_loc[1][0:R_SPLIT, :, :, :]):
                pool.memset(m, 0.0).then_inc(consts[1], 1)
            pool.wait_ge(const_step, 11)
            pool.memset(v_pad[1][:, :, :, D:D + 1], 1.0).then_inc(consts[1], 1)

            def widen(group):
                g, p, k = group
                pool.wait_ge(loaded[p], 16 * N_LOAD2 * (k + 1))
                if not (isinstance(g, int) and g < 2):
                    pool.wait_ge(b_full, B_USES * (g - 1))
                pool.tensor_tensor(turn[:, 1:2], turn[:, 0:1], turn[:, 0:1], ALU.add)
                pool.tensor_copy(v_pad[p][:, :, :, 0:D], v_in[p][:, :, :].rearrange("p i (h d) -> p i h d", d=D)).then_inc(v_ready, 1)

            def centre(group, n):
                g, p, k = group
                at = slice(n * TC, (n + 1) * TC)
                pool.wait_ge(bias_done, 2 * g + n + 1)
                pool.tensor_tensor(prob_c[:, at, :, :], logit[:, at, :, TOP:], best[:, at, :, 0:1].broadcast_to([P, TC, HG, NB]),
                                   ALU.subtract).then_inc(centred_c, 1)

            def masked_max(group, n):
                g, p, k = group
                at = slice(n * TC, (n + 1) * TC)
                pool.wait_ge(a_read, A_USES * g + A_END[n])
                pool.wait_ge(bias_done, 2 * g + n + 1)
                if n or not is_first(group):
                    pool.wait_ge(sel_done, 2 * g + n)
                pool.tensor_tensor(sel_max[:, :, :, :], block_max[:, at, :, :], bias[:, at, :, :], ALU.add).then_inc(bm_done, 1)

            def total(group, c):
                g, p, k = group
                for n in range(2):
                    pool.wait_ge(b_read[n], b_count(g, B_BACK[c] + n) + 1)
                pool.tensor_tensor(part2[:, :, :, :], part[:, 0, :, :, :], part[:, 1, :, :, :], ALU.add).then_inc(summed, 1)
                pool.wait_ge(summed, 2 * g + c + 1)
                if not is_first(group):
                    pool.wait_ge(mixed_out[c], 16 * g)
                pool.tensor_tensor(mixed[:, c * TC:(c + 1) * TC, :].rearrange("p i (h d) -> p i h d", d=D),
                                   part2[:, :, :, :], part[:, 2, :, :, :], ALU.add).then_inc(mixed_done, 1)

            def step(second, first):
                if second:
                    total(second, 0)
                if first:
                    centre(first, 0)
                    masked_max(first, 0)
                    widen(first)
                    centre(first, 1)
                    masked_max(first, 1)
                if second:
                    total(second, 1)
            steps(pool, step)

        @block.scalar
        def _(act):
            def take(group, use):
                g, p, k = group
                what, n = M_WHAT[use]
                old = is_first(group)
                act.wait_ge(m_full, M_USES * g + use + 1)
                if what == "logit":
                    if not old:
                        act.wait_ge(m_full, M_USES * (g - 1) + M_PROB[n // 2] + 1)
                    out, in_ = logit[:, 2 * n:2 * n + 2, :, TOP:], ps_m[:, :].rearrange("p (i h n) -> p i h n", i=2, n=NB)
                elif what == "bias":
                    if not old:
                        kk = k - 1 + p
                        act.wait_ge(bias_in[1 - p][n], 16 * 2 * (kk + 1))
                    out, in_ = bias_t[n][:, :, :], ps_mb.rearrange("p (r t) -> p r t", r=2)
                elif what == "prob":
                    half, pair = n
                    out, in_ = prob_ct[:, pair, half * CH:(half + 1) * CH], ps_m[:, :]
                    if not old:
                        act.wait_ge(b_full, B_USES * (g - 1) + half + 1)
                elif what == "shift":
                    if not old:
                        kk = k - 1 + p
                        act.wait_ge(shift_in[1 - p][n], 16 * 6 * (kk + 1))
                    out, in_ = shift_t[n][:, :], ps_mb[0:6 * TC * HG, 0:P]
                act.activation(out, in_, ACT.Copy).then_inc(m_free, 1)

            def exp_comp(group, n):
                g, p, k = group
                at = slice(n * TC, (n + 1) * TC)
                act.wait_ge(centred_c, 2 * g + n + 1)
                act.activation(prob_c[:, at, :, :], prob_c[:, at, :, :], ACT.Exp).then_inc(exp_c, 1)

            def exps(group, n):
                g, p, k = group
                kind, c, j = SECOND[n]
                if kind == "selected":
                    r, w = SEL.index((c, j)), width(c, j)
                    for pair in range(2):
                        u = B_SEL[r] + pair
                        act.wait_ge(b_full, B_USES * g + u + 1)
                        if pair == 0 and not (is_first(group) and r < 2):
                            act.wait_ge(pv_sel, len(SEL) * g + r - 1)
                        act.activation(prob_s[r % 2][:, 2 * pair:2 * pair + 2, 0:w], ps_b[:, u % 2, :, 0:w],
                                       ACT.Exp).then_inc(b_read[u % 2], 1)
                elif kind == "local":
                    u, w = B_LOC[j], band_width(j)
                    act.wait_ge(b_full, B_USES * g + u + 1)
                    if not (is_first(group) and j < 3):
                        act.wait_ge(pv_loc, NT * g + max(j - 2, 0))
                    act.activation(prob_l[j % 4][:, :, 0:w].rearrange("p (a h) q -> p a h q", a=2),
                                   ps_b[:, u % 2, :, 0:2 * BAND].rearrange("p a (h q) -> p a h q", h=2)[:, :, :, 0:w],
                                   ACT.Exp).then_inc(b_read[u % 2], 1)

            def evacuate_comp(group):
                g, p, k = group
                for c in range(HC):
                    act.wait_ge(b_full, B_USES * g + c + 1)
                    act.activation(mixed_t[:, 2 + c, :], ps_b[:, c, 0, :], ACT.Copy).then_inc(b_read[c], 1)

            def evacuate(group, c, kind):
                g, p, k = group
                if kind == 0:
                    act.wait_ge(pv_sel, len(SEL) * g + (TC, len(SEL))[c])
                else:
                    act.wait_ge(pv_loc, NT * g + TC * (c + 1))
                if c or not is_first(group):
                    act.wait_ge(b_full, B_USES * g + (0, B_BACK[0] + 1)[c])
                act.activation(mixed_t[:, kind, :], ps_o[:, :], ACT.Copy).then_inc(o_free, 1)

            def step(second, first):
                for n in range(END + 1):
                    if second:
                        if n == 0:
                            evacuate_comp(second)
                        elif n < len(SECOND):
                            exps(second, n)
                        kind, c, j = SECOND[min(n, len(SECOND)) - 1]
                        if 1 < n <= len(SECOND) and (kind, c) != (SECOND + [(None, 0, 0)])[n][:2]:
                            evacuate(second, c, ("selected", "local").index(kind))
                        if n == LATE_SHIFT_AT:
                            take(second, M_SHIFT[1])
                    if first:
                        for use in FIRST_AT.get(n, ()):
                            take(first, use)
                        for half in range(2):
                            if n == EXP_AT[half]:
                                exp_comp(first, half)
            act.wait_ge(consts[0], N_CONST[0])
            steps(act, step)

        @block.vector
        def _(dve):
            def rank(group, i):
                g, p, k = group
                if i % 2 == 0:
                    dve.wait_ge(m_free, M_USES * g + M_LOGIT[i // 2] + 1)
                    if not is_first(group):
                        dve.wait_ge(centred_c, 2 * (g - 1) + i // TC + 1)
                    dve.memset(pad[:, i // 2:i // 2 + 1], 0.0)
                for h in range(HG):
                    last = dve.max(best[:, i, h, :], logit[:, i, h, 0:TOP + NB // NT * (i + 1)])
                last.then_inc(maxed, 1)

            def mark(group, i):
                g, p, k = group
                w = TOP + NB // NT * (i + 1)
                dve.wait_ge(maxed, NT * g + i + 1)
                dve.memset(best[:, i, :, TOP:], SENTINEL).then_inc(ranked, 1)
                dve.wait_ge(ranked, NT * g + i + 1)
                dve.memset(pad[:, TC + i:TC + i + 1], 0.0)
                for h in range(HG):
                    last = dve.match_replace(marked[:, i, h, 0:w], best[:, i, h, :], logit[:, i, h, 0:w], TAKEN)
                last.then_inc(picked, 1)

            def set_bias(group, n):
                g, p, k = group
                at = slice(n * TC, (n + 1) * TC)
                dve.wait_ge(picked, NT * g + TC * (n + 1))
                if not is_first(group):
                    dve.wait_ge(m_full, M_USES * (g - 1) + M_BIAS[n] + 1)
                    dve.wait_ge(bm_done, 2 * (g - 1) + n + 1)
                dve.tensor_scalar(bias[:, at, :, :], marked[:, at, :, TOP:], TAKEN / 2, OUT_OF_REACH,
                                  ALU.is_lt, ALU.mult).then_inc(bias_done, 1)

            def block_maxima(group, u):
                g, p, k = group
                i, heads, k0, w, local = A_UNITS[u]
                n = i // TC
                bank = ps_a[:, u % 2, 0:len(heads) * w]
                dve.wait_ge(a_full, A_USES * g + u + 1)
                if u in (0, A_END[0]) and not is_first(group):
                    dve.wait_ge(bm_done, 2 * (g - 1) + n + 1)
                last = dve.tensor_reduce(block_max[:, i, heads[0]:heads[0] + len(heads), k0 // G:(k0 + w) // G],
                                         bank.rearrange("p (h b t) -> p h b t", h=len(heads), t=G), AX.X, ALU.max)
                for n_h, h in enumerate(heads if local else ()):
                    first_key = max(i * P - WIN, 0)
                    of = n_h * w + first_key - k0
                    size = (i + 1) * P - first_key
                    last = dve.tensor_tensor_reduce(
                        out=banded[:, u % 2, h, 0:size], in0=ps_a[:, u % 2, of:of + size], in1=band_q[:, BAND - size:],
                        scale=1.0, scalar=SENTINEL, op0=ALU.add, op1=ALU.max,
                        accum_out=peak[:, n, 1, h * TC + i % TC:h * TC + i % TC + 1])
                last.then_inc(a_read, 1)

            def shifts(group, n):
                g, p, k = group
                dve.wait_ge(bm_done, 2 * g + n + 1)
                dve.tensor_reduce(peak[:, n, 0, :].rearrange("p (h i) -> p i h", h=HG), sel_max[:, :, :, :],
                                  AX.X, ALU.max).then_inc(sel_done, 1)
                dve.wait_ge(sel_done, 2 * g + n + 1)
                if n or not is_first(group):
                    dve.wait_ge(m_full, M_USES * g + (0, M_SHIFT[0] + 1)[n])
                s0 = 8 * g + 4 * n
                dve.tensor_scalar(shift[:, :, 0, :], peak[:, n, :, :], -1.0, None, ALU.mult).then_inc(shift_step, 1)
                dve.wait_ge(shift_step, s0 + 1)
                dve.scalar_tensor_tensor(peak_rest[:, :, :], peak[:, n, :, :], -1.0, shift[:, :, 0, :],
                                         ALU.mult, ALU.subtract).then_inc(shift_step, 1)
                dve.wait_ge(shift_step, s0 + 2)
                dve.tensor_copy(shift[:, :, 1, :], peak_rest[:, :, :]).then_inc(shift_step, 1)
                dve.wait_ge(shift_step, s0 + 3)
                dve.tensor_tensor(shift[:, :, 2, :], peak_rest[:, :, :], shift[:, :, 1, :], ALU.subtract).then_inc(shift_step, 1)

            def weigh(group, c):
                g, p, k = group
                done = 4 * g + 2 * c
                if c or not is_first(group):
                    dve.wait_ge(mixed_done, 2 * g + c)
                dve.wait_ge(loaded[p], 16 * N_LOAD2 * (k + 1))
                for n, (kinds, gates) in enumerate(((slice(0, 2), slice(1, 3)), (slice(2, 3), slice(0, 1)))):
                    u = B_BACK[c] + n
                    m = kinds.stop - kinds.start
                    sums = ps_b[:, u % 2, 0:m, :].rearrange("p s (i h r) -> p s i h r", i=TC, h=HG)
                    dve.wait_ge(b_full, B_USES * g + u + 1)
                    dve.reciprocal(weight[:, kinds, :, :], sums[:, :, :, :, D]).then_inc(recip, 1)
                    dve.wait_ge(recip, done + n + 1)
                    dve.tensor_tensor(gated[:, kinds, :, :], weight[:, kinds, :, :],
                                      gate[p][:, c * TC:(c + 1) * TC, gates].rearrange("p i s -> p s i").unsqueeze(3)
                                      .broadcast_to([P, m, TC, HG]), ALU.mult).then_inc(gated_done, 1)
                    dve.wait_ge(gated_done, done + n + 1)
                    for s in range(m):
                        last = dve.tensor_tensor(part[:, kinds.start + s, :, :, :], sums[:, s, :, :, 0:D],
                                                 gated[:, kinds.start + s, :, :].unsqueeze(3).broadcast_to([P, TC, HG, D]), ALU.mult)
                    last.then_inc(b_read[u % 2], 1)

            def step(second, first):
                weighed = not second
                for u in range(A_USES):
                    if not weighed and A_AT[u] >= SLOTS * BACK_AT[0] + SLOTS - 1:
                        weighed = True
                        weigh(second, 0)
                    if first:
                        block_maxima(first, u)
                    if second and u == LATE_SHIFT_AFTER:
                        shifts(second, 1)
                    if first:
                        for i in range(NT):
                            if u == MAX_AFTER[i]:
                                rank(first, i)
                            if u == MARK_AFTER[i]:
                                mark(first, i)
                        if u in BIAS_AFTER:
                            set_bias(first, BIAS_AFTER.index(u))
                        if u == SHIFT_AFTER:
                            shifts(first, 0)
                if second:
                    weigh(second, 1)
            def zero(m, done):
                dve.memset(m, 0.0).then_inc(done, 1)

            def ones_of_keys(p):
                rows = keys[p][R_SPLIT:ROWS, :, :].rearrange("r h n -> r (h n)").bitcast(F32)
                dve.memset(rows, PAIR_OF_ONES).then_inc(consts[p], 1)
            zero(q_first[0][0:R_SPLIT, :, :, :], consts[0])
            zero(k_first[0][0:R_SPLIT, :, :], consts[0])
            ones_of_keys(0)
            zero(q_loc[0][0:R_SPLIT, :, :, :], consts[0])
            zero(vc_pad[0][:, :, :], zeros)
            zero(vc_pad[1][:, :, :], zeros)
            zero(v_pad[0][:, :, :, :], zeros)
            zero(marked[:, :, :, :], consts[0])
            zero(block_max[:, :, :, :], consts[0])
            dve.wait_ge(zeros, 3)
            dve.memset(v_pad[0][:, :, :, D:D + 1], 1.0).then_inc(consts[0], 1)
            for p in range(2):
                for h in range(2):
                    dve.memset(vc_pad[p][h * NB:(h + 1) * NB, :, 32 * h + D:32 * h + D + 1], 1.0).then_inc(consts[p], 1)
            dve.wait_ge(key_blocks, 1)
            for p in range(2):
                if p:
                    ones_of_keys(1)
                for h in range(HG):
                    if p or h:
                        dve.tensor_copy(keys[p][0:NB, h, 0:T], keys[0][0:NB, 0, 0:T]).then_inc(consts[p], 1)
            dve.wait_ge(consts[0], N_CONST[0])
            steps(dve, step)

        @block.tensor
        def _(pe):
            def bank_m(group, use):
                g, p, k = group
                if not (is_first(group) and use == 0):
                    pe.wait_ge(m_free, M_USES * g + use)

            def first_part(group, use):
                g, p, k = group
                what, n = M_WHAT[use]
                if what == "logit":
                    if n == 0:
                        pe.wait_ge(loaded_first[p], 16 * N_LOAD1 * (k + 1))
                    bank_m(group, use)
                    for i in (2 * n, 2 * n + 1):
                        at = i % 2 * HG * NB
                        pe.matmul(ps_m[:, at:at + HG * NB], ident_b[:, :],
                                  cmask[:, i, :].unsqueeze(1).broadcast_to([P, HG, NB]), start=True, stop=False)
                        for h in range(HG):
                            last = pe.matmul(ps_m[:, at + h * NB:at + (h + 1) * NB], q_first[p][:, i // TC, h, i % TC * P:(i % TC + 1) * P],
                                             k_first[p][:, h, T:NK], start=False, stop=(h == HG - 1))
                elif what == "bias":
                    pe.wait_ge(bias_done, 2 * g + n + 1)
                    bank_m(group, use)
                    for pair in range(2):
                        for i in range(TC):
                            at = (pair * TC + i) * P
                            last = pe.transpose(ps_mb[:, at:at + P],
                                                bias[:, n * TC + i, 2 * pair:2 * pair + 2, :].rearrange("p h n -> p (h n)"), ident_b[:, :])
                elif what == "prob":
                    half, pair = n
                    pe.wait_ge(exp_c, 2 * g + half + 1)
                    bank_m(group, use)
                    for i in range(TC):
                        last = pe.transpose(ps_m[:, i * P:(i + 1) * P],
                                            prob_c[:, half * TC + i, 2 * pair:2 * pair + 2, :].rearrange("p h n -> p (h n)"), ident_f[:, :])
                else:
                    pe.wait_ge(shift_step, 8 * g + 4 * n + 4)
                    bank_m(group, use)
                    last = pe.transpose(ps_mb[0:6 * TC * HG, 0:P], shift[:, :, :, :].rearrange("p a s r -> p (a s r)"), ident_b[:, :])
                last.then_inc(m_full, 1)

            def logits_a(group, u):
                g, p, k = group
                i, heads, k0, w, local = A_UNITS[u]
                if u == 0:
                    pe.wait_ge(loaded_first[p], 16 * N_LOAD1 * (k + 1))
                if not (is_first(group) and u < 2):
                    pe.wait_ge(a_read, A_USES * g + u - 1)
                for n_h, h in enumerate(heads):
                    last = pe.matmul(ps_a[:, u % 2, n_h * w:(n_h + 1) * w], q_first[p][:, i // TC, h, i % TC * P:(i % TC + 1) * P],
                                     k_first[p][:, h, k0:k0 + w], start=True, stop=(i > 0))
                    if i == 0:
                        last = pe.matmul(ps_a[:, u % 2, n_h * w:n_h * w + TOP * G], ident_b[:, :], causal_q[:, :],
                                         start=False, stop=True)
                last.then_inc(a_full, 1)

            def bank_b(group, u):
                if not (is_first(group) and u < 2):
                    pe.wait_ge(b_read[u % 2], b_count(group[0], u))

            def logits_b(group, n, part):
                g, p, k = group
                kind, c, j = SECOND[n]
                tile = slice(j * P, (j + 1) * P)
                if kind == "selected":
                    r, w = SEL.index((c, j)), width(c, j)
                    if j == 0 and part == 0:
                        pe.wait_ge(bias_in[p][c], 16 * 2 * (k + 1))
                        pe.wait_ge(shift_in[p][c], 16 * 6 * (k + 1))
                    for pair in (part,):
                        u = B_SEL[r] + pair
                        bank_b(group, u)
                        for n_h in range(2):
                            h = 2 * pair + n_h
                            partial = c == 0 and j == 0
                            last = pe.matmul(ps_b[:, u % 2, n_h, 0:w], keys[p][:, h, tile], q_sel[p][:, c, h, CH - w:],
                                             start=True, stop=not partial)
                            if partial:
                                last = pe.matmul(ps_b[:, u % 2, n_h, 0:TOP * G], ident_b[:, :], causal_k[:, :],
                                                 start=False, stop=True)
                        last.then_inc(b_full, 1)
                elif kind == "compressed":
                    u = part
                    if part == 0:
                        pe.wait_ge(loaded[p], 16 * N_LOAD2 * (k + 1))
                        pe.wait_ge(m_free, M_USES * g + M_PROB[1] + 1)
                    bank_b(group, u)
                    for pair in range(2):
                        last = pe.matmul(ps_b[64 * pair:64 * pair + 64, u, 0, :], vc_pad[p][:, pair, :],
                                         prob_ct[:, pair, part * CH:(part + 1) * CH], start=True, stop=True)
                    last.then_inc(b_full, 1)
                elif part == 0:
                    u, w = B_LOC[j], band_width(j)
                    if j == TC - 1:
                        pe.wait_ge(shift_in[p][1], 16 * 6 * (k + 1))
                    bank_b(group, u)
                    for h in range(HG):
                        out = ps_b[:, u % 2, h // 2, h % 2 * BAND:h % 2 * BAND + w]
                        at = j % TC * P
                        here = min(w, CH - at)
                        pe.matmul(out[:, 0:here], keys[p][:, h, tile], q_loc[p][:, c, h, at:at + here], start=True, stop=False)
                        if here < w:
                            pe.matmul(out[:, here:w], keys[p][:, h, tile], q_loc[p][:, c + 1, h, 0:w - here], start=False, stop=False)
                        last = pe.matmul(out, ident_b[:, :], band_k[:, 0:w], start=False, stop=True)
                    last.then_inc(b_full, 1)

            def sums(group, n):
                g, p, k = group
                kind, c, j = SECOND[n]
                if kind == "selected":
                    r, w = SEL.index((c, j)), width(c, j)
                    if j == 0:
                        if c == 0:
                            pe.wait_ge(v_ready, g + 1)
                        if c or not is_first(group):
                            pe.wait_ge(o_free, 4 * g + 2 * c)
                    for pair in range(2):
                        u = B_SEL[r] + pair
                        pe.wait_ge(b_read[u % 2], b_count(g, u) + 1)
                    for h in range(HG):
                        last = pe.matmul(ps_o[32 * h:32 * h + 32, CH - w:], v_pad[p][:, j, h, :],
                                         prob_s[r % 2][:, h, 0:w], start=(j == 0), stop=(j == TC * (c + 1) - 1))
                    last.then_inc(pv_sel, 1)
                elif kind == "local":
                    u = B_LOC[j]
                    at = j % TC * P
                    if j % TC == 0:
                        pe.wait_ge(o_free, 4 * g + 2 * c + 1)
                    pe.wait_ge(b_read[u % 2], b_count(g, u) + 1)
                    for h in range(HG):
                        last = pe.matmul(ps_o[32 * h:32 * h + 32, at:at + P], v_pad[p][:, j, h, :],
                                         prob_l[j % 4][:, h, 0:P], start=True, stop=(j == 0))
                    if j:
                        for h in range(HG):
                            last = pe.matmul(ps_o[32 * h:32 * h + 32, at:at + WIN], v_pad[p][:, j - 1, h, :],
                                             prob_l[(j - 1) % 4][:, h, P:BAND], start=False, stop=True)
                    last.then_inc(pv_loc, 1)

            def back(group, c):
                g, p, k = group
                pe.wait_ge(o_free, 4 * g + 2 * c + 2)
                for n, kinds in enumerate(((0, 1), (2 + c,))):
                    u = B_BACK[c] + n
                    bank_b(group, u)
                    for s, kind in enumerate(kinds):
                        for i in range(TC):
                            last = pe.transpose(ps_b[:, u % 2, s, i * P:(i + 1) * P], mixed_t[:, kind, i * P:(i + 1) * P], ident_f[:, :])
                    last.then_inc(b_full, 1)

            def step(second, first):
                for n in range(END + 1):
                    for slot in range(SLOTS):
                        if first:
                            for u in range(A_USES):
                                if A_AT[u] == n * SLOTS + slot:
                                    logits_a(first, u)
                        if second:
                            if n < len(SECOND) and slot < 2:
                                logits_b(second, n, slot)
                            if slot == 2 and 1 < n <= len(SECOND):
                                sums(second, n - 1)
                            if slot == 2 and n in BACK_AT:
                                back(second, BACK_AT.index(n))
                    if second and n == LATE_SHIFT_AT:
                        first_part(second, M_SHIFT[1])
                    if first:
                        for use in FIRST_AT.get(n, ()):
                            first_part(first, use)
            pe.wait_ge(consts[0], N_CONST[0])
            steps(pe, step)


def feed_forward(nc, dram, ident_f, ident_b):
    with ExitStack() as ctx:
        def sb(name, shape, dt=F32):
            return ctx.enter_context(nc.sbuf_tensor(name, shape, dt))

        def ps(name, shape, dt=F32):
            return ctx.enter_context(nc.psum_tensor(name, shape, dt))

        def sem(name):
            return ctx.enter_context(nc.semaphore(name))

        NE1 = E + 1
        PAD = 8 - K2
        wo = sb("wo", [P, DM])
        w1 = sb("w1", [P, E, F])
        w2 = sb("w2", [P, E, DM])
        w_gu = sb("w_gu", [P, 2 * F])
        w_sd = sb("w_sd", [P, DM])
        w_rs = sb("w_rs", [P, NE1])
        xr = sb("xr", [P, TILES, DM])
        attn = [sb(f"attn_in{p}", [P, TC, DM]) for p in range(2)]
        attn_t = sb("attn_t", [P, CH])
        total = sb("total3", [P, TILES])
        mean = sb("mean3", [P, TILES])
        centred = sb("centred3", [P, TILES, DM])
        squares = sb("squares3", [P, TC, DM])
        sqsum = sb("sqsum3", [P, TILES])
        rstd = sb("rstd3", [P, TILES])
        eps = sb("eps3", [P, 1])
        normed = sb("normed3", [P, TC, DM])
        nt_chunk = sb("nt_chunk", [P, CH])
        nt = sb("nt", [P, B * T])
        logit = sb("logit3", [P, TILES, PAD + E])
        best = sb("best3", [P, TILES, 8])
        marked = sb("marked3", [P, TILES, PAD + E])
        chosen = sb("chosen", [P, TILES, E])
        prob = sb("prob3", [P, TILES, E])
        prob_sum = sb("prob_sum", [P, TILES])
        prob_inv = sb("prob_inv", [P, TILES])
        share = sb("share", [P, TILES, NE1])
        share_rest = sb("share_rest", [P, TILES, NE1])
        share_split = sb("share_split", [P, TILES, P], BF16)
        share_t = sb("share_t", [P, B * T], BF16)
        spread = sb("spread", [P, NE1, P], BF16)
        hidden = [sb(f"hidden{n}", [P, CH]) for n in range(3)]
        shared = sb("shared", [P, CH])
        weighed = [sb(f"weighed{n}", [P, CH]) for n in range(3)]
        out_t = sb("out_t", [P, CH])
        out_sb = sb("out_sb", [P, TC, DM])

        ps_t = ps("ps_t3", [P, CH])
        ps_y = ps("ps_y3", [P, TC, DM])
        ps_h = ps("ps_h3", [P, 2, CH])
        ps_c = ps("ps_c3", [P, 2, CH])
        ps_out = ps("ps_out3", [P, CH])

        a_in = [sem(f"a_in{p}") for p in range(2)]
        x3_in, w3_in, consts, const_step = map(sem, ("x3_in", "w3_in", "consts3", "const_step3"))
        at_ps, at_done, y_ps, added, totals, means, centre, squared, sqsums = map(
            sem, ("at_ps", "at_done", "y_ps", "added3", "totals3", "means3", "centre3", "squared3", "sqsums3"))
        sdevs, rstds, norms, t_ps, nt_done, l_ps, l_done = map(
            sem, ("sdevs3", "rstds3", "norms3", "t_ps3", "nt_done3", "l_ps3", "l_done3"))
        route, exp_done, ct_ps, ct_done = map(sem, ("route", "exp_done3", "ct_ps", "ct_done"))
        h_full, c_full, c_read, down, both, o_done, out_done = map(
            sem, ("h_full", "c_full", "c_read", "down", "both", "o_done", "out_done"))
        h_read = [sem(f"h_read{n}") for n in range(2)]
        stored = sem("stored")
        block = ctx.enter_context(nc.Block())
        N_W = 7

        def chunks(engine, chunk):
            chunk(0, 0, 0)
            chunk(1, 1, 0)
            with engine.Fori(1, CHUNKS // 2) as k:
                chunk(2 * k, 0, k)
                chunk(2 * k + 1, 1, k)

        def started(c):
            return not (isinstance(c, int) and c == 0)

        @block.sync
        def _(sp):
            def chunk(c, p, k):
                if not isinstance(c, int):
                    sp.wait_ge(at_ps, c - 1)
                sp.dma_start(attn[p][:, :, :], dram["attn"].rearrange("b t r -> (b t) r")[ds(c * CH, CH), :]
                             .rearrange("(i p) r -> p i r", p=P)).then_inc(a_in[p], 16)
            chunks(sp, chunk)

            def store(c, p, k):
                sp.wait_ge(out_done, c + 1)
                sp.dma_start(dram["out"][ds(c * CH, CH), :].rearrange("(i p) n -> p i n", p=P), out_sb[:, :, :]).then_inc(stored, 16)
            chunks(sp, store)
            sp.wait_ge(stored, 16 * CHUNKS)

        @block.gpsimd
        def _(pool):
            pool.memset(spread[:, :, :], 0.0).then_inc(const_step, 1)
            pool.memset(share_split[:, :, :], 0.0).then_inc(consts, 1)
            pool.memset(eps[:, :], EPS).then_inc(consts, 1)
            pool.memset(logit[:, :, 0:PAD], SENTINEL).then_inc(consts, 1)
            for s in range(3):
                pool.wait_ge(const_step, s + 1)
                pool.affine_select(out=spread[:, :, :], in_=spread[:, :, :], compare_op=ALU.not_equal, fill=1.0,
                                   base=-s * NE1, pattern=[[-1, NE1], [0, P]], channel_multiplier=1).then_inc(const_step, 1)
            pool.wait_ge(const_step, 4)

            def chunk(c, p, k):
                pool.wait_ge(centre, c + 1)
                if started(c):
                    pool.wait_ge(sqsums, c)
                x = centred[:, ds(c * TC, TC), :]
                pool.tensor_tensor(squares[:, :, :], x, x, ALU.mult).then_inc(squared, 1)
            chunks(pool, chunk)

        @block.scalar
        def _(act):
            act.dma_start(wo[:, :], dram["wo"]).then_inc(w3_in, 16)
            for c in range(CHUNKS):
                act.dma_start(xr[:, c * TC:(c + 1) * TC, :],
                              dram["x"][c * CH:(c + 1) * CH, :].rearrange("(i p) n -> p i n", p=P)).then_inc(x3_in, 16)
            act.dma_start(w_rs[:, 0:E], dram["router_w"]).then_inc(w3_in, 16)
            act.dma_start(w_rs[:, E:NE1], dram["sgate_w"]).then_inc(w3_in, 16)
            act.dma_start(w1[:, :, :], dram["w1"].rearrange("e d f -> d e f")).then_inc(w3_in, 16)
            act.dma_start(w2[:, :, :], dram["w2"].rearrange("e f d -> f e d")).then_inc(w3_in, 16)
            act.dma_start(w_gu[:, :], dram["sgu"]).then_inc(w3_in, 16)
            act.dma_start(w_sd[:, :], dram["sdown"]).then_inc(w3_in, 16)
            act.wait_ge(consts, 3)

            def copy_attn(c, p, k):
                act.wait_ge(at_ps, c + 1)
                if started(c):
                    act.wait_ge(y_ps, c)
                act.activation(attn_t[:, :], ps_t[:, :], ACT.Copy).then_inc(at_done, 1)
            chunks(act, copy_attn)
            act.wait_ge(sqsums, CHUNKS)
            act.activation(sqsum[:, :], sqsum[:, :], ACT.Sqrt, bias=eps[:, 0:1], scale=1.0 / DM).then_inc(sdevs, 1)

            def copy_normed(c, p, k):
                act.wait_ge(t_ps, c + 1)
                if started(c):
                    act.wait_ge(l_ps, c)
                act.activation(nt_chunk[:, :], ps_t[:, :], ACT.Copy).then_inc(nt_done, 1)
                act.activation(nt[:, ds(c * CH, CH)], ps_t[:, :], ACT.Copy).then_inc(nt_done, 1)
                act.wait_ge(l_ps, c + 1)
                act.activation(logit[:, ds(c * TC, TC), PAD:], ps_y[:, :, 0:E], ACT.Copy).then_inc(l_done, 1)
                act.activation(share[:, ds(c * TC, TC), E:NE1], ps_y[:, :, E:NE1], ACT.Copy).then_inc(l_done, 1)
            chunks(act, copy_normed)
            act.wait_ge(l_done, 2 * CHUNKS)
            act.activation(share[:, :, E:NE1], share[:, :, E:NE1], ACT.Exp, scale=-1.0).then_inc(exp_done, 1)
            act.wait_ge(route, 2)
            act.activation(prob[:, :, :], prob[:, :, :], ACT.Exp).then_inc(exp_done, 1)
            for n in range(4):
                act.wait_ge(ct_ps, n + 1)
                act.activation(share_t[:, n * 2 * CH:(n + 1) * 2 * CH], ps_t[:, :].bitcast(BF16), ACT.Copy).then_inc(ct_done, 1)

            def experts(c, p, k):
                for e in range(NE1):
                    act.wait_ge(h_full, (NE1 + 1) * c + e + 1)
                    if e >= 3 or started(c):
                        act.wait_ge(c_read, NE1 * c + e - 2)
                    act.activation(hidden[e % 3][:, :], ps_h[:, e % 2, :], ACT.Silu).then_inc(h_read[e % 2], 1)
                act.wait_ge(down, NE1 * (c + 1))
                if started(c):
                    act.wait_ge(c_full, (NE1 + 1) * c)
                act.activation(out_t[:, :], ps_out[:, :], ACT.Copy).then_inc(o_done, 1)
            chunks(act, experts)

        @block.vector
        def _(dve):
            dve.wait_ge(x3_in, 16 * CHUNKS)
            dve.wait_ge(consts, 3)

            def residual(c, p, k):
                at = ds(c * TC, TC)
                dve.wait_ge(y_ps, c + 1)
                dve.tensor_tensor(xr[:, at, :], xr[:, at, :], ps_y[:, :, :], ALU.add).then_inc(added, 1)
                dve.wait_ge(added, c + 1)
                dve.tensor_reduce(total[:, at], xr[:, at, :], AX.X, ALU.add).then_inc(totals, 1)
                dve.wait_ge(totals, c + 1)
                dve.tensor_scalar(mean[:, at], total[:, at], 1.0 / DM, None, ALU.mult).then_inc(means, 1)
                dve.wait_ge(means, c + 1)
                dve.tensor_tensor(centred[:, at, :], xr[:, at, :], mean[:, at].unsqueeze(2).broadcast_to([P, TC, DM]),
                                  ALU.subtract).then_inc(centre, 1)
                dve.wait_ge(squared, c + 1)
                dve.tensor_reduce(sqsum[:, at], squares[:, :, :], AX.X, ALU.add).then_inc(sqsums, 1)
            chunks(dve, residual)
            dve.wait_ge(sdevs, 1)
            dve.reciprocal(rstd[:, :], sqsum[:, :]).then_inc(rstds, 1)
            dve.wait_ge(rstds, 1)

            def norm(c, p, k):
                at = ds(c * TC, TC)
                if started(c):
                    dve.wait_ge(t_ps, c)
                dve.tensor_tensor(normed[:, :, :], centred[:, at, :], rstd[:, at].unsqueeze(2).broadcast_to([P, TC, DM]),
                                  ALU.mult).then_inc(norms, 1)
            chunks(dve, norm)
            dve.wait_ge(l_done, 2 * CHUNKS)
            for i in range(TILES):
                last = dve.max(best[:, i, :], logit[:, i, :])
            last.then_inc(route, 1)
            dve.wait_ge(route, 1)
            dve.tensor_tensor(prob[:, :, :], logit[:, :, PAD:], best[:, :, 0:1].broadcast_to([P, TILES, E]), ALU.subtract).then_inc(route, 1)
            dve.memset(best[:, :, K2:], SENTINEL).then_inc(route, 1)
            dve.wait_ge(route, 3)
            for i in range(TILES):
                last = dve.match_replace(marked[:, i, :], best[:, i, :], logit[:, i, :], TAKEN)
            last.then_inc(route, 1)
            dve.wait_ge(exp_done, 2)
            dve.tensor_reduce(prob_sum[:, :], prob[:, :, :], AX.X, ALU.add).then_inc(route, 1)
            dve.tensor_scalar(share[:, :, E:NE1], share[:, :, E:NE1], 1.0, None, ALU.add).then_inc(route, 1)
            dve.wait_ge(route, 6)
            dve.reciprocal(prob_inv[:, :], prob_sum[:, :]).then_inc(route, 1)
            dve.reciprocal(share[:, :, E:NE1], share[:, :, E:NE1]).then_inc(route, 1)
            dve.tensor_scalar(chosen[:, :, :], marked[:, :, PAD:], TAKEN / 2, None, ALU.is_ge).then_inc(route, 1)
            dve.wait_ge(route, 9)
            dve.tensor_tensor(chosen[:, :, :], chosen[:, :, :], prob[:, :, :], ALU.mult).then_inc(route, 1)
            dve.wait_ge(route, 10)
            dve.tensor_tensor(share[:, :, 0:E], chosen[:, :, :], prob_inv[:, :].unsqueeze(2).broadcast_to([P, TILES, E]),
                              ALU.mult).then_inc(route, 1)
            dve.wait_ge(route, 11)
            dve.tensor_copy(share_split[:, :, 0 * NE1:1 * NE1], share[:, :, :]).then_inc(route, 1)
            dve.wait_ge(route, 12)
            dve.tensor_tensor(share_rest[:, :, :], share[:, :, :], share_split[:, :, 0 * NE1:1 * NE1], ALU.subtract).then_inc(route, 1)
            dve.wait_ge(route, 13)
            dve.tensor_copy(share_split[:, :, 1 * NE1:2 * NE1], share_rest[:, :, :]).then_inc(route, 1)
            dve.wait_ge(route, 14)
            dve.tensor_tensor(share_split[:, :, 2 * NE1:3 * NE1], share_rest[:, :, :], share_split[:, :, 1 * NE1:2 * NE1], ALU.subtract).then_inc(route, 1)

            def experts(c, p, k):
                n = NE1 + 1
                for e in range(NE1):
                    u = n * c + e
                    dve.wait_ge(h_read[e % 2], n // 2 * c + e // 2 + 1)
                    if e == E:
                        dve.wait_ge(h_full, n * c + n)
                        if started(c):
                            dve.wait_ge(c_read, NE1 * c)
                        dve.tensor_tensor(shared[:, :], hidden[e % 3][:, :], ps_h[:, 1, :], ALU.mult).then_inc(h_read[1], 1)
                        dve.wait_ge(h_read[1], n // 2 * (c + 1))
                    dve.wait_ge(c_full, u + 1)
                    if e >= 3 or started(c):
                        dve.wait_ge(down, NE1 * c + e - 2)
                    of = shared if e == E else hidden[e % 3]
                    dve.tensor_tensor(weighed[e % 3][:, :], of[:, :], ps_c[:, e % 2, :], ALU.mult).then_inc(c_read, 1)
                dve.wait_ge(c_full, n * (c + 1))
                if started(c):
                    dve.wait_ge(stored, 16 * c)
                dve.tensor_tensor(out_sb[:, :, :], xr[:, ds(c * TC, TC), :],
                                  ps_c[:, 1, :].rearrange("p (i n) -> p i n", i=TC), ALU.add).then_inc(out_done, 1)
            chunks(dve, experts)

        @block.tensor
        def _(pe):
            pe.wait_ge(w3_in, 16 * N_W)
            pe.wait_ge(const_step, 4)

            def project(c, p, k):
                pe.wait_ge(a_in[p], 16 * (k + 1))
                if started(c):
                    pe.wait_ge(at_done, c)
                for i in range(TC):
                    last = pe.transpose(ps_t[:, i * P:(i + 1) * P], attn[p][:, i, :], ident_f[:, :])
                last.then_inc(at_ps, 1)
                pe.wait_ge(at_done, c + 1)
                if started(c):
                    pe.wait_ge(added, c)
                for i in range(TC):
                    last = pe.matmul(ps_y[:, i, :], attn_t[:, i * P:(i + 1) * P], wo[:, :], start=True, stop=True)
                last.then_inc(y_ps, 1)
            chunks(pe, project)

            def route_logits(c, p, k):
                pe.wait_ge(norms, c + 1)
                if started(c):
                    pe.wait_ge(nt_done, 2 * c)
                else:
                    pe.wait_ge(at_done, CHUNKS)
                for i in range(TC):
                    last = pe.transpose(ps_t[:, i * P:(i + 1) * P], normed[:, i, :], ident_f[:, :])
                last.then_inc(t_ps, 1)
                pe.wait_ge(nt_done, 2 * c + 1)
                if started(c):
                    pe.wait_ge(l_done, 2 * c)
                else:
                    pe.wait_ge(added, CHUNKS)
                for i in range(TC):
                    last = pe.matmul(ps_y[:, i, 0:NE1], nt_chunk[:, i * P:(i + 1) * P], w_rs[:, :], start=True, stop=True)
                last.then_inc(l_ps, 1)
            chunks(pe, route_logits)
            pe.wait_ge(route, 15)
            pe.wait_ge(nt_done, 2 * CHUNKS)
            for n in range(4):
                if n:
                    pe.wait_ge(ct_done, n)
                for i in range(2 * TC):
                    last = pe.transpose(ps_t[:, :].bitcast(BF16)[:, i * P:(i + 1) * P],
                                        share_split[:, n * 2 * TC + i, :], ident_b[:, :])
                last.then_inc(ct_ps, 1)
            pe.wait_ge(ct_done, 4)

            def experts(c, p, k):
                n = NE1 + 1
                x = nt[:, ds(c * CH, CH)]

                def up(u):
                    w = w1[:, u, :] if u < E else w_gu[:, (u - E) * F:(u - E + 1) * F]
                    if u >= 2 or started(c):
                        pe.wait_ge(h_read[u % 2], n // 2 * c + u // 2)
                    pe.matmul(ps_h[:, u % 2, :], w, x, start=True, stop=True).then_inc(h_full, 1)

                def shares(e):
                    if e >= 2:
                        pe.wait_ge(c_read, NE1 * c + e - 1)
                    elif started(c):
                        pe.wait_ge(*((c_read, NE1 * c) if e == 0 else (out_done, c)))
                    pe.matmul(ps_c[:, e % 2, :], spread[:, e, :], share_t[:, ds(c * CH, CH)], start=True, stop=True).then_inc(c_full, 1)

                def join(e):
                    if e == 0 and started(c):
                        pe.wait_ge(o_done, c)
                    pe.wait_ge(c_read, NE1 * c + e + 1)
                    w = w2[:, e, :] if e < E else w_sd[:, :]
                    pe.matmul(ps_out[:, :], w, weighed[e % 3][:, :], start=(e == 0), stop=(e == NE1 - 1)).then_inc(down, 1)
                for e in range(NE1):
                    up(e)
                    if e == E:
                        up(n - 1)
                    shares(e)
                    if e:
                        join(e - 1)
                join(NE1 - 1)
                pe.wait_ge(o_done, c + 1)
                for i in range(TC):
                    last = pe.transpose(ps_c[:, 1, i * P:(i + 1) * P], out_t[:, i * P:(i + 1) * P], ident_f[:, :])
                last.then_inc(c_full, 1)
            chunks(pe, experts)


def program(nc, dram, made):
    dram["x"] = dram["x"].rearrange("b t n -> (b t) n")
    dram["out"] = dram["out"].rearrange("b t n -> (b t) n")
    for name, shape, dt in (("q", (B, 3 * D, HC, H, CH), BF16), ("k", (B, 3 * D, H, NK), BF16), ("v", (B, T, DM), F32),
                            ("vc", (B, NB, DM), F32), ("gates", (B, P, NT, 3), F32), ("attn", (B, T, DM), F32)):
        dram[name] = nc.dram_tensor(f"made_{name}", shape, dt, kind=made).ap()
    with nc.sbuf_tensor("ident_f", [P, P], F32) as ident_f, nc.sbuf_tensor("ident_b", [P, P], BF16) as ident_b:
        project(nc, dram, ident_f, ident_b)
        attend(nc, dram, ident_b, ident_f)
        feed_forward(nc, dram, ident_f, ident_b)


_INS = {"L0_attn_x": "x", "L0_attn_Wq": "wq", "L0_attn_Wk": "wk", "L0_attn_Wv": "wv", "L0_attn_Wo": "wo",
        "L0_attn_Wck": "wck", "L0_attn_Wcv": "wcv", "L0_attn_Wg": "wg", "L0_attn_bg": "bg",
        "L0_ffn_router_w": "router_w", "L0_ffn_w1": "w1", "L0_ffn_w2": "w2", "L0_ffn_shared_gate_up": "sgu",
        "L0_ffn_shared_down": "sdown", "L0_ffn_shared_gate_w": "sgate_w"}


def kernel(**inputs):
    import numpy as np
    import concourse.bacc as bacc
    from concourse.bass_utils import run_bass_kernel_spmd

    nc = bacc.Bacc("TRN2", target_bir_lowering=False, num_devices=1)
    arrays, dram = {}, {}
    for name, short in _INS.items():
        a = np.ascontiguousarray(inputs[name])
        arrays[f"in_{short}"] = a
        dram[short] = nc.dram_tensor(f"in_{short}", a.shape, mybir.dt.from_np(a.dtype), kind="ExternalInput").ap()
    dram["out"] = nc.dram_tensor("out", (B, T, DM), F32, kind="ExternalOutput").ap()
    program(nc, dram, "Internal")
    return run_bass_kernel_spmd(nc, [arrays], core_ids=[0]).results[0]["out"]
```

```python
from contextlib import ExitStack

import numpy as np

import concourse.bass as bass
from concourse import mybir

F32 = mybir.dt.float32
BF16 = mybir.dt.bfloat16
ALU = mybir.AluOpType
ACT = mybir.ActivationFunctionType
AX = mybir.AxisListType

P = 128
B, T, DM = 4, 1024, 128
H, D = 16, 8
G, NB = 16, T // 16
TOP = 4
WIN = 32
TILES = B * T // P
NT = T // P
CH = 512
TC = CH // P
CHUNKS = B * T // CH
HC = T // CH
NK = T + NB
SCALE = float(D) ** -0.5
EPS = 1e-5
OUT_OF_REACH = -1e30
SENTINEL = -3e38
TAKEN = 3e38
HG = 4
GROUPS = B * H // HG
QUADS = H // HG
SPLITS = ((0, 0), (1, 0), (2, 0), (0, 1), (1, 1), (0, 2))
R_SPLIT = 64
R_SHIFT = R_SPLIT + len(SPLITS) * D
ROWS = R_SHIFT + 3
E, F = 8, 128
PAIR_OF_ONES = float(np.array([0x3F803F80], np.uint32).view(np.float32)[0])
K2 = 2
ds = bass.ds

BAND = P + WIN
SEL = [(c, j) for c in range(HC) for j in range(TC * (c + 1))]
SECOND = [("compressed", 0, 0)] + [x for c in range(HC) for x in
                                   [("selected", c, j) for j in range(TC * (c + 1))]
                                   + [("local", c, j) for j in range(TC * c, TC * (c + 1))]]
END = len(SECOND) + 1
BACK_AT = [SECOND.index(("local", c, TC * (c + 1) - 1)) + 2 for c in range(HC)]


def width(c, j):
    return min(CH, (c + 1) * CH - j * P)


def band_width(j):
    return BAND if j < NT - 1 else P


def uses_of_b():
    sel, loc, back, u = [], [], [], 2
    for n in range(END + 1):
        kind = SECOND[n][0] if n < len(SECOND) else None
        if kind == "selected":
            sel.append(u)
            u += 2
        elif kind == "local":
            loc.append(u)
            u += 1
        if n in BACK_AT:
            back.append(u)
            u += 2
    return sel, loc, back, u


B_SEL, B_LOC, B_BACK, B_USES = uses_of_b()


def b_count(g, u):
    return B_USES // 2 * g + u // 2


def units_of_a():
    out, end = [], []
    for i in range(NT):
        keys = (i + 1) * P
        for w, k0, local in ((min(keys, CH), max(keys - CH, 0), True), (max(keys - CH, 0), 0, False)):
            if w:
                n = CH // w
                out += [(i, tuple(range(h, h + n)), k0, w, local) for h in range(0, HG, n)]
        if i % TC == TC - 1:
            end.append(len(out))
    return out, end


A_UNITS, A_END = units_of_a()
A_USES = len(A_UNITS)
SLOTS = 3
M_WHAT = ([("logit", n) for n in range(4)] + [("bias", 0), ("bias", 1), ("shift", 0), ("prob", (0, 0)),
          ("prob", (0, 1)), ("prob", (1, 0)), ("prob", (1, 1)), ("shift", 1)])
M_USES = len(M_WHAT)
M_LOGIT = [M_WHAT.index(("logit", n)) for n in range(4)]
M_BIAS = [M_WHAT.index(("bias", n)) for n in range(2)]
M_PROB = [M_WHAT.index(("prob", (n, 1))) for n in range(2)]
M_SHIFT = [M_WHAT.index(("shift", n)) for n in range(2)]
A_AT = [0, 3, 6, 7, 9, 10, 13, 17, 19, 23, 26, 27, 28, 31, 32, 33, 33, 35, 36, 38, 39, 40, 42, 43, 45, 50, 52, 53, 54, 55, 56, 58, 59, 61, 62, 63, 66, 67]
M_AT = [2, 3, 4, 5, 12, 15, 16, 17, 18, 19, 21]
LATE_SHIFT_AT = 2
EXP_AT = [14, 17]
LATE_SHIFT_AFTER = 1
MAX_AFTER = [6, 7, 8, 9, 12, 14, 16, 18]
MARK_AFTER = [8, 9, 10, 10, 13, 16, 18, 20]
BIAS_AFTER = [12, 21]
SHIFT_AFTER = 23
N_FIRST_CONST = 8
N_CONST = (10, 11)


def uses_at(n):
    return [use for use, at in enumerate(M_AT) if at == n]


def is_first(group):
    return isinstance(group[0], int) and group[0] == 0


def before(group):
    g, p, k = group
    return g - 1, 1 - p, k - 1 + p


def after(group):
    g, p, k = group
    return g + 1, 1 - p, k + p


def project(nc, dram, ident_f, ident_b):
    with ExitStack() as ctx:
        def sb(name, shape, dt=F32):
            return ctx.enter_context(nc.sbuf_tensor(name, shape, dt))

        def ps(name, shape, dt=F32):
            return ctx.enter_context(nc.psum_tensor(name, shape, dt))

        def sem(name):
            return ctx.enter_context(nc.semaphore(name))

        xs = sb("xs", [P, TILES, DM])
        wq = sb("wq", [P, DM])
        wk = sb("wk", [P, DM])
        wv = sb("wv", [P, DM])
        wqt = sb("wqt", [P, DM])
        wvg = sb("wvg", [P, DM + 3])
        wg_rep = sb("wg_rep", [P, 3])
        bg_rep = sb("bg_rep", [P, 3])
        wc_rep = sb("wc_rep", [P, 2, G, D])
        wc_diag = sb("wc_diag", [P, 2, G, H, D])
        head_of_row = sb("head_of_row", [P, H])
        late = sb("late", [P, 1])
        eps = sb("eps", [P, 1])
        total = sb("total", [P, TILES])
        mean = sb("mean", [P, TILES])
        squares = [sb(f"squares{p}", [P, TC, DM]) for p in range(2)]
        sqsum = sb("sqsum", [P, TILES])
        sdev = sb("sdev", [P, TILES])
        rstd = sb("rstd", [P, TILES])
        normed = sb("normed", [P, TC, DM])
        normed_t = [sb(f"normed_t{p}", [P, CH]) for p in range(2)]
        kt = sb("kt", [P, B * T])
        vt = sb("vt", [P, B * T])
        q_split = [sb(f"q_split{p}", [P, 3, CH], BF16) for p in range(2)]
        k_split = [sb(f"k_split{p}", [P, 3, CH], BF16) for p in range(2)]
        q_rest = sb("q_rest", [P, CH])
        k_rest = sb("k_rest", [P, CH])
        v_out = [sb(f"v_out{p}", [P, TC, DM]) for p in range(2)]
        gates = sb("gates", [P, TILES, 3])
        gate_max = sb("gate_max", [P, TILES])
        gate_sum = sb("gate_sum", [P, TILES])
        gate_inv = sb("gate_inv", [P, TILES])
        kc_split = sb("kc_split", [P, 3, B * NB], BF16)
        kc_rest = sb("kc_rest", [P, B * NB])
        vct = sb("vct", [P, B * NB])
        vc_out = sb("vc_out", [NB, B, DM])

        ps_t = ps("ps_t", [P, CH])
        ps_q = ps("ps_q", [P, CH])
        ps_k = ps("ps_k", [P, CH])
        ps_vt = ps("ps_vt", [P, CH])
        ps_v = ps("ps_v", [P, TC, 256])
        ps_w = ps("ps_w", [P, CH])

        x_in, w_in, diag_made = map(sem, ("x_in", "w_in", "diag_made"))
        wt_ps, wqt_done, wg_ps, wvg_done = map(sem, ("wt_ps", "wqt_done", "wg_ps", "wvg_done"))
        consts, const_step, sums, means, centre = map(sem, ("consts", "const_step", "sums", "means", "centre"))
        squared, sqsums, sdevs, rstds, norms = map(sem, ("squared", "sqsums", "sdevs", "rstds", "norms"))
        t_ps, nt_done, q_ps, k_ps, vt_ps, v_ps = map(sem, ("t_ps", "nt_done", "q_ps", "k_ps", "vt_ps", "v_ps"))
        q0_done, k0_done, vt_done, v_done = map(sem, ("q0_done", "k0_done", "vt_done", "v_done"))
        qr_done, q1_done, q2_done, kr_done, k1_done, k2_done = map(
            sem, ("qr_done", "q1_done", "q2_done", "kr_done", "k1_done", "k2_done"))
        q_out, k_out, v_stored = ([sem(f"{name}{p}") for p in range(2)] for name in ("q_out", "k_out", "v_stored"))
        kc_ps, vc_ps, kc_step, vct_done, vc_tr, vc_done = map(
            sem, ("kc_ps", "vc_ps", "kc_step", "vct_done", "vc_tr", "vc_done"))
        gate_step, gate_exp, end_out = map(sem, ("gate_step", "gate_exp", "end_out"))
        ctx.enter_context(nc.allow_non_contiguous_dma(reason="rows of a few elements"))
        block = ctx.enter_context(nc.Block())
        N_W = 3 + H + 1 + 2 * H

        def chunks(engine, chunk):
            last = CHUNKS // 2 - 1
            chunk(0, 0, 0)
            chunk(1, 1, 0)
            with engine.Fori(1, last) as k:
                chunk(2 * k, 0, k)
                chunk(2 * k + 1, 1, k)
            chunk(2 * last, 0, last)
            chunk(2 * last + 1, 1, last)

        def started(c):
            return not (isinstance(c, int) and c == 0)

        def repeats(c):
            return not (isinstance(c, int) and c < 2)

        def ends(c):
            return isinstance(c, int) and c == CHUNKS - 1

        def store_compressed(engine, s):
            engine.wait_ge(kc_step, (1, 3, 6)[s])
            for b in range(B):
                engine.dma_start(dram["k"][b, s * D:(s + 1) * D, :, T:NK].rearrange("r h n -> h r n"),
                                 kc_split[:, s, b * NB:(b + 1) * NB]).then_inc(end_out, 16)

        @block.sync
        def _(sp):
            for c in range(CHUNKS):
                sp.dma_start(xs[:, c * TC:(c + 1) * TC, :],
                             dram["x"][c * CH:(c + 1) * CH, :].rearrange("(i p) n -> p i n", p=P)).then_inc(x_in, 16)
            with sp.Fori(0, B) as b:
                for half in range(HC):
                    c = b * HC + half
                    for name, split, last, out in (("q", q_split, q2_done, q_out), ("k", k_split, k2_done, k_out)):
                        sp.wait_ge(last, c + 1)
                        for s in range(3):
                            at = dram[name][ds(b, 1), s * D:(s + 1) * D]
                            if name == "q":
                                at = at[:, :, half, :, :].rearrange("a r h t -> h (a r) t")
                            else:
                                at = at[:, :, :, half * CH:(half + 1) * CH].rearrange("a r h t -> h (a r) t")
                            sp.dma_start(at, split[half][:, s, :]).then_inc(out[half], 16)
                    sp.wait_ge(v_done, 2 * c + 2)
                    sp.dma_start(dram["v"][ds(b, 1), half * CH:(half + 1) * CH, :]
                                 .rearrange("a (i p) r -> p (a i) r", p=P), v_out[half][:, :, :]).then_inc(v_stored[half], 16)
            store_compressed(sp, 0)
            sp.wait_ge(gate_step, 7)
            sp.dma_start(dram["gates"].rearrange("b p i k -> p b (i k)"),
                         gates[:, :, :].rearrange("p (b i) k -> p b (i k)", b=B)).then_inc(end_out, 16)
            sp.wait_ge(vc_done, 1)
            sp.dma_start(dram["vc"].rearrange("b n r -> n b r"), vc_out[:, :, :]).then_inc(end_out, 16)
            store_compressed(sp, 2)
            for p in range(2):
                sp.wait_ge(q_out[p], 3 * 16 * CHUNKS // 2)
                sp.wait_ge(k_out[p], 3 * 16 * CHUNKS // 2)
                sp.wait_ge(v_stored[p], 16 * CHUNKS // 2)
            sp.wait_ge(end_out, 16 * (3 * B + 2))

        @block.gpsimd
        def _(pool):
            pool.memset(ident_f[:, :], 0.0).then_inc(const_step, 1)
            pool.memset(ident_b[:, :], 0.0).then_inc(const_step, 1)
            pool.memset(head_of_row[:, :], 1.0).then_inc(const_step, 1)
            pool.memset(late[:, :], 1.0).then_inc(const_step, 1)
            pool.memset(eps[:, :], EPS).then_inc(consts, 1)
            pool.wait_ge(const_step, 4)
            for m in (ident_f, ident_b):
                pool.affine_select(out=m[:, :], in_=m[:, :], compare_op=ALU.not_equal, fill=1.0, base=0,
                                   pattern=[[-1, P]], channel_multiplier=1).then_inc(consts, 1)
            pool.affine_select(out=late[:, :], in_=late[:, :], compare_op=ALU.is_ge, fill=0.0, base=-G,
                               pattern=[[0, 1]], channel_multiplier=1).then_inc(consts, 1)
            pool.affine_select(out=head_of_row[:, :], in_=head_of_row[:, :], compare_op=ALU.is_ge, fill=0.0,
                               base=0, pattern=[[-D, H]], channel_multiplier=1).then_inc(const_step, 1)
            pool.wait_ge(const_step, 5)
            pool.affine_select(out=head_of_row[:, :], in_=head_of_row[:, :], compare_op=ALU.is_ge, fill=0.0,
                               base=D - 1, pattern=[[D, H]], channel_multiplier=-1).then_inc(consts, 1)

            def square(c, p, k):
                pool.wait_ge(centre, c + 1)
                if repeats(c):
                    pool.wait_ge(sqsums, c - 1)
                x = xs[:, ds(c * TC, TC), :]
                pool.tensor_tensor(squares[p][:, :, :], x, x, ALU.mult).then_inc(squared, 1)
            chunks(pool, square)
            pool.wait_ge(consts, 5)
            pool.wait_ge(w_in, 16 * N_W)
            for i in range(2):
                for g in range(G):
                    last = pool.tensor_tensor(
                        wc_diag[:, i, g, :, :], wc_rep[:, i, g, :].unsqueeze(1).broadcast_to([P, H, D]),
                        head_of_row[:, :].unsqueeze(2).broadcast_to([P, H, D]), ALU.mult)
                    last.then_inc(diag_made, 1)

        @block.scalar
        def _(act):
            for w, name in ((wq, "wq"), (wk, "wk"), (wv, "wv")):
                act.dma_start(w[:, :], dram[name]).then_inc(w_in, 16)
            act.dma_start(bg_rep[:, :], dram["bg"].partition_broadcast(P)).then_inc(w_in, 16)
            for h in range(H):
                rows = slice(h * D, (h + 1) * D)
                act.dma_start(wg_rep[rows, :], dram["wg"]).then_inc(w_in, 16)
                for i, name in enumerate(("wck", "wcv")):
                    act.dma_start(wc_rep[rows, i, :, :], dram[name].rearrange("(g d) e -> d g e", d=D)).then_inc(w_in, 16)
            act.wait_ge(consts, 1)
            act.wait_ge(sqsums, CHUNKS)
            act.activation(sdev[:, :], sqsum[:, :], ACT.Sqrt, bias=eps[:, 0:1], scale=1.0 / DM).then_inc(sdevs, 1)

            def copy_normed(c, p, k):
                act.wait_ge(t_ps, c + 1)
                if repeats(c):
                    act.wait_ge(v_ps, c - 1)
                act.activation(normed_t[p][:, :], ps_t[:, :], ACT.Copy).then_inc(nt_done, 1)

            def chunk(c, p, k):
                act.wait_ge(q_ps, c + 1)
                if repeats(c):
                    act.wait_ge(q_out[p], 48 * k)
                act.activation(q_split[p][:, 0, :], ps_q[:, :], ACT.Copy, scale=SCALE).then_inc(q0_done, 1)
                act.wait_ge(k_ps, c + 1)
                if repeats(c):
                    act.wait_ge(k_out[p], 48 * k)
                act.activation(k_split[p][:, 0, :], ps_k[:, :], ACT.Copy).then_inc(k0_done, 1)
                act.activation(kt[:, ds(c * CH, CH)], ps_k[:, :], ACT.Copy).then_inc(k0_done, 1)
                act.wait_ge(vt_ps, c + 1)
                act.activation(vt[:, ds(c * CH, CH)], ps_vt[:, :], ACT.Copy).then_inc(vt_done, 1)
                if not ends(c):
                    copy_normed(c + 1, 1 - p, k + p)
                act.wait_ge(v_ps, c + 1)
                if repeats(c):
                    act.wait_ge(v_stored[p], 16 * k)
                act.activation(v_out[p][:, :, :], ps_v[:, :, 0:DM], ACT.Copy).then_inc(v_done, 1)
                act.activation(gates[:, ds(c * TC, TC), :], ps_v[:, :, DM:DM + 3], ACT.Copy).then_inc(v_done, 1)
            copy_normed(0, 0, 0)
            chunks(act, chunk)
            act.wait_ge(gate_step, 3)
            act.activation(gates[:, :, :], gates[:, :, :], ACT.Exp).then_inc(gate_exp, 1)
            act.wait_ge(vc_ps, 1)
            act.activation(vct[:, :], ps_vt[:, 0:B * NB], ACT.Copy).then_inc(vct_done, 1)
            act.wait_ge(vc_tr, 1)
            act.activation(vc_out[:, :, :], ps_t[0:NB, :].rearrange("n (b r) -> n b r", b=B), ACT.Copy).then_inc(vc_done, 1)
            store_compressed(act, 1)

        @block.vector
        def _(dve):
            def centre_x(c, p, k):
                at = ds(c * TC, TC)
                dve.wait_ge(x_in, 16 * CHUNKS)
                dve.tensor_reduce(total[:, at], xs[:, at, :], AX.X, ALU.add).then_inc(sums, 1)
                dve.wait_ge(sums, c + 1)
                dve.tensor_scalar(mean[:, at], total[:, at], 1.0 / DM, None, ALU.mult).then_inc(means, 1)
                dve.wait_ge(means, c + 1)
                dve.tensor_tensor(xs[:, at, :], xs[:, at, :], mean[:, at].unsqueeze(2).broadcast_to([P, TC, DM]),
                                  ALU.subtract).then_inc(centre, 1)
                if started(c):
                    sum_squares(c - 1, 1 - p)

            def sum_squares(c, p):
                dve.wait_ge(squared, c + 1)
                dve.tensor_reduce(sqsum[:, ds(c * TC, TC)], squares[p][:, :, :], AX.X, ALU.add).then_inc(sqsums, 1)
            chunks(dve, centre_x)
            sum_squares(CHUNKS - 1, 1)
            dve.wait_ge(wt_ps, 1)
            dve.tensor_copy(wqt[:, :], ps_w[:, 0:DM]).then_inc(wqt_done, 1)
            dve.wait_ge(w_in, 16 * N_W)
            dve.tensor_copy(wvg[:, 0:DM], wv[:, :]).then_inc(wvg_done, 1)
            dve.wait_ge(wg_ps, 1)
            dve.tensor_scalar(wvg[:, DM:DM + 3], ps_w[:, DM:DM + 3], 1.0 / H, None, ALU.mult).then_inc(wvg_done, 1)
            dve.wait_ge(sdevs, 1)
            dve.reciprocal(rstd[:, :], sdev[:, :]).then_inc(rstds, 1)
            dve.wait_ge(rstds, 1)
            dve.wait_ge(centre, CHUNKS)

            def norm(c, p, k):
                at = ds(c * TC, TC)
                if started(c):
                    dve.wait_ge(t_ps, c)
                dve.tensor_tensor(normed[:, :, :], xs[:, at, :], rstd[:, at].unsqueeze(2).broadcast_to([P, TC, DM]),
                                  ALU.mult).then_inc(norms, 1)

            def chunk(c, p, k):
                if not ends(c):
                    norm(c + 1, 1 - p, k + p)
                dve.wait_ge(q0_done, c + 1)
                if started(c):
                    dve.wait_ge(q2_done, c)
                dve.scalar_tensor_tensor(q_rest[:, :], ps_q[:, :], SCALE, q_split[p][:, 0, :],
                                         ALU.mult, ALU.subtract).then_inc(qr_done, 1)
                dve.wait_ge(k0_done, 2 * c + 2)
                if started(c):
                    dve.wait_ge(k2_done, c)
                dve.tensor_tensor(k_rest[:, :], kt[:, ds(c * CH, CH)], k_split[p][:, 0, :], ALU.subtract).then_inc(kr_done, 1)
                dve.wait_ge(qr_done, c + 1)
                dve.tensor_copy(q_split[p][:, 1, :], q_rest[:, :]).then_inc(q1_done, 1)
                dve.wait_ge(kr_done, c + 1)
                dve.tensor_copy(k_split[p][:, 1, :], k_rest[:, :]).then_inc(k1_done, 1)
                dve.wait_ge(q1_done, c + 1)
                dve.tensor_tensor(q_split[p][:, 2, :], q_rest[:, :], q_split[p][:, 1, :], ALU.subtract).then_inc(q2_done, 1)
                dve.wait_ge(k1_done, c + 1)
                dve.tensor_tensor(k_split[p][:, 2, :], k_rest[:, :], k_split[p][:, 1, :], ALU.subtract).then_inc(k2_done, 1)
            norm(0, 0, 0)
            chunks(dve, chunk)
            dve.wait_ge(v_done, 2 * CHUNKS)
            dve.tensor_tensor(gates[:, :, :], gates[:, :, :], bg_rep[:, :].unsqueeze(1).broadcast_to([P, TILES, 3]),
                              ALU.add).then_inc(gate_step, 1)
            dve.wait_ge(gate_step, 1)
            dve.tensor_reduce(gate_max[:, :], gates[:, :, :], AX.X, ALU.max).then_inc(gate_step, 1)
            dve.wait_ge(gate_step, 2)
            dve.tensor_tensor(gates[:, :, :], gates[:, :, :], gate_max[:, :].unsqueeze(2).broadcast_to([P, TILES, 3]),
                              ALU.subtract).then_inc(gate_step, 1)
            dve.wait_ge(gate_exp, 1)
            dve.tensor_reduce(gate_sum[:, :], gates[:, :, :], AX.X, ALU.add).then_inc(gate_step, 1)
            dve.wait_ge(gate_step, 4)
            dve.reciprocal(gate_inv[:, :], gate_sum[:, :]).then_inc(gate_step, 1)
            dve.wait_ge(gate_step, 5)
            dve.tensor_tensor(gates[:, :, :], gates[:, :, :], gate_inv[:, :].unsqueeze(2).broadcast_to([P, TILES, 3]),
                              ALU.mult).then_inc(gate_step, 1)
            dve.wait_ge(gate_step, 6)
            dve.wait_ge(consts, 5)
            first = gates[:, :, :].rearrange("p (b i) k -> p b (i k)", b=B)[:, :, 0:1]
            dve.tensor_tensor(first, first, late[:, 0:1].unsqueeze(1).broadcast_to([P, B, 1]), ALU.mult).then_inc(gate_step, 1)
            dve.wait_ge(kc_ps, 1)
            dve.tensor_copy(kc_split[:, 0, :], ps_k[:, 0:B * NB]).then_inc(kc_step, 1)
            dve.wait_ge(kc_step, 1)
            dve.tensor_tensor(kc_rest[:, :], ps_k[:, 0:B * NB], kc_split[:, 0, :], ALU.subtract).then_inc(kc_step, 1)
            dve.wait_ge(kc_step, 2)
            dve.tensor_copy(kc_split[:, 1, :], kc_rest[:, :]).then_inc(kc_step, 1)
            dve.wait_ge(kc_step, 3)
            dve.tensor_tensor(kc_split[:, 2, :], kc_rest[:, :], kc_split[:, 1, :], ALU.subtract).then_inc(kc_step, 3)

        @block.tensor
        def _(pe):
            pe.wait_ge(w_in, 16 * N_W)
            pe.wait_ge(consts, 5)
            pe.transpose(ps_w[:, 0:DM], wq[:, :], ident_f[:, :]).then_inc(wt_ps, 1)
            pe.wait_ge(wqt_done, 1)
            pe.matmul(ps_w[:, DM:DM + 3], wqt[:, :], wg_rep[:, :], start=True, stop=True).then_inc(wg_ps, 1)
            pe.wait_ge(wvg_done, 2)

            def turn(c):
                pe.wait_ge(norms, c + 1)
                if started(c):
                    pe.wait_ge(nt_done, c)
                for i in range(TC):
                    last = pe.transpose(ps_t[:, i * P:(i + 1) * P], normed[:, i, :], ident_f[:, :])
                last.then_inc(t_ps, 1)

            def chunk(c, p, k):
                pe.wait_ge(nt_done, c + 1)
                if started(c):
                    pe.wait_ge(qr_done, c)
                pe.matmul(ps_q[:, :], wq[:, :], normed_t[p][:, :], start=True, stop=True).then_inc(q_ps, 1)
                if started(c):
                    pe.wait_ge(k0_done, 2 * c)
                pe.matmul(ps_k[:, :], wk[:, :], normed_t[p][:, :], start=True, stop=True).then_inc(k_ps, 1)
                if started(c):
                    pe.wait_ge(vt_done, c)
                pe.matmul(ps_vt[:, :], wv[:, :], normed_t[p][:, :], start=True, stop=True).then_inc(vt_ps, 1)
                if not ends(c):
                    turn(c + 1)
                if started(c):
                    pe.wait_ge(v_done, 2 * c)
                for i in range(TC):
                    last = pe.matmul(ps_v[:, i, 0:DM + 3], normed_t[p][:, i * P:(i + 1) * P], wvg[:, :], start=True, stop=True)
                last.then_inc(v_ps, 1)
            turn(0)
            chunks(pe, chunk)
            pe.wait_ge(diag_made, 2 * G)
            pe.wait_ge(k0_done, 2 * CHUNKS)
            pe.wait_ge(vt_done, CHUNKS)
            for i, (src, dst, made) in enumerate(((kt, ps_k, kc_ps), (vt, ps_vt, vc_ps))):
                of_offset = src[:, :].rearrange("p (n g) -> p g n", g=G)
                for g in range(G):
                    last = pe.matmul(dst[:, 0:B * NB], wc_diag[:, i, g, :, :].rearrange("p h d -> p (h d)"),
                                     of_offset[:, g, :], start=(g == 0), stop=(g == G - 1))
                last.then_inc(made, 1)
            pe.wait_ge(vct_done, 1)
            for b in range(B):
                last = pe.transpose(ps_t[0:NB, b * P:(b + 1) * P], vct[:, b * NB:(b + 1) * NB], ident_f[:, :])
            last.then_inc(vc_tr, 1)


def attend(nc, dram, ident_b, ident_f):
    with ExitStack() as ctx:
        def sb(name, shape, dt=F32):
            return ctx.enter_context(nc.sbuf_tensor(name, shape, dt))

        def ps(name, shape, dt=F32):
            return ctx.enter_context(nc.psum_tensor(name, shape, dt))

        def sem(name):
            return ctx.enter_context(nc.semaphore(name))

        cmask = sb("cmask", [P, NT, NB], BF16)
        causal_q = sb("causal_q", [P, TOP * G], BF16)
        causal_k = sb("causal_k", [P, TOP * G], BF16)
        band_q = sb("band_q", [P, BAND], BF16)
        band_k = sb("band_k", [P, BAND], BF16)
        q_loc = [sb(f"q_loc{p}", [ROWS, HC, HG, CH], BF16) for p in range(2)]
        q_sel = [sb(f"q_sel{p}", [ROWS, HC, HG, CH], BF16) for p in range(2)]
        keys = [sb(f"keys{p}", [ROWS, HG, NK], BF16) for p in range(2)]
        q_first = [sb(f"q_first{p}", [R_SHIFT, HC, HG, CH], BF16) for p in range(2)]
        k_first = [sb(f"k_first{p}", [R_SHIFT, HG, NK], BF16) for p in range(2)]
        v_in = [sb(f"v_in{p}", [P, NT, HG * D]) for p in range(2)]
        v_pad = [sb(f"v_pad{p}", [P, NT, HG, 32]) for p in range(2)]
        vc_pad = [sb(f"vc_pad{p}", [P, 2, 64]) for p in range(2)]
        gate = [sb(f"gate{p}", [P, NT, 3]) for p in range(2)]
        logit = sb("logit", [P, NT, HG, TOP + NB])
        best = sb("best", [P, NT, HG, 8])
        marked = sb("marked", [P, NT, HG, TOP + NB])
        bias = sb("bias", [P, NT, HG, NB], BF16)
        block_max = sb("block_max", [P, NT, HG, NB])
        sel_max = sb("sel_max", [P, TC, HG, NB])
        prob_c = (marked[:, :, :, :].rearrange("p i h n -> p (i h n)")[:, 0:NT * HG * NB]
                  .rearrange("p (i h n) -> p i h n", i=NT, h=HG))
        prob_ct = sb("prob_ct", [P, 2, T])
        peak = sb("peak", [P, 2, 2, TC * HG])
        peak_rest = sb("peak_rest", [P, 2, TC * HG])
        shift = sb("shift", [P, 2, 3, TC * HG], BF16)
        bias_t = [sb(f"bias_t{n}", [P, 2, CH], BF16) for n in range(2)]
        shift_t = [sb(f"shift_t{n}", [6 * TC * HG, P], BF16) for n in range(2)]
        banded = sb("banded", [P, 2, HG, BAND], BF16)
        pad = sb("pad", [P, TC + NT])
        turn = sb("turn", [P, 4])
        prob_s = [sb(f"prob_s{n}", [P, HG, CH]) for n in range(2)]
        prob_l = [sb(f"prob_l{n}", [P, HG, BAND]) for n in range(4)]
        mixed_t = sb("mixed_t", [P, 4, CH])
        weight = sb("weight", [P, 3, TC, HG])
        gated = sb("gated", [P, 3, TC, HG])
        part = sb("part", [P, 3, TC, HG, D])
        part2 = sb("part2", [P, TC, HG, D])
        mixed = sb("mixed", [P, NT, HG * D])

        ps_a = ps("ps_a", [P, 2, CH])
        ps_b = ps("ps_b", [P, 2, 2, CH])
        ps_o = ps("ps_o", [P, CH])
        ps_m = ps("ps_m", [P, CH])
        ps_mb = ps_m[:, :].bitcast(BF16)

        loaded_first = [sem(f"loaded_first{p}") for p in range(2)]
        loaded = [sem(f"loaded{p}") for p in range(2)]
        bias_in = [[sem(f"bias_in{p}{n}") for n in range(2)] for p in range(2)]
        shift_in = [[sem(f"shift_in{p}{n}") for n in range(2)] for p in range(2)]
        consts = [sem(f"s_consts{p}") for p in range(2)]
        first_consts = sem("first_consts")
        const_step, key_blocks, v_ready, zeros = map(sem, ("s_const_step", "key_blocks", "v_ready", "zeros"))
        m_full, m_free, a_full, a_read = map(sem, ("m_full", "m_free", "a_full", "a_read"))
        maxed, ranked, picked, bias_done = map(sem, ("maxed", "ranked", "picked", "bias_done"))
        centred_c, exp_c, bm_done, sel_done, shift_step = map(
            sem, ("centred_c", "exp_c", "bm_done", "sel_done", "shift_step"))
        b_full = sem("b_full")
        b_read = [sem(f"b_read{n}") for n in range(2)]
        pv_sel, pv_loc = map(sem, ("pv_sel", "pv_loc"))
        o_free, recip, gated_done, summed, mixed_done = map(
            sem, ("o_free", "recip", "gated_done", "summed", "mixed_done"))
        mixed_out = [sem(f"mixed_out{p}") for p in range(2)]
        ctx.enter_context(nc.allow_non_contiguous_dma(reason="rows of heads"))
        block = ctx.enter_context(nc.Block())

        def steps(engine, step):
            step(None, (0, 0, 0))
            step((0, 0, 0), (1, 1, 0))
            step((1, 1, 0), (2, 0, 1))
            last = GROUPS // 2 - 1
            with engine.Fori(1, last - 1) as k:
                step((2 * k, 0, k), (2 * k + 1, 1, k))
                step((2 * k + 1, 1, k), (2 * k + 2, 0, k + 1))
            step((GROUPS - 4, 0, last - 1), (GROUPS - 3, 1, last - 1))
            step((GROUPS - 3, 1, last - 1), (GROUPS - 2, 0, last))
            step((GROUPS - 2, 0, last), (GROUPS - 1, 1, last))
            step((GROUPS - 1, 1, last), None)

        N_LOAD1 = 2 * 3
        N_LOAD2 = 3 * 3 + 1 + HG + 1

        def load_splits(sp, to, name, group, sem):
            g = group[0]
            b, h0 = ds(g // QUADS, 1), ds(g % QUADS * HG, HG)
            at = R_SPLIT
            for n in (3, 2, 1):
                if name == "q":
                    src = dram["q"][b, 0:n * D, :, h0, :].rearrange("a r c h t -> (a r) c (h t)")
                    dst = to[at:at + n * D, :, :, :].rearrange("r c h t -> r c (h t)")
                    sp.dma_start(dst, src).then_inc(sem, 16)
                else:
                    s = 3 - n
                    src = (dram["k"][b, s * D:(s + 1) * D, h0, :].rearrange("a r h t -> a r (h t)")
                           .broadcast_to([n, D, HG * NK]))
                    sp.dma_start(to[at:at + n * D, :, :].rearrange("r h t -> r (h t)"), src).then_inc(sem, 16)
                at += n * D

        @block.sync
        def _(sp):
            def load_first(group):
                g, p, k = group
                if not (isinstance(g, int) and g < 2):
                    sp.wait_ge(a_full, A_USES * (g - 1))
                load_splits(sp, q_first[p], "q", group, loaded_first[p])
                load_splits(sp, k_first[p], "k", group, loaded_first[p])

            def load_second(group):
                g, p, k = group
                if not (isinstance(g, int) and g < 2):
                    sp.wait_ge(b_full, B_USES * (g - 1))
                load_splits(sp, keys[p], "k", group, loaded[p])
                load_splits(sp, q_sel[p], "q", group, loaded[p])
                load_splits(sp, q_loc[p], "q", group, loaded[p])
                rows = ds(g % QUADS * (HG * D), HG * D)
                sp.dma_start(v_in[p][:, :, :], dram["v"][ds(g // QUADS, 1), :, rows]
                             .rearrange("a (i p) r -> p (a i) r", p=P)).then_inc(loaded[p], 16)
                sp.dma_start(gate[p][:, :, :], dram["gates"][ds(g // QUADS, 1), :, :, :]
                             .rearrange("a p i k -> p (a i) k")).then_inc(loaded[p], 16)
                for h in range(HG):
                    r0, c0 = h % 2 * NB, h % 2 * 32
                    sp.dma_start(vc_pad[p][r0:r0 + NB, h // 2, c0:c0 + D],
                                 dram["vc"][ds(g // QUADS, 1), :, ds(g % QUADS * (HG * D) + h * D, D)]
                                 .rearrange("a n r -> n (a r)")).then_inc(loaded[p], 16)

            def place(group, n):
                g, p, k = group
                sp.wait_ge(m_free, M_USES * g + M_BIAS[n] + 1)
                for odd in range(2):
                    sp.dma_start(q_sel[p][0:NB, n, odd::2, :],
                                 bias_t[n][odd * NB:(odd + 1) * NB, :, :]).then_inc(bias_in[p][n], 16)

            def place_shift(group, n):
                g, p, k = group
                sp.wait_ge(m_free, M_USES * g + M_SHIFT[n] + 1)
                w = TC * HG
                for kind, q in enumerate((q_sel, q_loc)):
                    for s in range(3):
                        r0 = (3 * kind + s) * w
                        sp.dma_start(q[p][R_SHIFT + s:R_SHIFT + s + 1, n, :, :].rearrange("s h (i q) -> s (h i) q", q=P),
                                     shift_t[n][r0:r0 + w, :]).then_inc(shift_in[p][n], 16)

            def store(group, c):
                g, p, k = group
                sp.wait_ge(mixed_done, 2 * g + c + 1)
                b, quad = g // QUADS, g % QUADS
                sp.dma_start(dram["attn"][ds(b, 1), c * CH:(c + 1) * CH, ds(quad * HG * D, HG * D)]
                             .rearrange("a (i p) r -> p (a i) r", p=P), mixed[:, c * TC:(c + 1) * TC, :]).then_inc(mixed_out[c], 16)

            def step(second, first):
                if first and is_first(first):
                    load_first(first)
                    sp.wait_ge(consts[0], N_CONST[0])
                    load_second(first)
                    sp.wait_ge(consts[1], N_CONST[1])
                    load_first(after(first))
                if second:
                    place_shift(second, 1)
                    if not is_first(second):
                        store(before(second), 1)
                if first:
                    if not is_first(first):
                        load_second(first)
                    place(first, 0)
                if second:
                    store(second, 0)
                if first:
                    place(first, 1)
                    place_shift(first, 0)
                    if not (isinstance(first[0], int) and first[0] >= GROUPS - 2):
                        load_first(after(after(first)))
                elif second:
                    store(second, 1)
            steps(sp, step)
            for n in range(2):
                sp.wait_ge(mixed_out[n], 16 * GROUPS)

        @block.gpsimd
        def _(pool):
            for m in (cmask, causal_q, band_q, causal_k, band_k):
                pool.memset(m[...], 0.0).then_inc(const_step, 1)
            pool.memset(logit[:, :, :, 0:TOP], SENTINEL).then_inc(first_consts, 1)
            pool.memset(keys[0][0:R_SPLIT, 0, 0:T], 1.0).then_inc(const_step, 1)
            pool.memset(turn[:, 0:1], 0.0).then_inc(const_step, 1)
            pool.wait_ge(const_step, 7)

            def reach(m, base, pattern, multiplier, done):
                pool.affine_select(out=m, in_=m, compare_op=ALU.is_ge, fill=OUT_OF_REACH, base=base,
                                   pattern=pattern, channel_multiplier=multiplier).then_inc(done, 1)
            reach(cmask[:, :, :], -G, [[P, NT], [-G, NB]], 1, first_consts)
            reach(causal_q[:, :], 0, [[-1, TOP * G]], 1, first_consts)
            reach(band_q[:, :], 0, [[1, BAND]], -1, const_step)
            reach(band_k[:, :], 0, [[1, BAND]], -1, const_step)
            pool.affine_select(out=keys[0][0:NB, 0, 0:T], in_=keys[0][0:NB, 0, 0:T], compare_op=ALU.is_ge, fill=0.0,
                               base=0, pattern=[[1, T]], channel_multiplier=-G).then_inc(const_step, 1)
            pool.wait_ge(const_step, 10)
            reach(band_q[:, :], WIN, [[-1, BAND]], 1, first_consts)
            pool.affine_select(out=keys[0][0:NB, 0, 0:T], in_=keys[0][0:NB, 0, 0:T], compare_op=ALU.is_ge, fill=0.0,
                               base=G - 1, pattern=[[-1, T]], channel_multiplier=G).then_inc(key_blocks, 1)
            pool.memset(marked[:, :, :, :], 0.0).then_inc(first_consts, 1)
            reach(causal_k[:, :], 0, [[1, TOP * G]], -1, consts[0])
            reach(band_k[:, :], WIN, [[-1, BAND]], 1, consts[0])
            for p in range(2):
                pool.memset(v_pad[p][:, :, :, :], 0.0).then_inc(const_step, 1)
                pool.memset(q_loc[p][0:R_SPLIT, :, :, :], 0.0).then_inc(consts[p], 1)
                pool.wait_ge(const_step, 11 + p)
                pool.memset(v_pad[p][:, :, :, D:D + 1], 1.0).then_inc(consts[p], 1)
            for m in (q_first[1][0:R_SPLIT, :, :, :], k_first[1][0:R_SPLIT, :, :]):
                pool.memset(m, 0.0).then_inc(consts[1], 1)

            def widen(group):
                g, p, k = group
                pool.wait_ge(loaded[p], 16 * N_LOAD2 * (k + 1))
                if not (isinstance(g, int) and g < 2):
                    pool.wait_ge(b_full, B_USES * (g - 1))
                pool.tensor_tensor(turn[:, 1:2], turn[:, 0:1], turn[:, 0:1], ALU.add)
                pool.tensor_copy(v_pad[p][:, :, :, 0:D], v_in[p][:, :, :].rearrange("p i (h d) -> p i h d", d=D)).then_inc(v_ready, 1)

            def centre(group, n):
                g, p, k = group
                at = slice(n * TC, (n + 1) * TC)
                pool.wait_ge(bias_done, 2 * g + n + 1)
                pool.tensor_tensor(prob_c[:, at, :, :], logit[:, at, :, TOP:], best[:, at, :, 0:1].broadcast_to([P, TC, HG, NB]),
                                   ALU.subtract).then_inc(centred_c, 1)

            def masked_max(group, n):
                g, p, k = group
                at = slice(n * TC, (n + 1) * TC)
                pool.wait_ge(a_read, A_USES * g + A_END[n])
                pool.wait_ge(bias_done, 2 * g + n + 1)
                if n or not is_first(group):
                    pool.wait_ge(sel_done, 2 * g + n)
                pool.tensor_tensor(sel_max[:, :, :, :], block_max[:, at, :, :], bias[:, at, :, :], ALU.add).then_inc(bm_done, 1)

            def total(group, c):
                g, p, k = group
                for n in range(2):
                    pool.wait_ge(b_read[n], b_count(g, B_BACK[c] + n) + 1)
                pool.tensor_tensor(part2[:, :, :, :], part[:, 0, :, :, :], part[:, 1, :, :, :], ALU.add).then_inc(summed, 1)
                pool.wait_ge(summed, 2 * g + c + 1)
                if not is_first(group):
                    pool.wait_ge(mixed_out[c], 16 * g)
                pool.tensor_tensor(mixed[:, c * TC:(c + 1) * TC, :].rearrange("p i (h d) -> p i h d", d=D),
                                   part2[:, :, :, :], part[:, 2, :, :, :], ALU.add).then_inc(mixed_done, 1)

            def step(second, first):
                if second:
                    total(second, 0)
                if first:
                    centre(first, 0)
                    masked_max(first, 0)
                    widen(first)
                    centre(first, 1)
                    masked_max(first, 1)
                if second:
                    total(second, 1)
            steps(pool, step)

        @block.scalar
        def _(act):
            def take(group, use):
                g, p, k = group
                what, n = M_WHAT[use]
                old = is_first(group)
                act.wait_ge(m_full, M_USES * g + use + 1)
                if what == "logit":
                    if not old:
                        act.wait_ge(m_full, M_USES * (g - 1) + M_PROB[n // 2] + 1)
                    out, in_ = logit[:, 2 * n:2 * n + 2, :, TOP:], ps_m[:, :].rearrange("p (i h n) -> p i h n", i=2, n=NB)
                elif what == "bias":
                    if not old:
                        kk = k - 1 + p
                        act.wait_ge(bias_in[1 - p][n], 16 * 2 * (kk + 1))
                    out, in_ = bias_t[n][:, :, :], ps_mb.rearrange("p (r t) -> p r t", r=2)
                elif what == "prob":
                    half, pair = n
                    out, in_ = prob_ct[:, pair, half * CH:(half + 1) * CH], ps_m[:, :]
                    if not old:
                        act.wait_ge(b_full, B_USES * (g - 1) + half + 1)
                elif what == "shift":
                    if not old:
                        kk = k - 1 + p
                        act.wait_ge(shift_in[1 - p][n], 16 * 6 * (kk + 1))
                    out, in_ = shift_t[n][:, :], ps_mb[0:6 * TC * HG, 0:P]
                act.activation(out, in_, ACT.Copy).then_inc(m_free, 1)

            def exp_comp(group, n):
                g, p, k = group
                at = slice(n * TC, (n + 1) * TC)
                act.wait_ge(centred_c, 2 * g + n + 1)
                act.activation(prob_c[:, at, :, :], prob_c[:, at, :, :], ACT.Exp).then_inc(exp_c, 1)

            def exps(group, n):
                g, p, k = group
                kind, c, j = SECOND[n]
                if kind == "selected":
                    r, w = SEL.index((c, j)), width(c, j)
                    for pair in range(2):
                        u = B_SEL[r] + pair
                        act.wait_ge(b_full, B_USES * g + u + 1)
                        if pair == 0 and not (is_first(group) and r < 2):
                            act.wait_ge(pv_sel, len(SEL) * g + r - 1)
                        act.activation(prob_s[r % 2][:, 2 * pair:2 * pair + 2, 0:w], ps_b[:, u % 2, :, 0:w],
                                       ACT.Exp).then_inc(b_read[u % 2], 1)
                elif kind == "local":
                    u, w = B_LOC[j], band_width(j)
                    act.wait_ge(b_full, B_USES * g + u + 1)
                    if not (is_first(group) and j < 3):
                        act.wait_ge(pv_loc, NT * g + max(j - 2, 0))
                    act.activation(prob_l[j % 4][:, :, 0:w].rearrange("p (a h) q -> p a h q", a=2),
                                   ps_b[:, u % 2, :, 0:2 * BAND].rearrange("p a (h q) -> p a h q", h=2)[:, :, :, 0:w],
                                   ACT.Exp).then_inc(b_read[u % 2], 1)

            def evacuate_comp(group):
                g, p, k = group
                for c in range(HC):
                    act.wait_ge(b_full, B_USES * g + c + 1)
                    act.activation(mixed_t[:, 2 + c, :], ps_b[:, c, 0, :], ACT.Copy).then_inc(b_read[c], 1)

            def evacuate(group, c, kind):
                g, p, k = group
                if kind == 0:
                    act.wait_ge(pv_sel, len(SEL) * g + (TC, len(SEL))[c])
                else:
                    act.wait_ge(pv_loc, NT * g + TC * (c + 1))
                if c or not is_first(group):
                    act.wait_ge(b_full, B_USES * g + (0, B_BACK[0] + 1)[c])
                act.activation(mixed_t[:, kind, :], ps_o[:, :], ACT.Copy).then_inc(o_free, 1)

            def step(second, first):
                for n in range(END + 1):
                    if second:
                        if n == 0:
                            evacuate_comp(second)
                        elif n < len(SECOND):
                            exps(second, n)
                        kind, c, j = SECOND[min(n, len(SECOND)) - 1]
                        if 1 < n <= len(SECOND) and (kind, c) != (SECOND + [(None, 0, 0)])[n][:2]:
                            evacuate(second, c, ("selected", "local").index(kind))
                        if n == LATE_SHIFT_AT:
                            take(second, M_SHIFT[1])
                    if first:
                        for use in uses_at(n):
                            take(first, use)
                        for half in range(2):
                            if n == EXP_AT[half]:
                                exp_comp(first, half)
            act.wait_ge(first_consts, N_FIRST_CONST)
            steps(act, step)

        @block.vector
        def _(dve):
            def rank(group, i):
                g, p, k = group
                if i % 2 == 0:
                    dve.wait_ge(m_free, M_USES * g + M_LOGIT[i // 2] + 1)
                    if not is_first(group):
                        dve.wait_ge(centred_c, 2 * (g - 1) + i // TC + 1)
                    dve.memset(pad[:, i // 2:i // 2 + 1], 0.0)
                for h in range(HG):
                    last = dve.max(best[:, i, h, :], logit[:, i, h, 0:TOP + NB // NT * (i + 1)])
                last.then_inc(maxed, 1)

            def mark(group, i):
                g, p, k = group
                w = TOP + NB // NT * (i + 1)
                dve.wait_ge(maxed, NT * g + i + 1)
                dve.memset(best[:, i, :, TOP:], SENTINEL).then_inc(ranked, 1)
                dve.wait_ge(ranked, NT * g + i + 1)
                dve.memset(pad[:, TC + i:TC + i + 1], 0.0)
                for h in range(HG):
                    last = dve.match_replace(marked[:, i, h, 0:w], best[:, i, h, :], logit[:, i, h, 0:w], TAKEN)
                last.then_inc(picked, 1)

            def set_bias(group, n):
                g, p, k = group
                at = slice(n * TC, (n + 1) * TC)
                dve.wait_ge(picked, NT * g + TC * (n + 1))
                if not is_first(group):
                    dve.wait_ge(m_full, M_USES * (g - 1) + M_BIAS[n] + 1)
                    dve.wait_ge(bm_done, 2 * (g - 1) + n + 1)
                dve.tensor_scalar(bias[:, at, :, :], marked[:, at, :, TOP:], TAKEN / 2, OUT_OF_REACH,
                                  ALU.is_lt, ALU.mult).then_inc(bias_done, 1)

            def block_maxima(group, u):
                g, p, k = group
                i, heads, k0, w, local = A_UNITS[u]
                n = i // TC
                bank = ps_a[:, u % 2, 0:len(heads) * w]
                dve.wait_ge(a_full, A_USES * g + u + 1)
                if u in (0, A_END[0]) and not is_first(group):
                    dve.wait_ge(bm_done, 2 * (g - 1) + n + 1)
                last = dve.tensor_reduce(block_max[:, i, heads[0]:heads[0] + len(heads), k0 // G:(k0 + w) // G],
                                         bank.rearrange("p (h b t) -> p h b t", h=len(heads), t=G), AX.X, ALU.max)
                for n_h, h in enumerate(heads if local else ()):
                    first_key = max(i * P - WIN, 0)
                    of = n_h * w + first_key - k0
                    size = (i + 1) * P - first_key
                    last = dve.tensor_tensor_reduce(
                        out=banded[:, u % 2, h, 0:size], in0=ps_a[:, u % 2, of:of + size], in1=band_q[:, BAND - size:],
                        scale=1.0, scalar=SENTINEL, op0=ALU.add, op1=ALU.max,
                        accum_out=peak[:, n, 1, h * TC + i % TC:h * TC + i % TC + 1])
                last.then_inc(a_read, 1)

            def shifts(group, n):
                g, p, k = group
                dve.wait_ge(bm_done, 2 * g + n + 1)
                dve.tensor_reduce(peak[:, n, 0, :].rearrange("p (h i) -> p i h", h=HG), sel_max[:, :, :, :],
                                  AX.X, ALU.max).then_inc(sel_done, 1)
                dve.wait_ge(sel_done, 2 * g + n + 1)
                if n or not is_first(group):
                    dve.wait_ge(m_full, M_USES * g + (0, M_SHIFT[0] + 1)[n])
                s0 = 8 * g + 4 * n
                dve.tensor_scalar(shift[:, :, 0, :], peak[:, n, :, :], -1.0, None, ALU.mult).then_inc(shift_step, 1)
                dve.wait_ge(shift_step, s0 + 1)
                dve.scalar_tensor_tensor(peak_rest[:, :, :], peak[:, n, :, :], -1.0, shift[:, :, 0, :],
                                         ALU.mult, ALU.subtract).then_inc(shift_step, 1)
                dve.wait_ge(shift_step, s0 + 2)
                dve.tensor_copy(shift[:, :, 1, :], peak_rest[:, :, :]).then_inc(shift_step, 1)
                dve.wait_ge(shift_step, s0 + 3)
                dve.tensor_tensor(shift[:, :, 2, :], peak_rest[:, :, :], shift[:, :, 1, :], ALU.subtract).then_inc(shift_step, 1)

            def weigh(group, c):
                g, p, k = group
                done = 4 * g + 2 * c
                if c or not is_first(group):
                    dve.wait_ge(mixed_done, 2 * g + c)
                dve.wait_ge(loaded[p], 16 * N_LOAD2 * (k + 1))
                for n, (kinds, gates) in enumerate(((slice(0, 2), slice(1, 3)), (slice(2, 3), slice(0, 1)))):
                    u = B_BACK[c] + n
                    m = kinds.stop - kinds.start
                    sums = ps_b[:, u % 2, 0:m, :].rearrange("p s (i h r) -> p s i h r", i=TC, h=HG)
                    dve.wait_ge(b_full, B_USES * g + u + 1)
                    dve.reciprocal(weight[:, kinds, :, :], sums[:, :, :, :, D]).then_inc(recip, 1)
                    dve.wait_ge(recip, done + n + 1)
                    dve.tensor_tensor(gated[:, kinds, :, :], weight[:, kinds, :, :],
                                      gate[p][:, c * TC:(c + 1) * TC, gates].rearrange("p i s -> p s i").unsqueeze(3)
                                      .broadcast_to([P, m, TC, HG]), ALU.mult).then_inc(gated_done, 1)
                    dve.wait_ge(gated_done, done + n + 1)
                    for s in range(m):
                        last = dve.tensor_tensor(part[:, kinds.start + s, :, :, :], sums[:, s, :, :, 0:D],
                                                 gated[:, kinds.start + s, :, :].unsqueeze(3).broadcast_to([P, TC, HG, D]), ALU.mult)
                    last.then_inc(b_read[u % 2], 1)

            def step(second, first):
                weighed = not second
                for u in range(A_USES):
                    if not weighed and A_AT[u] >= SLOTS * BACK_AT[0] + SLOTS - 1:
                        weighed = True
                        weigh(second, 0)
                    if first:
                        block_maxima(first, u)
                    if second and u == LATE_SHIFT_AFTER:
                        shifts(second, 1)
                    if first:
                        for i in range(NT):
                            if u == MAX_AFTER[i]:
                                rank(first, i)
                            if u == MARK_AFTER[i]:
                                mark(first, i)
                        if u in BIAS_AFTER:
                            set_bias(first, BIAS_AFTER.index(u))
                        if u == SHIFT_AFTER:
                            shifts(first, 0)
                if second:
                    weigh(second, 1)
            def zero(m, done):
                dve.memset(m, 0.0).then_inc(done, 1)

            def ones_of_keys(p):
                rows = keys[p][R_SPLIT:ROWS, :, :].rearrange("r h n -> r (h n)").bitcast(F32)
                dve.memset(rows, PAIR_OF_ONES).then_inc(consts[p], 1)
            zero(q_first[0][0:R_SPLIT, :, :, :], first_consts)
            zero(k_first[0][0:R_SPLIT, :, :], first_consts)
            zero(block_max[:, :, :, :], first_consts)
            ones_of_keys(0)
            zero(vc_pad[0][:, :, :], zeros)
            zero(vc_pad[1][:, :, :], zeros)
            dve.wait_ge(zeros, 2)
            for p in range(2):
                for h in range(2):
                    dve.memset(vc_pad[p][h * NB:(h + 1) * NB, :, 32 * h + D:32 * h + D + 1], 1.0).then_inc(consts[p], 1)
            dve.wait_ge(key_blocks, 1)
            for p in range(2):
                if p:
                    ones_of_keys(1)
                for h in range(HG):
                    if p or h:
                        dve.tensor_copy(keys[p][0:NB, h, 0:T], keys[0][0:NB, 0, 0:T]).then_inc(consts[p], 1)
            dve.wait_ge(first_consts, N_FIRST_CONST)
            steps(dve, step)

        @block.tensor
        def _(pe):
            def bank_m(group, use):
                g, p, k = group
                if not (is_first(group) and use == 0):
                    pe.wait_ge(m_free, M_USES * g + use)

            def first_part(group, use):
                g, p, k = group
                what, n = M_WHAT[use]
                if what == "logit":
                    if n == 0:
                        pe.wait_ge(loaded_first[p], 16 * N_LOAD1 * (k + 1))
                    bank_m(group, use)
                    for i in (2 * n, 2 * n + 1):
                        at = i % 2 * HG * NB
                        pe.matmul(ps_m[:, at:at + HG * NB], ident_b[:, :],
                                  cmask[:, i, :].unsqueeze(1).broadcast_to([P, HG, NB]), start=True, stop=False)
                        for h in range(HG):
                            last = pe.matmul(ps_m[:, at + h * NB:at + (h + 1) * NB], q_first[p][:, i // TC, h, i % TC * P:(i % TC + 1) * P],
                                             k_first[p][:, h, T:NK], start=False, stop=(h == HG - 1))
                elif what == "bias":
                    pe.wait_ge(bias_done, 2 * g + n + 1)
                    bank_m(group, use)
                    for pair in range(2):
                        for i in range(TC):
                            at = (pair * TC + i) * P
                            last = pe.transpose(ps_mb[:, at:at + P],
                                                bias[:, n * TC + i, 2 * pair:2 * pair + 2, :].rearrange("p h n -> p (h n)"), ident_b[:, :])
                elif what == "prob":
                    half, pair = n
                    pe.wait_ge(exp_c, 2 * g + half + 1)
                    bank_m(group, use)
                    for i in range(TC):
                        last = pe.transpose(ps_m[:, i * P:(i + 1) * P],
                                            prob_c[:, half * TC + i, 2 * pair:2 * pair + 2, :].rearrange("p h n -> p (h n)"), ident_f[:, :])
                else:
                    pe.wait_ge(shift_step, 8 * g + 4 * n + 4)
                    bank_m(group, use)
                    last = pe.transpose(ps_mb[0:6 * TC * HG, 0:P], shift[:, :, :, :].rearrange("p a s r -> p (a s r)"), ident_b[:, :])
                last.then_inc(m_full, 1)

            def logits_a(group, u):
                g, p, k = group
                i, heads, k0, w, local = A_UNITS[u]
                if u == 0:
                    pe.wait_ge(loaded_first[p], 16 * N_LOAD1 * (k + 1))
                if not (is_first(group) and u < 2):
                    pe.wait_ge(a_read, A_USES * g + u - 1)
                for n_h, h in enumerate(heads):
                    last = pe.matmul(ps_a[:, u % 2, n_h * w:(n_h + 1) * w], q_first[p][:, i // TC, h, i % TC * P:(i % TC + 1) * P],
                                     k_first[p][:, h, k0:k0 + w], start=True, stop=(i > 0))
                    if i == 0:
                        last = pe.matmul(ps_a[:, u % 2, n_h * w:n_h * w + TOP * G], ident_b[:, :], causal_q[:, :],
                                         start=False, stop=True)
                last.then_inc(a_full, 1)

            def bank_b(group, u):
                if not (is_first(group) and u < 2):
                    pe.wait_ge(b_read[u % 2], b_count(group[0], u))

            def logits_b(group, n, part):
                g, p, k = group
                kind, c, j = SECOND[n]
                tile = slice(j * P, (j + 1) * P)
                if kind == "selected":
                    r, w = SEL.index((c, j)), width(c, j)
                    if j == 0 and part == 0:
                        pe.wait_ge(bias_in[p][c], 16 * 2 * (k + 1))
                        pe.wait_ge(shift_in[p][c], 16 * 6 * (k + 1))
                    for pair in (part,):
                        u = B_SEL[r] + pair
                        bank_b(group, u)
                        for n_h in range(2):
                            h = 2 * pair + n_h
                            partial = c == 0 and j == 0
                            last = pe.matmul(ps_b[:, u % 2, n_h, 0:w], keys[p][:, h, tile], q_sel[p][:, c, h, CH - w:],
                                             start=True, stop=not partial)
                            if partial:
                                last = pe.matmul(ps_b[:, u % 2, n_h, 0:TOP * G], ident_b[:, :], causal_k[:, :],
                                                 start=False, stop=True)
                        last.then_inc(b_full, 1)
                elif kind == "compressed":
                    u = part
                    if part == 0:
                        pe.wait_ge(loaded[p], 16 * N_LOAD2 * (k + 1))
                        pe.wait_ge(m_free, M_USES * g + M_PROB[1] + 1)
                    bank_b(group, u)
                    for pair in range(2):
                        last = pe.matmul(ps_b[64 * pair:64 * pair + 64, u, 0, :], vc_pad[p][:, pair, :],
                                         prob_ct[:, pair, part * CH:(part + 1) * CH], start=True, stop=True)
                    last.then_inc(b_full, 1)
                elif part == 0:
                    u, w = B_LOC[j], band_width(j)
                    if j == TC - 1:
                        pe.wait_ge(shift_in[p][1], 16 * 6 * (k + 1))
                    bank_b(group, u)
                    for h in range(HG):
                        out = ps_b[:, u % 2, h // 2, h % 2 * BAND:h % 2 * BAND + w]
                        at = j % TC * P
                        here = min(w, CH - at)
                        pe.matmul(out[:, 0:here], keys[p][:, h, tile], q_loc[p][:, c, h, at:at + here], start=True, stop=False)
                        if here < w:
                            pe.matmul(out[:, here:w], keys[p][:, h, tile], q_loc[p][:, c + 1, h, 0:w - here], start=False, stop=False)
                        last = pe.matmul(out, ident_b[:, :], band_k[:, 0:w], start=False, stop=True)
                    last.then_inc(b_full, 1)

            def sums(group, n):
                g, p, k = group
                kind, c, j = SECOND[n]
                if kind == "selected":
                    r, w = SEL.index((c, j)), width(c, j)
                    if j == 0:
                        if c == 0:
                            pe.wait_ge(v_ready, g + 1)
                        if c or not is_first(group):
                            pe.wait_ge(o_free, 4 * g + 2 * c)
                    for pair in range(2):
                        u = B_SEL[r] + pair
                        pe.wait_ge(b_read[u % 2], b_count(g, u) + 1)
                    for h in range(HG):
                        last = pe.matmul(ps_o[32 * h:32 * h + 32, CH - w:], v_pad[p][:, j, h, :],
                                         prob_s[r % 2][:, h, 0:w], start=(j == 0), stop=(j == TC * (c + 1) - 1))
                    last.then_inc(pv_sel, 1)
                elif kind == "local":
                    u = B_LOC[j]
                    at = j % TC * P
                    if j % TC == 0:
                        pe.wait_ge(o_free, 4 * g + 2 * c + 1)
                    pe.wait_ge(b_read[u % 2], b_count(g, u) + 1)
                    for h in range(HG):
                        last = pe.matmul(ps_o[32 * h:32 * h + 32, at:at + P], v_pad[p][:, j, h, :],
                                         prob_l[j % 4][:, h, 0:P], start=True, stop=(j == 0))
                    if j:
                        for h in range(HG):
                            last = pe.matmul(ps_o[32 * h:32 * h + 32, at:at + WIN], v_pad[p][:, j - 1, h, :],
                                             prob_l[(j - 1) % 4][:, h, P:BAND], start=False, stop=True)
                    last.then_inc(pv_loc, 1)

            def back(group, c):
                g, p, k = group
                pe.wait_ge(o_free, 4 * g + 2 * c + 2)
                for n, kinds in enumerate(((0, 1), (2 + c,))):
                    u = B_BACK[c] + n
                    bank_b(group, u)
                    for s, kind in enumerate(kinds):
                        for i in range(TC):
                            last = pe.transpose(ps_b[:, u % 2, s, i * P:(i + 1) * P], mixed_t[:, kind, i * P:(i + 1) * P], ident_f[:, :])
                    last.then_inc(b_full, 1)

            def step(second, first):
                for n in range(END + 1):
                    for slot in range(SLOTS):
                        if first:
                            for u in range(A_USES):
                                if A_AT[u] == n * SLOTS + slot:
                                    logits_a(first, u)
                        if second:
                            if n < len(SECOND) and slot < 2:
                                logits_b(second, n, slot)
                            if slot == 2 and 1 < n <= len(SECOND):
                                sums(second, n - 1)
                            if slot == 2 and n in BACK_AT:
                                back(second, BACK_AT.index(n))
                    if second and n == LATE_SHIFT_AT:
                        first_part(second, M_SHIFT[1])
                    if first:
                        for use in uses_at(n):
                            first_part(first, use)
            pe.wait_ge(first_consts, N_FIRST_CONST)
            steps(pe, step)


def feed_forward(nc, dram, ident_f, ident_b):
    with ExitStack() as ctx:
        def sb(name, shape, dt=F32):
            return ctx.enter_context(nc.sbuf_tensor(name, shape, dt))

        def ps(name, shape, dt=F32):
            return ctx.enter_context(nc.psum_tensor(name, shape, dt))

        def sem(name):
            return ctx.enter_context(nc.semaphore(name))

        NE1 = E + 1
        PAD = 8 - K2
        wo = sb("wo", [P, DM])
        w1 = sb("w1", [P, E, F])
        w2 = sb("w2", [P, E, DM])
        w_gu = sb("w_gu", [P, 2 * F])
        w_sd = sb("w_sd", [P, DM])
        w_rs = sb("w_rs", [P, NE1])
        xr = sb("xr", [P, TILES, DM])
        attn = [sb(f"attn_in{p}", [P, TC, DM]) for p in range(2)]
        attn_t = [sb(f"attn_t{p}", [P, CH]) for p in range(2)]
        total = sb("total3", [P, TILES])
        mean = sb("mean3", [P, TILES])
        centred = sb("centred3", [P, TILES, DM])
        squares = [sb(f"squares3{p}", [P, TC, DM]) for p in range(2)]
        sqsum = sb("sqsum3", [P, TILES])
        rstd = sb("rstd3", [P, TILES])
        eps = sb("eps3", [P, 1])
        normed = [sb(f"normed3{p}", [P, TC, DM]) for p in range(2)]
        nt_chunk = [sb(f"nt_chunk{p}", [P, CH]) for p in range(2)]
        nt = sb("nt", [P, B * T])
        logit = sb("logit3", [P, TILES, PAD + E])
        best = sb("best3", [P, TILES, 8])
        marked = sb("marked3", [P, TILES, PAD + E])
        chosen = sb("chosen", [P, TILES, E])
        prob = sb("prob3", [P, TILES, E])
        prob_sum = sb("prob_sum", [P, TILES])
        prob_inv = sb("prob_inv", [P, TILES])
        share = sb("share", [P, TILES, NE1])
        share_rest = sb("share_rest", [P, TILES, NE1])
        share_split = sb("share_split", [P, TILES, P], BF16)
        share_t = sb("share_t", [P, B * T], BF16)
        spread = sb("spread", [P, NE1, P], BF16)
        hidden = [sb(f"hidden{n}", [P, CH]) for n in range(3)]
        shared = sb("shared", [P, CH])
        weighed = [sb(f"weighed{n}", [P, CH]) for n in range(3)]
        out_t = sb("out_t", [P, CH])
        out_sb = sb("out_sb", [P, TC, DM])

        ps_h = ps("ps_h3", [P, 2, CH])
        ps_c = ps("ps_c3", [P, 2, CH])
        ps_out = ps("ps_out3", [P, CH])
        ps_s = [ps_out[:, :].bitcast(BF16), ps("ps_s3", [P, CH])[:, :].bitcast(BF16)]
        ps_t = [ps_h[:, p, :] for p in range(2)]
        ps_y = [ps_c[:, p, :].rearrange("p (i n) -> p i n", i=TC) for p in range(2)]

        a_in = [sem(f"a_in{p}") for p in range(2)]
        wo_in, w3_in, consts, const_step = map(sem, ("wo_in", "w3_in", "consts3", "const_step3"))
        at_ps, at_done, y_ps, added, totals, means, centre, squared, sqsums = map(
            sem, ("at_ps", "at_done", "y_ps", "added3", "totals3", "means3", "centre3", "squared3", "sqsums3"))
        sdevs, rstds, norms, t_ps, nt_done, l_ps, l_done = map(
            sem, ("sdevs3", "rstds3", "norms3", "t_ps3", "nt_done3", "l_ps3", "l_done3"))
        route, exp_done, ct_ps, ct_done = map(sem, ("route", "exp_done3", "ct_ps", "ct_done"))
        h_full, c_full, c_read, down, o_done, out_done = map(
            sem, ("h_full", "c_full", "c_read", "down", "o_done", "out_done"))
        h_read = [sem(f"h_read{n}") for n in range(2)]
        stored = sem("stored")
        block = ctx.enter_context(nc.Block())
        N_W = 6

        def chunks(engine, chunk):
            last = CHUNKS // 2 - 1
            chunk(0, 0, 0)
            chunk(1, 1, 0)
            with engine.Fori(1, last) as k:
                chunk(2 * k, 0, k)
                chunk(2 * k + 1, 1, k)
            chunk(2 * last, 0, last)
            chunk(2 * last + 1, 1, last)

        def started(c):
            return not (isinstance(c, int) and c == 0)

        def repeats(c):
            return not (isinstance(c, int) and c < 2)

        def ends(c):
            return isinstance(c, int) and c == CHUNKS - 1

        @block.sync
        def _(sp):
            def chunk(c, p, k):
                if repeats(c):
                    sp.wait_ge(at_ps, c - 1)
                sp.dma_start(attn[p][:, :, :], dram["attn"].rearrange("b t r -> (b t) r")[ds(c * CH, CH), :]
                             .rearrange("(i p) r -> p i r", p=P)).then_inc(a_in[p], 16)
                sp.dma_start(xr[:, ds(c * TC, TC), :], dram["x"][ds(c * CH, CH), :].rearrange("(i p) n -> p i n", p=P)).then_inc(a_in[p], 16)
            chunks(sp, chunk)

            def store(c, p, k):
                sp.wait_ge(out_done, c + 1)
                sp.dma_start(dram["out"][ds(c * CH, CH), :].rearrange("(i p) n -> p i n", p=P), out_sb[:, :, :]).then_inc(stored, 16)
            chunks(sp, store)
            sp.wait_ge(stored, 16 * CHUNKS)

        @block.gpsimd
        def _(pool):
            pool.memset(spread[:, :, :], 0.0).then_inc(const_step, 1)
            pool.memset(share_split[:, :, :], 0.0).then_inc(consts, 1)
            pool.memset(eps[:, :], EPS).then_inc(consts, 1)
            pool.memset(logit[:, :, 0:PAD], SENTINEL).then_inc(consts, 1)
            for s in range(3):
                pool.wait_ge(const_step, s + 1)
                pool.affine_select(out=spread[:, :, :], in_=spread[:, :, :], compare_op=ALU.not_equal, fill=1.0,
                                   base=-s * NE1, pattern=[[-1, NE1], [0, P]], channel_multiplier=1).then_inc(const_step, 1)
            pool.wait_ge(const_step, 4)

            def chunk(c, p, k):
                pool.wait_ge(centre, c + 1)
                if repeats(c):
                    pool.wait_ge(sqsums, c - 1)
                x = centred[:, ds(c * TC, TC), :]
                pool.tensor_tensor(squares[p][:, :, :], x, x, ALU.mult).then_inc(squared, 1)
            chunks(pool, chunk)

        @block.scalar
        def _(act):
            act.dma_start(wo[:, :], dram["wo"]).then_inc(wo_in, 16)
            act.dma_start(w_rs[:, 0:E], dram["router_w"]).then_inc(w3_in, 16)
            act.dma_start(w_rs[:, E:NE1], dram["sgate_w"]).then_inc(w3_in, 16)
            act.dma_start(w1[:, :, :], dram["w1"].rearrange("e d f -> d e f")).then_inc(w3_in, 16)
            act.dma_start(w2[:, :, :], dram["w2"].rearrange("e f d -> f e d")).then_inc(w3_in, 16)
            act.dma_start(w_gu[:, :], dram["sgu"]).then_inc(w3_in, 16)
            act.dma_start(w_sd[:, :], dram["sdown"]).then_inc(w3_in, 16)
            act.wait_ge(consts, 3)

            def copy_attn(c, p, k):
                act.wait_ge(at_ps, c + 1)
                if repeats(c):
                    act.wait_ge(y_ps, c - 1)
                act.activation(attn_t[p][:, :], ps_t[p], ACT.Copy).then_inc(at_done, 1)
            chunks(act, copy_attn)
            act.wait_ge(sqsums, CHUNKS)
            act.activation(sqsum[:, :], sqsum[:, :], ACT.Sqrt, bias=eps[:, 0:1], scale=1.0 / DM).then_inc(sdevs, 1)

            def copy_normed(c, p, k):
                act.wait_ge(t_ps, c + 1)
                if repeats(c):
                    act.wait_ge(l_ps, c - 1)
                act.activation(nt_chunk[p][:, :], ps_t[p], ACT.Copy).then_inc(nt_done, 1)
                act.activation(nt[:, ds(c * CH, CH)], ps_t[p], ACT.Copy).then_inc(nt_done, 1)
                act.wait_ge(l_ps, c + 1)
                act.activation(logit[:, ds(c * TC, TC), PAD:], ps_y[p][:, :, 0:E], ACT.Copy).then_inc(l_done, 1)
                act.activation(share[:, ds(c * TC, TC), E:NE1], ps_y[p][:, :, E:NE1], ACT.Copy).then_inc(l_done, 1)
            chunks(act, copy_normed)
            act.wait_ge(l_done, 2 * CHUNKS)
            act.activation(share[:, :, E:NE1], share[:, :, E:NE1], ACT.Exp, scale=-1.0).then_inc(exp_done, 1)
            act.wait_ge(route, 2)
            act.activation(prob[:, :, :], prob[:, :, :], ACT.Exp).then_inc(exp_done, 1)
            for n in range(4):
                act.wait_ge(ct_ps, n + 1)
                act.activation(share_t[:, n * 2 * CH:(n + 1) * 2 * CH], ps_s[n % 2], ACT.Copy).then_inc(ct_done, 1)

            def experts(c, p, k):
                for e in range(NE1):
                    act.wait_ge(h_full, (NE1 + 1) * c + e + 1)
                    if e >= 3 or started(c):
                        act.wait_ge(c_read, NE1 * c + e - 2)
                    act.activation(hidden[e % 3][:, :], ps_h[:, e % 2, :], ACT.Silu).then_inc(h_read[e % 2], 1)
                act.wait_ge(down, NE1 * (c + 1))
                if started(c):
                    act.wait_ge(c_full, (NE1 + 1) * c)
                act.activation(out_t[:, :], ps_out[:, :], ACT.Copy).then_inc(o_done, 1)
            chunks(act, experts)

        @block.vector
        def _(dve):
            dve.wait_ge(consts, 3)

            def residual(c, p, k):
                at = ds(c * TC, TC)
                dve.wait_ge(a_in[p], 2 * 16 * (k + 1))
                dve.wait_ge(y_ps, c + 1)
                dve.tensor_tensor(xr[:, at, :], xr[:, at, :], ps_y[p], ALU.add).then_inc(added, 1)
                dve.wait_ge(added, c + 1)
                dve.tensor_reduce(total[:, at], xr[:, at, :], AX.X, ALU.add).then_inc(totals, 1)
                dve.wait_ge(totals, c + 1)
                dve.tensor_scalar(mean[:, at], total[:, at], 1.0 / DM, None, ALU.mult).then_inc(means, 1)
                dve.wait_ge(means, c + 1)
                dve.tensor_tensor(centred[:, at, :], xr[:, at, :], mean[:, at].unsqueeze(2).broadcast_to([P, TC, DM]),
                                  ALU.subtract).then_inc(centre, 1)
                if started(c):
                    sum_squares(c - 1, 1 - p)

            def sum_squares(c, p):
                dve.wait_ge(squared, c + 1)
                dve.tensor_reduce(sqsum[:, ds(c * TC, TC)], squares[p][:, :, :], AX.X, ALU.add).then_inc(sqsums, 1)
            chunks(dve, residual)
            sum_squares(CHUNKS - 1, 1)
            dve.wait_ge(sdevs, 1)
            dve.reciprocal(rstd[:, :], sqsum[:, :]).then_inc(rstds, 1)
            dve.wait_ge(rstds, 1)

            def norm(c, p, k):
                at = ds(c * TC, TC)
                if repeats(c):
                    dve.wait_ge(t_ps, c - 1)
                dve.tensor_tensor(normed[p][:, :, :], centred[:, at, :], rstd[:, at].unsqueeze(2).broadcast_to([P, TC, DM]),
                                  ALU.mult).then_inc(norms, 1)
            chunks(dve, norm)
            dve.wait_ge(l_done, 2 * CHUNKS)
            for i in range(TILES):
                last = dve.max(best[:, i, :], logit[:, i, :])
            last.then_inc(route, 1)
            dve.wait_ge(route, 1)
            dve.tensor_tensor(prob[:, :, :], logit[:, :, PAD:], best[:, :, 0:1].broadcast_to([P, TILES, E]), ALU.subtract).then_inc(route, 1)
            dve.memset(best[:, :, K2:], SENTINEL).then_inc(route, 1)
            dve.wait_ge(route, 3)
            for i in range(TILES):
                last = dve.match_replace(marked[:, i, :], best[:, i, :], logit[:, i, :], TAKEN)
            last.then_inc(route, 1)
            dve.wait_ge(exp_done, 2)
            dve.tensor_reduce(prob_sum[:, :], prob[:, :, :], AX.X, ALU.add).then_inc(route, 1)
            dve.tensor_scalar(share[:, :, E:NE1], share[:, :, E:NE1], 1.0, None, ALU.add).then_inc(route, 1)
            dve.wait_ge(route, 6)
            dve.reciprocal(prob_inv[:, :], prob_sum[:, :]).then_inc(route, 1)
            dve.reciprocal(share[:, :, E:NE1], share[:, :, E:NE1]).then_inc(route, 1)
            dve.tensor_scalar(chosen[:, :, :], marked[:, :, PAD:], TAKEN / 2, None, ALU.is_ge).then_inc(route, 1)
            dve.wait_ge(route, 9)
            dve.tensor_tensor(chosen[:, :, :], chosen[:, :, :], prob[:, :, :], ALU.mult).then_inc(route, 1)
            dve.wait_ge(route, 10)
            dve.tensor_tensor(share[:, :, 0:E], chosen[:, :, :], prob_inv[:, :].unsqueeze(2).broadcast_to([P, TILES, E]),
                              ALU.mult).then_inc(route, 1)
            dve.wait_ge(route, 11)
            dve.tensor_copy(share_split[:, :, 0 * NE1:1 * NE1], share[:, :, :]).then_inc(route, 1)
            dve.wait_ge(route, 12)
            dve.tensor_tensor(share_rest[:, :, :], share[:, :, :], share_split[:, :, 0 * NE1:1 * NE1], ALU.subtract).then_inc(route, 1)
            dve.wait_ge(route, 13)
            dve.tensor_copy(share_split[:, :, 1 * NE1:2 * NE1], share_rest[:, :, :]).then_inc(route, 1)
            dve.wait_ge(route, 14)
            dve.tensor_tensor(share_split[:, :, 2 * NE1:3 * NE1], share_rest[:, :, :], share_split[:, :, 1 * NE1:2 * NE1], ALU.subtract).then_inc(route, 1)

            def experts(c, p, k):
                n = NE1 + 1
                for e in range(NE1):
                    u = n * c + e
                    dve.wait_ge(h_read[e % 2], n // 2 * c + e // 2 + 1)
                    if e == E:
                        dve.wait_ge(h_full, n * c + n)
                        if started(c):
                            dve.wait_ge(c_read, NE1 * c)
                        dve.tensor_tensor(shared[:, :], hidden[e % 3][:, :], ps_h[:, 1, :], ALU.mult).then_inc(h_read[1], 1)
                        dve.wait_ge(h_read[1], n // 2 * (c + 1))
                    dve.wait_ge(c_full, u + 1)
                    if e >= 3 or started(c):
                        dve.wait_ge(down, NE1 * c + e - 2)
                    of = shared if e == E else hidden[e % 3]
                    dve.tensor_tensor(weighed[e % 3][:, :], of[:, :], ps_c[:, e % 2, :], ALU.mult).then_inc(c_read, 1)
                dve.wait_ge(c_full, n * (c + 1))
                if started(c):
                    dve.wait_ge(stored, 16 * c)
                dve.tensor_tensor(out_sb[:, :, :], xr[:, ds(c * TC, TC), :],
                                  ps_c[:, 1, :].rearrange("p (i n) -> p i n", i=TC), ALU.add).then_inc(out_done, 1)
            chunks(dve, experts)

        @block.tensor
        def _(pe):
            pe.wait_ge(wo_in, 16)

            def turn_attn(c, p, k):
                pe.wait_ge(a_in[p], 2 * 16 * (k + 1))
                if repeats(c):
                    pe.wait_ge(at_done, c - 1)
                for i in range(TC):
                    last = pe.transpose(ps_t[p][:, i * P:(i + 1) * P], attn[p][:, i, :], ident_f[:, :])
                last.then_inc(at_ps, 1)

            def project(c, p, k):
                if not ends(c):
                    turn_attn(c + 1, 1 - p, k + p)
                pe.wait_ge(at_done, c + 1)
                if repeats(c):
                    pe.wait_ge(added, c - 1)
                for i in range(TC):
                    last = pe.matmul(ps_y[p][:, i, :], attn_t[p][:, i * P:(i + 1) * P], wo[:, :], start=True, stop=True)
                last.then_inc(y_ps, 1)
            turn_attn(0, 0, 0)
            chunks(pe, project)

            def turn_normed(c, p):
                pe.wait_ge(norms, c + 1)
                if repeats(c):
                    pe.wait_ge(nt_done, 2 * (c - 1))
                for i in range(TC):
                    last = pe.transpose(ps_t[p][:, i * P:(i + 1) * P], normed[p][:, i, :], ident_f[:, :])
                last.then_inc(t_ps, 1)

            def route_logits(c, p, k):
                if not ends(c):
                    turn_normed(c + 1, 1 - p)
                pe.wait_ge(nt_done, 2 * c + 1)
                if repeats(c):
                    pe.wait_ge(l_done, 2 * (c - 1))
                for i in range(TC):
                    last = pe.matmul(ps_y[p][:, i, 0:NE1], nt_chunk[p][:, i * P:(i + 1) * P], w_rs[:, :], start=True, stop=True)
                last.then_inc(l_ps, 1)
            pe.wait_ge(w3_in, 16 * N_W)
            pe.wait_ge(const_step, 4)
            pe.wait_ge(at_done, CHUNKS)
            pe.wait_ge(added, CHUNKS)
            turn_normed(0, 0)
            chunks(pe, route_logits)
            def up(c, u):
                n = NE1 + 1
                w = w1[:, u, :] if u < E else w_gu[:, (u - E) * F:(u - E + 1) * F]
                if u >= 2 or started(c):
                    pe.wait_ge(h_read[u % 2], n // 2 * c + u // 2)
                pe.matmul(ps_h[:, u % 2, :], w, nt[:, ds(c * CH, CH)], start=True, stop=True).then_inc(h_full, 1)
            pe.wait_ge(nt_done, 2 * CHUNKS)
            up(0, 0)
            up(0, 1)
            pe.wait_ge(route, 15)
            for n in range(4):
                if n >= 2:
                    pe.wait_ge(ct_done, n - 1)
                for i in range(2 * TC):
                    last = pe.transpose(ps_s[n % 2][:, i * P:(i + 1) * P],
                                        share_split[:, n * 2 * TC + i, :], ident_b[:, :])
                last.then_inc(ct_ps, 1)
            pe.wait_ge(ct_done, 4)

            def experts(c, p, k):
                def shares(e):
                    if e >= 2:
                        pe.wait_ge(c_read, NE1 * c + e - 1)
                    elif started(c):
                        pe.wait_ge(*((c_read, NE1 * c) if e == 0 else (out_done, c)))
                    pe.matmul(ps_c[:, e % 2, :], spread[:, e, :], share_t[:, ds(c * CH, CH)], start=True, stop=True).then_inc(c_full, 1)

                def join(e):
                    if e == 0 and started(c):
                        pe.wait_ge(o_done, c)
                    pe.wait_ge(c_read, NE1 * c + e + 1)
                    w = w2[:, e, :] if e < E else w_sd[:, :]
                    pe.matmul(ps_out[:, :], w, weighed[e % 3][:, :], start=(e == 0), stop=(e == NE1 - 1)).then_inc(down, 1)
                for e in range(NE1):
                    if e >= 2:
                        up(c, e)
                    if e == E:
                        up(c, NE1)
                    shares(e)
                    if e:
                        join(e - 1)
                if not ends(c):
                    up(c + 1, 0)
                join(NE1 - 1)
                if not ends(c):
                    up(c + 1, 1)
                pe.wait_ge(o_done, c + 1)
                for i in range(TC):
                    last = pe.transpose(ps_c[:, 1, i * P:(i + 1) * P], out_t[:, i * P:(i + 1) * P], ident_f[:, :])
                last.then_inc(c_full, 1)
            chunks(pe, experts)


def program(nc, dram, made):
    dram["x"] = dram["x"].rearrange("b t n -> (b t) n")
    dram["out"] = dram["out"].rearrange("b t n -> (b t) n")
    for name, shape, dt in (("q", (B, 3 * D, HC, H, CH), BF16), ("k", (B, 3 * D, H, NK), BF16), ("v", (B, T, DM), F32),
                            ("vc", (B, NB, DM), F32), ("gates", (B, P, NT, 3), F32), ("attn", (B, T, DM), F32)):
        dram[name] = nc.dram_tensor(f"made_{name}", shape, dt, kind=made).ap()
    with nc.sbuf_tensor("ident_f", [P, P], F32) as ident_f, nc.sbuf_tensor("ident_b", [P, P], BF16) as ident_b:
        project(nc, dram, ident_f, ident_b)
        attend(nc, dram, ident_b, ident_f)
        feed_forward(nc, dram, ident_f, ident_b)


_INS = {"L0_attn_x": "x", "L0_attn_Wq": "wq", "L0_attn_Wk": "wk", "L0_attn_Wv": "wv", "L0_attn_Wo": "wo",
        "L0_attn_Wck": "wck", "L0_attn_Wcv": "wcv", "L0_attn_Wg": "wg", "L0_attn_bg": "bg",
        "L0_ffn_router_w": "router_w", "L0_ffn_w1": "w1", "L0_ffn_w2": "w2", "L0_ffn_shared_gate_up": "sgu",
        "L0_ffn_shared_down": "sdown", "L0_ffn_shared_gate_w": "sgate_w"}


def kernel(**inputs):
    import numpy as np
    import concourse.bacc as bacc
    from concourse.bass_utils import run_bass_kernel_spmd

    nc = bacc.Bacc("TRN2", target_bir_lowering=False, num_devices=1)
    arrays, dram = {}, {}
    for name, short in _INS.items():
        a = np.ascontiguousarray(inputs[name])
        arrays[f"in_{short}"] = a
        dram[short] = nc.dram_tensor(f"in_{short}", a.shape, mybir.dt.from_np(a.dtype), kind="ExternalInput").ap()
    dram["out"] = nc.dram_tensor("out", (B, T, DM), F32, kind="ExternalOutput").ap()
    program(nc, dram, "Internal")
    return run_bass_kernel_spmd(nc, [arrays], core_ids=[0]).results[0]["out"]
```
